# Optimizing a Trainium2 kernel written in Bass

```python
import numpy as np
import jax
import jax.numpy as jnp

def _softmax(x, axis=-1):
    return jax.nn.softmax(x, axis=axis)

def _gelu(x):
    return jax.nn.gelu(x, approximate=True)

def _silu(x):
    return jax.nn.silu(x)

def _sigmoid(x):
    return jax.nn.sigmoid(x)

def _layernorm(x, axis=-1, eps=1e-05):
    m = jnp.mean(x, axis=axis, keepdims=True)
    v = jnp.var(x, axis=axis, keepdims=True)
    return (x - m) / jnp.sqrt(v + eps)

def _scatter_add(tgt, idx, src, axis=0):
    return tgt.at[idx].add(src)

def _segment_sum(src, seg, n):
    return jax.ops.segment_sum(src, seg, n)
kernel_name = 'mk_macaron_d2_jaxref_r8_de8af8'

def setup_inputs(seed: int=0):
    np.random.seed(seed)
    _w = jnp.asarray

    def _L0_attn_setup():
        import jax, jax.numpy as jnp
        import numpy as np
        B, TT, C, H, T = (4, 512, 128, 16, 128)
        K = C // H
        HEAD_DIV = 8.0
        EPS = 1e-05
        LAYER_ID, N_LAYER = (12, 24)
        key = jax.random.key(seed)
        ks = jax.random.split(key, 8)
        r01 = LAYER_ID / (N_LAYER - 1)
        r1a0 = 1.0 - LAYER_ID / N_LAYER
        ddd = (jnp.arange(C, dtype=jnp.float32) / C).reshape(1, 1, C)
        h = jnp.arange(H, dtype=jnp.float32)
        scale = 0.02
        return {'xq': jax.random.normal(ks[0], (B, TT, C), jnp.float32), 'time_mix_k': ddd ** r1a0, 'time_mix_v': ddd ** r1a0 + 0.3 * r01, 'time_mix_r': ddd ** (0.5 * r1a0), 'time_mix_g': ddd ** (0.5 * r1a0), 'time_decay': -8.0 + 7.0 * (h / (H - 1)) ** (0.7 + 1.3 * r01), 'time_faaaa': r01 * (1.0 - h / (H - 1)), 'W_r': jax.random.normal(ks[1], (C, C), jnp.float32) * scale, 'W_k': jax.random.normal(ks[2], (C, C), jnp.float32) * scale, 'W_v': jax.random.normal(ks[3], (C, C), jnp.float32) * scale, 'W_g': jax.random.normal(ks[4], (C, C), jnp.float32) * scale, 'W_o': jax.random.normal(ks[5], (C, C), jnp.float32) * scale, 'ln_w': jnp.ones((C,), jnp.float32), 'ln_b': jnp.zeros((C,), jnp.float32)}
    _L0_attn_in = _L0_attn_setup()

    def _L0_ffn_setup():
        import jax, jax.numpy as jnp
        import numpy as np
        B, S, H = (2, 128, 128)
        E, F = (8, 512)
        GATE_TEMP = 0.1
        key = jax.random.key(seed)
        ks = jax.random.split(key, 6)
        s_h = 1.0 / np.sqrt(H)
        s_f = 1.0 / np.sqrt(F)
        return {'hidden_states': jax.random.normal(ks[0], (B, S, H), dtype=jnp.float32), 'w_router': jax.random.normal(ks[1], (H, E), dtype=jnp.float32) * s_h, 'w_gating': jax.random.normal(ks[2], (H, E), dtype=jnp.float32) * s_h, 'w_gate': jax.random.normal(ks[3], (E, H, F), dtype=jnp.float32) * s_h, 'w_up': jax.random.normal(ks[4], (E, H, F), dtype=jnp.float32) * s_h, 'w_down': jax.random.normal(ks[5], (E, F, H), dtype=jnp.float32) * s_f}
    _L0_ffn_in = _L0_ffn_setup()

    def _L1_attn_setup():
        import jax, jax.numpy as jnp
        import numpy as np
        D_MODEL = 128
        NUM_HEADS = 16
        D_K = D_MODEL // NUM_HEADS
        B, S = (4, 256)
        key = jax.random.key(seed)
        k1, k2, k3 = jax.random.split(key, 3)
        x = jax.random.normal(k1, (B, S, D_MODEL), dtype=jnp.float32)
        w_qkv = jax.random.normal(k2, (3, NUM_HEADS, D_K, D_MODEL), dtype=jnp.float32) / np.sqrt(D_MODEL)
        w_o = jax.random.normal(k3, (D_MODEL, D_MODEL), dtype=jnp.float32) / np.sqrt(D_MODEL)
        return {'x': x, 'w_qkv': w_qkv, 'w_o': w_o}
    _L1_attn_in = _L1_attn_setup()

    def _L1_ffn_setup():
        import jax, jax.numpy as jnp
        import numpy as np
        B, S, D, E = (2, 256, 128, 8)
        key = jax.random.key(seed)
        ks = jax.random.split(key, 5)
        x = jax.random.normal(ks[0], (B, S, D), dtype=jnp.float32)
        router_w = jax.random.normal(ks[1], (E, D), dtype=jnp.float32) * 0.02
        router_b = jnp.zeros((E,), dtype=jnp.float32)
        expert_w = jax.random.normal(ks[2], (E, D, D), dtype=jnp.float32) * 0.02
        expert_b = jnp.zeros((E, D), dtype=jnp.float32)
        return {'x': x, 'router_w': router_w, 'router_b': router_b, 'expert_w': expert_w, 'expert_b': expert_b}
    _L1_ffn_in = _L1_ffn_setup()
    _d = {'L0_attn_xq': _L0_attn_in['xq'], 'L0_attn_time_mix_k': _L0_attn_in['time_mix_k'], 'L0_attn_time_mix_v': _L0_attn_in['time_mix_v'], 'L0_attn_time_mix_r': _L0_attn_in['time_mix_r'], 'L0_attn_time_mix_g': _L0_attn_in['time_mix_g'], 'L0_attn_time_decay': _L0_attn_in['time_decay'], 'L0_attn_time_faaaa': _L0_attn_in['time_faaaa'], 'L0_attn_W_r': _L0_attn_in['W_r'], 'L0_attn_W_k': _L0_attn_in['W_k'], 'L0_attn_W_v': _L0_attn_in['W_v'], 'L0_attn_W_g': _L0_attn_in['W_g'], 'L0_attn_W_o': _L0_attn_in['W_o'], 'L0_attn_ln_w': _L0_attn_in['ln_w'], 'L0_attn_ln_b': _L0_attn_in['ln_b'], 'L0_ffn_w_router': _L0_ffn_in['w_router'], 'L0_ffn_w_gating': _L0_ffn_in['w_gating'], 'L0_ffn_w_gate': _L0_ffn_in['w_gate'], 'L0_ffn_w_up': _L0_ffn_in['w_up'], 'L0_ffn_w_down': _L0_ffn_in['w_down'], 'L1_attn_w_qkv': _L1_attn_in['w_qkv'], 'L1_attn_w_o': _L1_attn_in['w_o'], 'L1_ffn_router_w': _L1_ffn_in['router_w'], 'L1_ffn_router_b': _L1_ffn_in['router_b'], 'L1_ffn_expert_w': _L1_ffn_in['expert_w'], 'L1_ffn_expert_b': _L1_ffn_in['expert_b']}
    _x0 = _d['L0_attn_xq']
    _d['L0_attn_xq'] = jax.random.normal(jax.random.fold_in(jax.random.key(seed), 1), (8, 512, 128), dtype=_x0.dtype)
    del _x0
    return _d

def reference(L0_attn_xq, L0_attn_time_mix_k, L0_attn_time_mix_v, L0_attn_time_mix_r, L0_attn_time_mix_g, L0_attn_time_decay, L0_attn_time_faaaa, L0_attn_W_r, L0_attn_W_k, L0_attn_W_v, L0_attn_W_g, L0_attn_W_o, L0_attn_ln_w, L0_attn_ln_b, L0_ffn_w_router, L0_ffn_w_gating, L0_ffn_w_gate, L0_ffn_w_up, L0_ffn_w_down, L1_attn_w_qkv, L1_attn_w_o, L1_ffn_router_w, L1_ffn_router_b, L1_ffn_expert_w, L1_ffn_expert_b):

    def _L0_attn_ref(xq, time_mix_k, time_mix_v, time_mix_r, time_mix_g, time_decay, time_faaaa, W_r, W_k, W_v, W_g, W_o, ln_w, ln_b):
        import jax, jax.numpy as jnp
        import numpy as np
        B, TT, C, H, T = (4, 512, 128, 16, 128)
        K = C // H
        HEAD_DIV = 8.0
        EPS = 1e-05
        LAYER_ID, N_LAYER = (12, 24)
        x = xq
        B_, TT_, C_ = x.shape
        N = TT_ // T
        xx = jnp.pad(x, ((0, 0), (1, 0), (0, 0)))[:, :-1]
        xr = x * time_mix_r + xx * (1 - time_mix_r)
        xk = x * time_mix_k + xx * (1 - time_mix_k)
        xv = x * time_mix_v + xx * (1 - time_mix_v)
        xg = x * time_mix_g + xx * (1 - time_mix_g)
        r = (xr @ W_r.T).reshape(B_, TT_, H, K).transpose(0, 2, 1, 3)
        k = (xk @ W_k.T).reshape(B_, TT_, H, K).transpose(0, 2, 1, 3)
        v = (xv @ W_v.T).reshape(B_, TT_, H, K).transpose(0, 2, 1, 3)
        g = jax.nn.silu(xg @ W_g.T)
        decay = jnp.exp(-jnp.exp(time_decay))
        u = time_faaaa
        ws = decay ** T
        i_idx = jnp.arange(T)
        wb = decay[:, None] ** i_idx
        wk = decay[:, None] ** (T - 1 - i_idx)
        diff = i_idx[:, None] - i_idx[None, :]
        pw = decay[:, None, None] ** jnp.maximum(diff - 1, 0)
        w_mat = jnp.where(diff > 0, pw, 0.0) + jnp.eye(T, dtype=x.dtype) * u[:, None, None]
        rc = r.reshape(B_, H, N, T, K).transpose(2, 0, 1, 3, 4)
        kc = k.reshape(B_, H, N, T, K).transpose(2, 0, 1, 3, 4)
        vc = v.reshape(B_, H, N, T, K).transpose(2, 0, 1, 3, 4)
        s0 = jnp.zeros((B_, H, K, K), x.dtype)

        def step(s, chunk):
            rr, kk, vv = chunk
            att = jnp.einsum('bhik,bhjk->bhij', rr, kk) * w_mat
            out = att @ vv + jnp.einsum('bhik,bhkv->bhiv', rr, s) * wb[None, :, :, None]
            s_new = ws[None, :, None, None] * s + jnp.einsum('bhjk,bhjv->bhkv', kk * wk[None, :, :, None], vv)
            return (s_new, out)
        _, xo = jax.lax.scan(step, s0, (rc, kc, vc))
        xo = xo.transpose(1, 0, 3, 2, 4).reshape(B_, TT_, H, K)
        y = xo / HEAD_DIV
        mu = y.mean(-1, keepdims=True)
        var = y.var(-1, keepdims=True)
        y = (y - mu) / jnp.sqrt(var + EPS)
        y = y * ln_w.reshape(H, K) + ln_b.reshape(H, K)
        y = y.reshape(B_, TT_, C_)
        return y * g @ W_o.T

    def _L0_ffn_ref(hidden_states, w_router, w_gating, w_gate, w_up, w_down):
        import jax, jax.numpy as jnp
        import numpy as np
        B, S, H = (2, 128, 128)
        E, F = (8, 512)
        GATE_TEMP = 0.1
        x = hidden_states
        router_probs = jax.nn.softmax(jnp.einsum('bsh,he->bse', x, w_router), axis=-1)
        gate_weights = jax.nn.softmax(jnp.einsum('bsh,he->bse', x, w_gating) / GATE_TEMP, axis=-1)
        g = jnp.einsum('bsh,ehf->ebsf', x, w_gate)
        u = jnp.einsum('bsh,ehf->ebsf', x, w_up)
        h = jax.nn.silu(g) * u
        expert_out = jnp.einsum('ebsf,efh->ebsh', h, w_down)
        cw = router_probs * gate_weights
        cw = cw / (jnp.sum(cw, axis=-1, keepdims=True) + 1e-09)
        out = jnp.einsum('ebsh,bse->bsh', expert_out, cw)
        return out

    def _L1_attn_ref(x, w_qkv, w_o):
        import jax, jax.numpy as jnp
        import numpy as np
        D_MODEL = 128
        NUM_HEADS = 16
        D_K = D_MODEL // NUM_HEADS
        B, S = (4, 256)
        seq_len = x.shape[-2]
        d_k = w_qkv.shape[-2]
        qkv = jnp.einsum('bsm,qhkm->qbhsk', x, w_qkv)
        Q, K, V = (qkv[0], qkv[1], qkv[2])
        scores = jnp.einsum('bhsk,bhtk->bhst', Q, K) / jnp.sqrt(jnp.asarray(d_k, x.dtype))
        causal = jnp.tril(jnp.ones((seq_len, seq_len), dtype=bool))
        scores = jnp.where(causal, scores, -jnp.inf)
        probs = jax.nn.softmax(scores, axis=-1)
        attn = jnp.einsum('bhst,bhtk->bhsk', probs, V)
        b, h, s, k = attn.shape
        attn_cat = jnp.transpose(attn, (0, 2, 1, 3)).reshape(b, s, h * k)
        return jnp.einsum('bsd,md->bsm', attn_cat, w_o)

    def _L1_ffn_ref(x, router_w, router_b, expert_w, expert_b):
        import jax, jax.numpy as jnp
        import numpy as np
        B, S, D, E = (2, 256, 128, 8)
        logits = jnp.einsum('bsd,ed->bse', x, router_w) + router_b
        probs = jax.nn.softmax(logits, axis=-1)
        weights = jnp.max(probs, axis=-1)
        top1 = jnp.argmax(probs, axis=-1)
        y_all = jnp.einsum('bsd,eod->bseo', x, expert_w) + expert_b
        y = jnp.take_along_axis(y_all, top1[:, :, None, None], axis=2)[:, :, 0, :]
        out = y * weights[:, :, None]
        return out
    x = L0_attn_xq
    x = x + 0.5 * _L0_ffn_ref(_layernorm(x, axis=-1), L0_ffn_w_router, L0_ffn_w_gating, L0_ffn_w_gate, L0_ffn_w_up, L0_ffn_w_down)
    x = x + _L0_attn_ref(_layernorm(x, axis=-1), L0_attn_time_mix_k, L0_attn_time_mix_v, L0_attn_time_mix_r, L0_attn_time_mix_g, L0_attn_time_decay, L0_attn_time_faaaa, L0_attn_W_r, L0_attn_W_k, L0_attn_W_v, L0_attn_W_g, L0_attn_W_o, L0_attn_ln_w, L0_attn_ln_b)
    x = x + 0.5 * _L0_ffn_ref(_layernorm(x, axis=-1), L0_ffn_w_router, L0_ffn_w_gating, L0_ffn_w_gate, L0_ffn_w_up, L0_ffn_w_down)
    x = x + 0.5 * _L1_ffn_ref(_layernorm(x, axis=-1), L1_ffn_router_w, L1_ffn_router_b, L1_ffn_expert_w, L1_ffn_expert_b)
    x = x + _L1_attn_ref(_layernorm(x, axis=-1), L1_attn_w_qkv, L1_attn_w_o)
    x = x + 0.5 * _L1_ffn_ref(_layernorm(x, axis=-1), L1_ffn_router_w, L1_ffn_router_b, L1_ffn_expert_w, L1_ffn_expert_b)
    return x

_drawn_inputs = setup_inputs


def setup_inputs(seed=0):
    import zlib

    import numpy as np

    out = dict(_drawn_inputs(seed))
    spreads = {'L0_attn_ln_w': (1.0, 0.6),
     'L0_attn_ln_b': (0.0, 0.8),
     'L1_ffn_router_b': (0.0, 0.291),
     'L1_ffn_expert_b': (0.0, 0.509)}
    factors = {'L0_attn_time_mix_k': 5.936,
     'L0_attn_time_mix_v': 6.916,
     'L0_attn_time_mix_r': 6.074,
     'L0_attn_time_mix_g': 6.757,
     'L0_attn_time_decay': 3.972,
     'L0_attn_time_faaaa': 8.0}
    for name, (base, spread) in spreads.items():
        noise = np.random.default_rng([zlib.crc32(name.encode()), seed]).standard_normal(out[name].shape)
        drawn = base * np.exp(spread * noise) if base else spread * noise
        out[name] = jnp.asarray(drawn.astype(out[name].dtype))
    for name, factor in factors.items():
        out[name] = (out[name] * factor).astype(out[name].dtype)
    return out
```

```python
from contextlib import ExitStack

import concourse.bass as bass
import numpy as np
from concourse import mybir

F32 = mybir.dt.float32
F16 = mybir.dt.float16
BF16 = mybir.dt.bfloat16
ALU = mybir.AluOpType
ACT = mybir.ActivationFunctionType
AX_X = mybir.AxisListType.X
ds = bass.ds

P = 128
BANK = 512
LN_EPS = 1e-5
GN_EPS = 1e-5
HEAD_DIV = 8.0
GATE_TEMP = 0.1
W_UP = 2.0 ** 6
W_DOWN = 1.0 / W_UP
M_UP = 2.0 ** 12
M_DOWN = 1.0 / M_UP
NEG_BIG = -1e30
EXP_CAP = 1e30

NB, S, C = 8, 512, 128
SUB = S // P
NS = NB * SUB
E, F = 8, 512
H, K = 16, 8
NG, HG = 4, 4
GC = HG * K
STK = 3 * GC
AUG = STK + HG
FC = F // P
PAIRS = E // 2
ITER = NB * PAIRS
CH = 2 * FC
HSLOTS = 4
LEAD = 2 * SUB
XW = S + 8
R_SCALE = float(1.0 / np.sqrt(np.float32(K)))
PHASES = ("F", "R", "F", "E", "M", "E")


def columns(parts):
    at, out = 0, {}
    for name, n in parts:
        out[name] = (at, n)
        at += n
    return out, at


LIN, LIN_N = columns([("mixed", 4 * C), ("wo_r", C), ("experts", E * C), ("router", E), ("q", C), ("k", C), ("v", C), ("wo_m", C)])
COL, COL_N = columns([("mix", 4), ("decay_row", 1), ("ln_w", 1), ("ln_b", 1), ("decay", H), ("bonus", H)])
CON, CON_N = columns([("ident", P), ("head_mean", P), ("head_mean16", H), ("same_head", P), ("rev_index", SUB * E),
                      ("logit_scale", SUB * 2 * E), ("row_head", HG), ("v_head", HG * C), ("distance", P), ("later", P),
                      ("position", P), ("to_end", 1)])
HALF, HALF_N = columns([("ident", P), ("pick_expert", E * P), ("ones", P), ("k_hi", NG * STK), ("k_lo", NG * STK),
                        ("q_hi", NG * STK), ("q_lo", NG * STK)])
BIG, BIG_N = columns([("ident", P), ("keys_after", P), ("queries_before", P)])


def build(nc, x, ffn_router, ffn_w, lin, col, bias, con, half, big, out):
    with ExitStack() as ctx:
        def sb(name, cols, dt=F32):
            return ctx.enter_context(nc.sbuf_tensor(name, [P, cols], dt))

        def sem(name):
            return ctx.enter_context(nc.semaphore(name))

        psum = ctx.enter_context(nc.psum_tensor("psum", [P, 8 * BANK], F32))

        def bank(i, a=0, b=BANK):
            return psum[:, i * BANK + a:i * BANK + b]

        x_tok = sb("x_tok", NS * C)
        facc = sb("facc", NB * S)
        x_hi = sb("x_hi", NB * XW, F16)
        x_lo = sb("x_lo", NB * XW, F16)
        con_sb = sb("con_sb", CON_N)
        half_sb = sb("half_sb", HALF_N, F16)
        big_sb = sb("big_sb", BIG_N, BF16)
        col_sb = sb("col_sb", COL_N)
        neg_half = sb("neg_half", SUB * H)
        e_const = sb("e_const", 2 * E)
        raw = sb("raw", LIN_N + E * C + E)
        bias_raw = raw[:, LIN_N:LIN_N + E * C + E]
        ffn_g = [sb(f"ffn_gate_{h}", E * F, F16) for h in ("hi", "lo")]
        ffn_u = [sb(f"ffn_up_{h}", E * F, F16) for h in ("hi", "lo")]
        ffn_d = [sb(f"ffn_down_{h}", E * F, F16) for h in ("hi", "lo")]
        fr_w = [sb(f"fr_{h}", 2 * E, F16) for h in ("hi", "lo")]
        fr_raw = sb("fr_raw", 2 * E)
        ln_stat = sb("ln_stat", SUB * 6)
        ln_mv = sb("ln_mv", SUB * 2)
        ln_var = sb("ln_var", SUB)
        ln_rstd = sb("ln_rstd", SUB)
        x_norm = sb("x_norm", S)
        merge_in = sb("merge_in", S)

        SCRATCH = 20850
        scratch = sb("scratch", SCRATCH)
        place = [0]

        def carve(cols, dt=F32):
            n = cols if dt == F32 else (cols + 1) // 2
            t = scratch[:, place[0]:place[0] + n]
            place[0] += n
            assert place[0] <= SCRATCH, place[0]
            return t if dt == F32 else t.bitcast(dt)

        x_T = carve(NB * S)
        cw_T = carve(NB * S, F16)
        lg = carve(SUB * 2 * E)
        lg_max = carve(SUB * 2)
        lg_shift = carve(SUB * 2 * E)
        lg_exp = carve(SUB * 2 * E)
        sm_sum = carve(SUB * 2)
        sm_prod = carve(SUB)
        sm_rec = carve(SUB)
        cw_num = carve(SUB * E)
        cw_raw = carve(SUB * E)
        cw_sum = carve(SUB)
        cw_eps = carve(SUB)
        cw_rec = carve(SUB)
        cw_out = carve(SUB * E)
        cw16 = carve(SUB * 2 * E, F16)
        xc = [carve(S) for _ in range(2)]
        xc_hi = [carve(S, F16) for _ in range(2)]
        xc_lo = [carve(S, F16) for _ in range(2)]
        gate_act = [carve(S) for _ in range(2)]
        h32 = [carve(S) for _ in range(2)]
        h_hi = [carve(S, F16) for _ in range(HSLOTS)]
        h_lo = [carve(S, F16) for _ in range(HSLOTS)]

        place[0] = 0
        e_w = [carve(E * C + E, F16) for _ in range(2)]
        bias_w = carve(E * C + E, F16)
        e_lg = carve(SUB * E)
        e_max = carve(SUB)
        e_shift = carve(SUB * E)
        e_exp = carve(SUB * E)
        e_sum = carve(SUB)
        e_rec = carve(SUB)
        e_prob = carve(SUB * E)
        e_top = carve(SUB)
        e_hit = carve(SUB * E)
        e_rank = carve(SUB * E)
        e_first = carve(SUB)
        e_one = carve(SUB * E)
        e_weight = carve(SUB)
        e_sel = carve(SUB * E)
        e_za = [carve(S) for _ in range(2)]
        e_zb = [carve(S) for _ in range(2)]
        e_z4 = [carve(S) for _ in range(2)]
        e_z2 = [carve(S // 2) for _ in range(2)]
        e_z1 = [carve(S // 4) for _ in range(2)]

        place[0] = 0
        mix_scale = carve(8)
        mix_w = [[carve(4 * C, F16) for _ in range(2)] for _ in range(2)]
        r_wo = [carve(C, F16) for _ in range(2)]
        decay_neg = carve(H)
        decay_row = carve(1)
        w_intra = carve(H * P)
        w_qexp = carve(P)
        w_query = carve(P)
        w_chunk = carve(1)
        w_kexp = carve(H)
        w_key = carve(H)
        rk = [[carve(S, F16) for _ in range(2)] for _ in range(2)]
        r_decay = carve(2 * S)
        r_st = [carve(NG * HG * P, F16) for _ in range(SUB)]
        k_stk = [carve(NG * P, F16) for _ in range(SUB)]
        k_w = [carve(C) for _ in range(SUB - 1)]
        v_tok = [carve(C) for _ in range(SUB - 1)]
        v_by_head = [carve(HG * C) for _ in range(SUB)]
        setup_at = place[0]
        att = [[carve(S) for _ in range(NG)] for _ in range(2)]
        st_new = carve(C)
        state = [None] + [carve(C) for _ in range(SUB - 1)]
        y_at = place[0]
        y8 = carve(S)
        y_c = carve(S)
        y_sq = carve(S)
        g_var = carve(SUB * H)
        g_rstd = carve(SUB * H)
        silu_g = carve(S)
        y_n, g_wide, y_aff, y_g = y8, y_sq, y_sq, y_c
        y_parts = [carve(S, F16) for _ in range(2)]
        y_end, place[0] = place[0], setup_at
        w_exp = carve(H * P)
        w_later = carve(H * P)
        assert place[0] <= setup_at + 2 * NG * S
        place[0] = y_at
        mixed = [carve(4 * C) for _ in range(2)]
        assert place[0] <= y_end

        place[0] = 0
        m_w = [carve(4 * C, F16) for _ in range(2)]
        qk = [[carve(S, F16) for _ in range(2)] for _ in range(2)]
        q_stack = [carve(S, F16) for _ in range(2)]
        k_stack = [carve(S, F16) for _ in range(NG)]
        q_by_head = [carve(HG * S, F16) for _ in range(NG)]
        m_aug = carve(S, F16)
        neg_max = carve(SUB * HG)
        max_pad = carve(SUB * P, F16)
        v_aug = carve(SUB * H * 32)
        probs = [carve(HG * S) for _ in range(2)]
        y_raw = carve(S)
        den_rec = carve(SUB * HG)
        y_tok = carve(S)
        yo = [carve(S, F16) for _ in range(2)]

        def con_(name):
            a, n = CON[name]
            return con_sb[:, a:a + n]

        def half_(name):
            a, n = HALF[name]
            return half_sb[:, a:a + n]

        def col_(name):
            a, n = COL[name]
            return col_sb[:, a:a + n]

        def raw_(name):
            a, n = LIN[name]
            return raw[:, a:a + n]

        def pick(name, g):
            return half_(name)[:, g * STK:(g + 1) * STK]

        ident = con_("ident")
        ident16 = half_("ident")

        def sub(t, s, n=1):
            return t[:, ds(s * P, n * P)]

        def seq(t, b):
            return t[:, ds(b * S, S)]

        def xsub(t, s):
            return t[:, ds((s // SUB) * XW + 8 + (s % SUB) * P, P)]

        def xchunk(t, b, n, before):
            return t[:, ds(b * XW + (8 + n * P - before), P)]

        def xseq(t, b, before=0):
            return t[:, ds(b * XW + (8 - before), S)]

        def by(t, n):
            return t.rearrange("p (n c) -> p n c", n=n)

        def over(t, n, c):
            return t.rearrange("p (n o) -> p n o", o=1).to_broadcast([P, n, c])

        s_x = [sem(n) for n in ("x_loaded_first", "x_loaded_second", "x_loaded_rest")]
        s_fr = sem("ffn_router_loaded")
        s_con = sem("consts_loaded")
        s_lin = sem("other_weights_loaded")
        s_wraw = [sem(f"ffn_w_loaded{q}") for q in range(2)]
        s_pool_const = sem("pool_consts_set")
        s_bz = sem("bias_rows_cleared")
        s_frhi, s_frlo, s_whi, s_wlo = sem("router_hi"), sem("router_lo"), sem("ffn_w_hi"), sem("ffn_w_lo")
        s_bn, s_mv, s_var, s_rstd, s_xn, s_xT, s_xTs, s_xhi, s_xlo = [sem(n) for n in (
            "bn_stats_done", "mean_var_done", "var_ready", "rstd_ready", "x_norm_ready", "xT_in_psum", "xT_copied",
            "x_hi_ready", "x_lo_ready")]
        s_mrg_in, s_mrg_ps, s_mrg = sem("merge_in_ready"), sem("merge_in_psum"), sem("merged")
        s_lg, s_lgs, s_exp, s_cw, s_cwTp, s_cwT = [sem(n) for n in (
            "logits_in_psum", "logits_shifted", "logits_exp", "cw_ready", "cwT_in_psum", "cwT_ready")]
        s_rstep = sem("routing_step")
        ROUTE_STEPS = 11
        s_bc, s_xc, s_xchi, s_xclo = [sem(n) for n in ("cw_broadcast", "xc_ready", "xc_hi_ready", "xc_lo_ready")]
        s_g, s_u, s_s, s_h, s_hhi, s_hlo, s_hfree = [sem(n) for n in (
            "gate_in_psum", "up_in_psum", "gate_act_ready", "h_ready", "h_hi_ready", "h_lo_ready", "h_slot_free")]
        s_facc = sem("ffn_out_added")
        s_ewhi, s_ewlo, s_bhi, s_blo = [sem(n) for n in ("e_w_hi", "e_w_lo", "bias_hi", "bias_lo")]
        s_elg, s_elgd, s_esh, s_eexp, s_esel = [sem(n) for n in (
            "e_logits_in_psum", "e_logits_scaled", "e_logits_shifted", "e_exp", "e_selected")]
        s_estep = sem("e_routing_step")
        E_STEPS = 9
        s_eya, s_eyb, s_eza, s_ezb, s_ez4, s_ez2, s_ez1, s_eadd = [sem(n) for n in (
            "e_low_experts_in_psum", "e_high_experts_in_psum", "e_low_weighted", "e_high_weighted", "e_four_left",
            "e_two_left", "e_one_left", "e_added")]
        s_st = sem("stored")

        plan, n_merge, seen = [], 0, dict(F=0, E=0, R=0, M=0)
        for i, kind in enumerate(PHASES):
            merge = i > 0 and PHASES[i - 1] == "F"
            plan.append(dict(i=i, kind=kind, n0=i * NS, use=seen[kind], merge=merge, g0=n_merge))
            n_merge += NB if merge else 0
            seen[kind] += 1

        def begin(eng, i):
            if i == 0:
                return
            before = plan[i - 1]
            if before["kind"] == "F":
                eng.wait_ge(s_facc, (before["use"] + 1) * (ITER + 1))
            if before["kind"] == "E":
                eng.wait_ge(s_eadd, (before["use"] + 1) * NS + 1)
            if before["kind"] == "R":
                eng.wait_ge(s_rout, NB + 1)
            if before["kind"] == "M":
                eng.wait_ge(s_mout, NB)

        s_rset, s_rexp, s_rwhi, s_rwlo = sem("rwkv_setup"), sem("rwkv_exps"), sem("rwkv_w_hi"), sem("rwkv_w_lo")
        s_rp, s_rhi, s_rlo, s_rdec, s_kp, s_khi, s_klo = [sem(n) for n in (
            "r_in_psum", "r_hi_ready", "r_lo_ready", "r_decay_ready", "k_in_psum", "k_hi_ready", "k_lo_ready")]
        s_y8, s_gmean, s_yc, s_ysq, s_gvarp, s_gvar, s_grstd, s_gp, s_sg, s_gwide, s_grb, s_yn, s_yaff, s_yg, s_yghi, s_yglo, s_rop, s_rout = [
            sem(n) for n in ("y_copied", "gn_mean_in_psum", "gn_centred", "gn_squares", "gn_var_in_psum", "gn_var_ready",
                             "gn_rstd_ready", "g_in_psum", "silu_g_ready", "gn_rstd_repeated", "gn_rstd_in_psum", "gn_normed", "gn_affine",
                             "y_gated", "y_hi_ready", "y_lo_ready", "rwkv_out_in_psum", "rwkv_added")]
        s_rst, s_kst, s_kv, s_rbyh, s_kstk, s_kw, s_vtok, s_vbyh, s_stp, s_stm, s_state, s_av = [sem(n) for n in (
            "r_stack_in_psum", "k_stack_in_psum", "kv_in_psum", "r_by_head", "k_stack_ready", "k_weighted", "v_ready",
            "v_by_head", "state_in_psum", "state_masked", "state_ready", "att_used")]
        s_attp, s_attw = sem("att_in_psum"), sem("att_weighted")
        s_mset, s_mpad0, s_mwhi, s_mwlo = sem("attention_setup"), sem("max_pad_cleared"), sem("attention_w_hi"), sem("attention_w_lo")
        s_mqp, s_mqhi, s_mqlo, s_mkp, s_mkhi, s_mklo, s_mvp, s_mv_in = [sem(n) for n in (
            "mq_in_psum", "mq_hi_ready", "mq_lo_ready", "mk_in_psum", "mk_hi_ready", "mk_lo_ready", "mv_in_psum", "mv_ready")]
        s_yTp, s_yohi, s_yolo, s_mop, s_mout = [sem(n) for n in (
            "my_transposed", "my_hi_ready", "my_lo_ready", "attention_out_in_psum", "attention_added")]
        s_mks, s_mqs, s_mkst, s_mqst, s_mqh, s_mmax, s_mpad, s_mTp, s_maug, s_mqaug, s_yraw, s_ytp, s_drec, s_ytok = [
            sem(n) for n in ("mk_stack_in_psum", "mq_stack_in_psum", "mk_stack_ready", "mq_stack_ready", "mq_by_head",
                             "max_ready", "max_padded", "max_transposed", "max_rows_ready", "max_rows_by_head",
                             "weighted_values_copied", "weighted_values_transposed",
                             "denominator_rec", "attention_normed")]
        s_p1, s_p1used = sem("scores_by_query_in_psum"), sem("scores_by_query_used")
        s_p2, s_p2exp = sem("scores_by_key_in_psum"), sem("probs_ready")
        s_pvq = sem("probs_used")
        block = ctx.enter_context(nc.Block())

        Q_TILES = [(0, 0, 4), (1, 0, 2), (1, 2, 2)] + [(q, r, 1) for q in (2, 3) for r in range(HG)]
        K_TILES = [(j, r, 1) for j in (0, 1) for r in range(HG)] + [(2, 0, 2), (2, 2, 2), (3, 0, 4)]
        QT, KT = len(Q_TILES), len(K_TILES)
        KT_END = [sum(t[0] <= j for t in K_TILES) for j in range(SUB)]
        UNITS = NB * NG
        PV_CREDIT = SUB * NG

        def units_done(n):
            return SUB * n + PV_CREDIT

        @block.sync
        def _(sp):
            def load_x(b):
                sp.dma_start(x_tok[:, b * S:(b + 1) * S], x[:, b * S:(b + 1) * S]).then_inc(s_x[min(b, 2)], 16)

            load_x(0)
            sp.dma_start(con_sb[:], con).then_inc(s_con, 16)
            sp.dma_start(half_sb[:], half).then_inc(s_con, 16)
            sp.dma_start(fr_raw[:], ffn_router).then_inc(s_fr, 16)
            load_x(1)
            for e in range(E):
                if e >= 2:
                    sp.wait_ge(s_wlo, 3 * (e - 1))
                q = e % 2
                sp.dma_start(raw[:, 3 * F * q:3 * F * (q + 1)], ffn_w[e]).then_inc(s_wraw[q], 16)
            for b in range(2, NB):
                load_x(b)
            sp.dma_start(big_sb[:], big).then_inc(s_con, 16)
            sp.dma_start(col_sb[:], col).then_inc(s_con, 16)
            sp.wait_ge(s_wlo, 3 * E)
            sp.dma_start(raw[:, 0:LIN_N], lin).then_inc(s_lin, 16)
            sp.wait_ge(s_bz, 1)
            sp.dma_start(bias_raw[0:1, :], bias[0:1, :]).then_inc(s_lin, 16)
            sp.dma_start(bias_raw[32:33, :], bias[1:2, :]).then_inc(s_lin, 16)
            sp.wait_ge(s_lin, 48)
            begin(sp, len(plan))
            sp.dma_start(out, x_tok[:]).then_inc(s_st, 16)
            sp.wait_ge(s_st, 16)

        @block.gpsimd
        def _(pool):
            def prep_rstd(n, g):
                pool.wait_ge(s_var, n + g)
                pool.tensor_tensor(ln_rstd[:, 0:g], ln_var[:, 0:g], neg_half[:, 0:g], ALU.pow).then_inc(s_rstd, g)

            pool.memset(neg_half[:], -0.5).then_inc(s_pool_const, 1)
            pool.memset(e_const[:], float(np.exp(1.0))).then_inc(s_pool_const, 1)
            pool.memset(by(x_hi[:], NB)[:, :, 0:8], 0.0).then_inc(s_pool_const, 1)
            pool.memset(by(x_lo[:], NB)[:, :, 0:8], 0.0).then_inc(s_pool_const, 1)
            pool.wait_ge(s_pool_const, 2)

            def clear_bias():
                pool.wait_ge(s_wlo, 3 * E)
                pool.memset(bias_raw, 0.0).then_inc(s_bz, 1)

            def ffn(ph):
                f, n0 = ph["use"], ph["n0"]
                r0, m0 = f * NS, f * NB * E

                def exps(n):
                    pool.wait_ge(s_lgs, n + 1)
                    pool.tensor_tensor(lg_exp[:, 0:2 * E], e_const[:], lg_shift[:, 0:2 * E], ALU.pow).then_inc(s_exp, 1)

                def xc_low(m, q):
                    pool.wait_ge(s_xchi, m + 1)
                    pool.tensor_tensor(xc_lo[q], xc[q], xc_hi[q], ALU.subtract).then_inc(s_xclo, 1)

                begin(pool, ph["i"])
                pool.memset(cw_T, 0.0).then_inc(s_pool_const, 1)
                pool.memset(facc[:], 0.0).then_inc(s_facc, 1)
                for s in (0, SUB):
                    prep_rstd(n0 + s, SUB)
                if f == 0:
                    clear_bias()
                xc_low(m0, 0)
                xc_low(m0 + 1, 1)

                def body(i, prepare, last):
                    s = i + LEAD
                    if prepare:
                        prep_rstd(n0 + s, 1)
                    if not last:
                        xc_low(m0 + 2 * i + 2, 0)
                    if prepare:
                        exps(r0 + s)
                    if not last:
                        xc_low(m0 + 2 * i + 3, 1)

                with pool.Fori(0, ITER - LEAD) as i:
                    body(i, True, False)
                with pool.Fori(ITER - LEAD, ITER - 1) as i:
                    body(i, False, False)
                body(ITER - 1, False, True)

            def moe(ph):
                n0, t0 = ph["n0"], ph["use"] * NS

                def fold(t, q):
                    pool.wait_ge(s_eza, t + 3)
                    pool.wait_ge(s_ezb, t + 3)
                    pool.tensor_tensor(e_z4[q], e_za[q], e_zb[q], ALU.add).then_inc(s_ez4, 1)
                    pool.wait_ge(s_ez4, t + 3)
                    pool.wait_ge(s_ez1, t + 1)
                    pool.tensor_tensor(e_z2[q], e_z4[q][:, 0:2 * C], e_z4[q][:, 2 * C:4 * C], ALU.add).then_inc(s_ez2, 1)

                prep_rstd(n0, SUB)

                def body(b, last):
                    if not last:
                        prep_rstd(n0 + SUB * b + SUB, SUB)
                    for k in range(SUB):
                        fold(t0 + b * SUB + k, k % 2)

                with pool.Fori(0, NB - 1) as b:
                    body(b, False)
                body(NB - 1, True)

            def rwkv(ph):
                n0 = ph["n0"]

                def gn_rstd(b):
                    pool.wait_ge(s_gvar, b + 1)
                    pool.tensor_tensor(g_rstd, g_var, neg_half[:, 0:SUB * H], ALU.pow).then_inc(s_grstd, 1)

                def gate(b):
                    pool.wait_ge(s_yaff, b + 1)
                    pool.wait_ge(s_sg, b + 1)
                    pool.tensor_tensor(y_g, y_aff, silu_g, ALU.mult).then_inc(s_yg, 1)

                def gate_low(b):
                    pool.wait_ge(s_yghi, b + 1)
                    pool.tensor_tensor(y_parts[1], y_g, y_parts[0], ALU.subtract).then_inc(s_yglo, 1)

                begin(pool, ph["i"])
                prep_rstd(n0, SUB)
                prep_rstd(n0 + SUB, SUB)

                def body(b, first, prep):
                    if not first:
                        gn_rstd(b - 1)
                    if prep:
                        prep_rstd(n0 + SUB * b + 2 * SUB, SUB)
                    if not first:
                        gate(b - 1)
                        gate_low(b - 1)

                body(0, True, True)
                with pool.Fori(1, NB - 2) as b:
                    body(b, False, True)
                body(NB - 2, False, False)
                body(NB - 1, False, False)
                gn_rstd(NB - 1)
                gate(NB - 1)
                gate_low(NB - 1)

            def attention(ph):
                n0 = ph["n0"]

                def mask_queries(u, g):
                    pool.wait_ge(s_mqst, u + 1)
                    pool.wait_ge(s_pvq, units_done(u - 3))
                    stack = q_stack[g % 2][0:STK].rearrange("p (o i) -> p o i", o=1).to_broadcast([STK, HG, S])
                    mask = con_("row_head")[0:STK].rearrange("p (r o) -> p r o", o=1).to_broadcast([STK, HG, S])
                    pool.tensor_tensor(by(q_by_head[g][0:STK], HG), stack, mask, ALU.mult).then_inc(s_mqh, 1)

                begin(pool, ph["i"])
                pool.memset(v_aug, 0.0).then_inc(s_mset, 1)
                pool.wait_ge(s_mset, 1)
                pool.memset(by(v_aug, SUB * H)[:, :, K:2 * K], 1.0).then_inc(s_mset, 1)
                prep_rstd(n0, SUB)
                prep_rstd(n0 + SUB, SUB)
                pool.wait_ge(s_con, 64)
                for u in range(3):
                    mask_queries(u, u)

                def body(b, prep, more):
                    for g in range(NG):
                        u = NG * b + g
                        if more or g < NG - 3:
                            mask_queries(u + 3, (g + 3) % NG)
                        if g == 1 and prep:
                            prep_rstd(n0 + SUB * b + 2 * SUB, SUB)

                body(0, True, True)
                with pool.Fori(1, NB - 2) as b:
                    body(b, True, True)
                body(NB - 2, False, True)
                body(NB - 1, False, False)

            for ph in plan:
                dict(F=ffn, E=moe, R=rwkv, M=attention)[ph["kind"]](ph)

        @block.scalar
        def _(act):
            def prep_merge(m, b):
                act.wait_ge(s_mrg_ps, m)
                act.activation(merge_in[:], seq(facc, b), ACT.Copy).then_inc(s_mrg_in, 1)

            def prep_xT(n, s, g, keep, at=6):
                act.wait_ge(s_xT, n + g)
                if keep:
                    act.activation(sub(x_T, s, g), bank(at, 0, g * P), ACT.Copy).then_inc(s_xTs, g)
                dst = xsub(x_hi, s) if g == 1 else xseq(x_hi, s // SUB)
                act.activation(dst, bank(at, 0, g * P), ACT.Copy).then_inc(s_xhi, g)

            def ffn(ph):
                f, n0 = ph["use"], ph["n0"]
                r0, m0, c0 = f * NS, f * NB * E, f * ITER * CH

                def copy_cwT(n, s, g):
                    act.wait_ge(s_cwTp, n + g)
                    act.activation(cw_T[0:2 * E, ds(s * P, g * P)], bank(7, 64, 64 + g * P // 2)[0:2 * E].bitcast(F16),
                                   ACT.Copy).then_inc(s_cwT, g)

                def silu(c, k):
                    act.wait_ge(s_g, c + 1)
                    if k >= 2 or f:
                        act.wait_ge(s_h, c - 1)
                    act.activation(gate_act[k % 2], bank(k % 2), ACT.Silu, scale=W_DOWN).then_inc(s_s, 1)

                def h_high(c, k):
                    act.wait_ge(s_h, c + 1)
                    act.wait_ge(s_hfree, c + 1)
                    act.activation(h_hi[k % HSLOTS], h32[k % 2], ACT.Copy).then_inc(s_hhi, 1)

                def xc_high(m, q, chunks_used):
                    act.wait_ge(s_xc, m + 1)
                    if chunks_used is not None:
                        act.wait_ge(s_u, chunks_used)
                    act.activation(xc_hi[q], xc[q], ACT.Copy).then_inc(s_xchi, 1)

                begin(act, ph["i"])
                if f == 0:
                    act.wait_ge(s_fr, 16)
                    act.activation(fr_w[0][:], fr_raw[:], ACT.Copy, scale=W_UP).then_inc(s_frhi, 1)
                for s in (0, SUB):
                    prep_xT(n0 + s, s, SUB, True)
                    act.wait_ge(s_lgs, r0 + s + SUB)
                    act.activation(lg_exp, lg_shift, ACT.Exp).then_inc(s_exp, SUB)
                    if s == 0:
                        act.wait_ge(s_pool_const, 4 + f + 1)
                    copy_cwT(r0 + s, s, SUB)
                if f == 0:
                    for e in range(E):
                        act.wait_ge(s_wraw[e % 2], 16 * (e // 2 + 1))
                        for t, w in enumerate((ffn_g, ffn_u, ffn_d)):
                            a = 3 * F * (e % 2) + t * F
                            act.activation(w[0][:, e * F:(e + 1) * F], raw[:, a:a + F], ACT.Copy, scale=W_UP).then_inc(s_whi, 1)
                xc_high(m0, 0, None)
                xc_high(m0 + 1, 1, None)
                silu(c0, 0)
                silu(c0 + 1, 1)
                h_high(c0, 0)

                def body(i, prepare, last):
                    c = c0 + i * CH
                    s = i + LEAD
                    for k in range(CH):
                        if not (last and k + 2 >= CH):
                            silu(c + k + 2, k + 2)
                        if not (last and k + 1 >= CH):
                            h_high(c + k + 1, k + 1)
                        if not last and k == 2:
                            xc_high(m0 + 2 * i + 2, 0, c + FC)
                        if not last and k == 6:
                            xc_high(m0 + 2 * i + 3, 1, c + 2 * FC)
                        if prepare and k == 3:
                            prep_xT(n0 + s, s, 1, True)
                        if prepare and k == 7:
                            copy_cwT(r0 + s, s, 1)

                with act.Fori(0, ITER - LEAD) as i:
                    body(i, True, False)
                with act.Fori(ITER - LEAD, ITER - 1) as i:
                    body(i, False, False)
                body(ITER - 1, False, True)

            def moe(ph):
                n0, use = ph["n0"], ph["use"]
                t0, b0 = use * NS, use * NB

                def exps(b):
                    act.wait_ge(s_esh, b + 1)
                    act.activation(e_exp, e_shift, ACT.Exp).then_inc(s_eexp, 1)

                def weigh(t, b, k):
                    act.wait_ge(s_esel, 2 * b + 2)
                    act.wait_ge(s_eya, t + 1)
                    act.wait_ge(s_ez4, t + 1)
                    for e in range(E // 2):
                        ins = act.activation(e_za[k % 2][:, e * C:(e + 1) * C], bank(2 * (k % 2), e * C, (e + 1) * C), ACT.Copy,
                                             scale=e_sel[:, k * E + e:k * E + e + 1])
                        if e == E // 2 - 1:
                            ins.then_inc(s_eza, 1)

                begin(act, ph["i"])
                act.wait_ge(s_lin, 48)
                act.wait_ge(s_con, 64)
                act.activation(e_w[0], raw[:, LIN["experts"][0]:LIN["experts"][0] + E * C + E], ACT.Copy, scale=W_UP).then_inc(s_ewhi, 1)
                act.activation(bias_w, bias_raw, ACT.Copy, scale=W_UP).then_inc(s_bhi, 1)
                if ph["merge"]:
                    prep_merge(ph["g0"], 0)
                prep_xT(n0, 0, SUB, False)
                exps(b0)

                def body(b, last):
                    if not last and ph["merge"]:
                        prep_merge(ph["g0"] + b + 1, b + 1)
                    for k in range(SUB):
                        weigh(t0 + b * SUB + k, b0 + b, k)
                        if k == 1 and not last:
                            prep_xT(n0 + SUB * b + SUB, (b + 1) * SUB, SUB, False)
                    if not last:
                        exps(b0 + b + 1)

                with act.Fori(0, NB - 1) as b:
                    body(b, False)
                body(NB - 1, True)

            def rwkv(ph):
                n0 = ph["n0"]

                def r_high(b):
                    act.wait_ge(s_rp, b + 1)
                    act.wait_ge(s_rst, SUB * b)
                    act.activation(rk[0][0], bank(6), ACT.Copy, scale=W_DOWN).then_inc(s_rhi, 1)

                def k_high(b):
                    act.wait_ge(s_kp, b + 1)
                    act.wait_ge(s_kst, SUB * b)
                    act.activation(rk[1][0], bank(6), ACT.Copy, scale=W_DOWN).then_inc(s_khi, 1)

                def stacks(u, n):
                    act.wait_ge(s_rst, u + 1)
                    act.wait_ge(s_attp, SUB * u + SUB)
                    dst = r_st[n][0:STK].rearrange("p (g r i) -> p g r i", g=NG, r=HG)
                    for r in range(HG):
                        ins = act.activation(dst[:, :, r], by(bank(5)[0:STK], NG), ACT.Copy, scale=con_("row_head")[0:STK, r:r + 1])
                    ins.then_inc(s_rbyh, 1)
                    act.wait_ge(s_kst, u + 1)
                    act.activation(k_stk[n][0:STK], bank(3)[0:STK], ACT.Copy).then_inc(s_kstk, 1)

                def y_copy(b):
                    act.wait_ge(s_av, SUB * b + 2 * SUB)
                    act.wait_ge(s_rout, b + 1)
                    act.activation(y8, bank(4), ACT.Copy, scale=1.0 / HEAD_DIV).then_inc(s_y8, 1)

                def squares(b):
                    act.wait_ge(s_yc, b + 1)
                    act.activation(y_sq, y_c, ACT.Square).then_inc(s_ysq, 1)

                def gate_silu(b):
                    act.wait_ge(s_gp, b + 1)
                    act.activation(silu_g, bank(2), ACT.Silu, scale=W_DOWN).then_inc(s_sg, 1)

                def widen_rstd(b):
                    act.wait_ge(s_grstd, b + 1)
                    act.activation(by(g_wide, SUB * H), over(g_rstd, SUB * H, K), ACT.Copy).then_inc(s_gwide, 1)

                def affine(b):
                    act.wait_ge(s_yn, b + 1)
                    act.activation(y_aff, y_n, ACT.Identity, scale=col_("ln_w"), bias=col_("ln_b")).then_inc(s_yaff, 1)

                def y_high(b):
                    act.wait_ge(s_yg, b + 1)
                    act.activation(y_parts[0], y_g, ACT.Copy).then_inc(s_yghi, 1)

                begin(act, ph["i"])
                act.wait_ge(s_lin, 48)
                act.wait_ge(s_con, 64)
                act.activation(w_kexp, col_("decay"), ACT.Exp).then_inc(s_rexp, 1)
                act.activation(w_qexp[:, 0:1], col_("decay_row"), ACT.Exp).then_inc(s_rexp, 1)
                act.wait_ge(s_rset, 2)
                for h in range(H):
                    ins = act.activation(w_exp[:, h * P:(h + 1) * P], con_("distance"), ACT.Exp, scale=decay_neg[:, h:h + 1])
                ins.then_inc(s_rexp, 1)
                act.activation(w_kexp, decay_neg, ACT.Exp, scale=con_("to_end")).then_inc(s_rexp, 1)
                act.activation(w_chunk, decay_row, ACT.Exp, scale=float(P)).then_inc(s_rexp, 1)
                act.activation(w_qexp, con_("position"), ACT.Exp, scale=decay_row).then_inc(s_rexp, 1)
                for m in range(2):
                    act.wait_ge(s_rset, 4 + m)
                    act.activation(mix_w[m][0], mixed[m], ACT.Copy).then_inc(s_rwhi, 1)
                act.activation(r_wo[0], raw_("wo_r"), ACT.Copy, scale=W_UP).then_inc(s_rwhi, 1)
                for b in range(2):
                    if ph["merge"]:
                        prep_merge(ph["g0"] + b, b)
                    prep_xT(n0 + SUB * b, SUB * b, SUB, False)
                r_high(0)
                k_high(0)
                stacks(0, 0)
                stacks(1, 1)

                def body(b, first, prep, more):
                    for n in range(SUB):
                        if n == 0 and not first:
                            y_copy(b - 1)
                        if n == 0 and prep and ph["merge"]:
                            prep_merge(ph["g0"] + b + 2, b + 2)
                        if more or n < SUB - 2:
                            stacks(SUB * b + n + 2, (n + 2) % SUB)
                        if n == 0 and not first:
                            squares(b - 1)
                        if n == 1 and more:
                            r_high(b + 1)
                        if n == 1 and not first:
                            gate_silu(b - 1)
                        if n == 1 and more:
                            k_high(b + 1)
                        if n == 2 and prep:
                            prep_xT(n0 + SUB * b + 2 * SUB, SUB * b + 2 * SUB, SUB, False)
                        if n == 2 and not first:
                            widen_rstd(b - 1)
                            affine(b - 1)
                        if n == 3 and not first:
                            y_high(b - 1)

                body(0, True, True, True)
                with act.Fori(1, NB - 2) as b:
                    body(b, False, True, True)
                body(NB - 2, False, False, True)
                body(NB - 1, False, False, False)
                for step in (y_copy, squares, gate_silu, widen_rstd, affine, y_high):
                    step(NB - 1)

            def attention(ph):
                n0 = ph["n0"]

                def q_high(b):
                    act.wait_ge(s_mqp, b + 1)
                    act.wait_ge(s_mqs, NG * b)
                    act.activation(qk[0][0], bank(4), ACT.Copy, scale=W_DOWN).then_inc(s_mqhi, 1)

                def k_high(b):
                    act.wait_ge(s_mkp, b + 1)
                    act.wait_ge(s_mks, NG * b)
                    act.activation(qk[1][0], bank(4), ACT.Copy, scale=W_DOWN).then_inc(s_mkhi, 1)

                def query_stack(u, g):
                    act.wait_ge(s_mqs, u + 1)
                    act.wait_ge(s_mqh, u + 1)
                    act.activation(q_stack[g % 2][0:STK], bank(6)[0:STK], ACT.Copy).then_inc(s_mqst, 1)

                def maxima(u):
                    act.wait_ge(s_mTp, u + 1)
                    act.wait_ge(s_mqaug, u)
                    act.activation(m_aug[STK:AUG], bank(6)[STK:AUG], ACT.Copy).then_inc(s_maug, 1)

                def exps(u, g):
                    for t, (j, r, n) in enumerate(K_TILES):
                        w = S - j * P
                        act.wait_ge(s_p2, KT * u + t + 1)
                        act.wait_ge(s_pvq, SUB * u + j - 1 + PV_CREDIT)
                        act.activation(probs[j % 2][:, r * w:(r + n) * w], bank((g + t) % 2, 0, n * w), ACT.Exp,
                                       scale=R_SCALE).then_inc(s_p2exp, 1)

                def values(u):
                    act.wait_ge(s_pvq, units_done(u + 1))
                    act.wait_ge(s_ytp, u)
                    act.activation(y_raw, bank(7), ACT.Copy).then_inc(s_yraw, 1)

                def out_high(b):
                    act.wait_ge(s_yTp, b + 1)
                    act.wait_ge(s_mop, b + 1)
                    act.activation(yo[0], bank(4), ACT.Copy).then_inc(s_yohi, 1)

                begin(act, ph["i"])
                act.wait_ge(s_lin, 48)
                act.wait_ge(s_con, 64)
                a = LIN["q"][0]
                act.activation(m_w[0], raw[:, a:a + 4 * C], ACT.Copy, scale=W_UP).then_inc(s_mwhi, 1)
                for b in range(2):
                    prep_xT(n0 + SUB * b, SUB * b, SUB, False, 4)
                q_high(0)
                k_high(0)
                for u in range(3):
                    query_stack(u, u)
                maxima(0)

                def body(b, first, prep, more):
                    for g in range(NG):
                        u = NG * b + g
                        if more or g < NG - 1:
                            maxima(u + 1)
                        if g == 0 and not first:
                            out_high(b - 1)
                        if g == 1 and more:
                            k_high(b + 1)
                        exps(u, g)
                        values(u)
                        if more or g < NG - 3:
                            query_stack(u + 3, (g + 3) % NG)
                        if g == 0 and more:
                            q_high(b + 1)
                        if g == 2 and prep:
                            prep_xT(n0 + SUB * b + 2 * SUB, SUB * b + 2 * SUB, SUB, False, 4)

                body(0, True, True, True)
                with act.Fori(1, NB - 2) as b:
                    body(b, False, True, True)
                body(NB - 2, False, False, True)
                body(NB - 1, False, False, False)
                out_high(NB - 1)

            for ph in plan:
                dict(F=ffn, E=moe, R=rwkv, M=attention)[ph["kind"]](ph)

        @block.vector
        def _(dve):
            def prep_add(m, b):
                dve.wait_ge(s_mrg_ps, m + 1)
                dve.tensor_tensor(seq(x_tok, b), seq(x_tok, b), bank(6), ALU.add).then_inc(s_mrg, 1)

            def prep_bn(n, s, g):
                for q in range(g):
                    ins = dve.bn_stats(ln_stat[:, 6 * q:6 * q + 6], sub(x_tok, s + q))
                ins.then_inc(s_bn, g)
                dve.wait_ge(s_bn, n + g)

            def prep_aggr(n, g):
                for q in range(g):
                    ins = dve.bn_aggr(ln_mv[:, 2 * q:2 * q + 2], ln_stat[:, 6 * q:6 * q + 6])
                ins.then_inc(s_mv, g)
                dve.wait_ge(s_mv, n + g)
                dve.tensor_scalar(ln_var[:, 0:g], ln_mv[:, 1:2 * g:2], LN_EPS, None, ALU.add).then_inc(s_var, g)

            def prep_norm(n, s, g):
                dve.wait_ge(s_rstd, n + g)
                dve.wait_ge(s_xT, n)
                for q in range(g):
                    ins = dve.tensor_scalar(x_norm[:, q * P:(q + 1) * P], sub(x_tok, s + q), ln_mv[:, 2 * q:2 * q + 1],
                                            ln_rstd[:, q:q + 1], ALU.subtract, ALU.mult)
                ins.then_inc(s_xn, g)

            def prep_low(n, s, g, at=6):
                dve.wait_ge(s_xhi, n + g)
                lo, hi = [xsub(t, s) if g == 1 else xseq(t, s // SUB) for t in (x_lo, x_hi)]
                dve.tensor_tensor(lo, bank(at, 0, g * P), hi, ALU.subtract).then_inc(s_xlo, g)

            def low_weights(w, cols, a):
                return dve.scalar_tensor_tensor(w[1][:, cols], raw[:, a:a + cols.stop - cols.start], W_UP, w[0][:, cols], ALU.mult, ALU.subtract)

            def all_loaded():
                for s, n in zip(s_x, (1, 1, NB - 2)):
                    dve.wait_ge(s, 16 * n)

            def ffn(ph):
                f, n0 = ph["use"], ph["n0"]
                r0, m0, c0, a0 = f * NS, f * NB * E, f * ITER * CH, f * ITER

                def step(n, g, k):
                    dve.wait_ge(s_rstep, n * ROUTE_STEPS + k * g)

                def shift_logits(n, g):
                    dve.wait_ge(s_lg, n + g)
                    w = 2 * E * g
                    dve.tensor_tensor(lg[:, 0:w], bank(7, 0, w), con_("logit_scale")[:, 0:w], ALU.mult).then_inc(s_rstep, g)
                    step(n, g, 1)
                    dve.tensor_reduce(lg_max[:, 0:2 * g], by(lg[:, 0:w], 2 * g), AX_X, ALU.max).then_inc(s_rstep, g)
                    step(n, g, 2)
                    dve.tensor_tensor(by(lg_shift[:, 0:w], 2 * g), by(lg[:, 0:w], 2 * g), over(lg_max[:, 0:2 * g], 2 * g, E),
                                      ALU.subtract).then_inc(s_lgs, g)

                def combine(n, g):
                    w = 2 * E * g
                    ex = lg_exp[:, 0:w].rearrange("p (g s e) -> p g s e", g=g, s=2)
                    num, cwr, cwo = [by(t[:, 0:E * g], g) for t in (cw_num, cw_raw, cw_out)]
                    parts = cw16[:, 0:w].rearrange("p (g s e) -> p g s e", g=g, s=2)
                    dve.wait_ge(s_exp, n + g)
                    dve.tensor_reduce(sm_sum[:, 0:2 * g], by(lg_exp[:, 0:w], 2 * g), AX_X, ALU.add).then_inc(s_rstep, g)
                    dve.tensor_tensor(num, ex[:, :, 0], ex[:, :, 1], ALU.mult).then_inc(s_rstep, g)
                    step(n, g, 4)
                    dve.tensor_tensor(sm_prod[:, 0:g], sm_sum[:, 0:2 * g:2], sm_sum[:, 1:2 * g:2], ALU.mult).then_inc(s_rstep, g)
                    step(n, g, 5)
                    dve.reciprocal(sm_rec[:, 0:g], sm_prod[:, 0:g]).then_inc(s_rstep, g)
                    step(n, g, 6)
                    dve.tensor_tensor(cwr, num, over(sm_rec[:, 0:g], g, E), ALU.mult).then_inc(s_rstep, g)
                    step(n, g, 7)
                    dve.tensor_reduce(cw_sum[:, 0:g], cwr, AX_X, ALU.add).then_inc(s_rstep, g)
                    step(n, g, 8)
                    dve.tensor_scalar(cw_eps[:, 0:g], cw_sum[:, 0:g], 1e-9, None, ALU.add).then_inc(s_rstep, g)
                    step(n, g, 9)
                    dve.reciprocal(cw_rec[:, 0:g], cw_eps[:, 0:g]).then_inc(s_rstep, g)
                    step(n, g, 10)
                    dve.tensor_tensor(cwo, cwr, over(cw_rec[:, 0:g], g, E), ALU.mult).then_inc(s_rstep, g)
                    step(n, g, 11)
                    dve.wait_ge(s_cwTp, n)
                    dve.tensor_copy(parts[:, :, 0], cwo).then_inc(s_cw, g)
                    dve.wait_ge(s_cw, 2 * n + g)
                    dve.tensor_tensor(parts[:, :, 1], cwo, parts[:, :, 0], ALU.subtract).then_inc(s_cw, g)

                def scale_x(m, q, b, first):
                    dve.wait_ge(s_bc, m + 1)
                    if not first:
                        dve.wait_ge(s_xclo, m - 1)
                    dve.tensor_tensor(xc[q], seq(x_T, b), bank(5), ALU.mult).then_inc(s_xc, 1)

                def hidden(c, k, first):
                    dve.wait_ge(s_u, c + 1)
                    dve.wait_ge(s_s, c + 1)
                    if not first:
                        dve.wait_ge(s_hhi, c - 1)
                        dve.wait_ge(s_hlo, c - 1)
                    dve.scalar_tensor_tensor(h32[k % 2], bank(2 + k % 2), W_DOWN, gate_act[k % 2], ALU.mult, ALU.mult).then_inc(s_h, 1)

                def h_low(c, k):
                    dve.wait_ge(s_hhi, c + 1)
                    dve.tensor_tensor(h_lo[k % HSLOTS], h32[k % 2], h_hi[k % HSLOTS], ALU.subtract).then_inc(s_hlo, 1)

                begin(dve, ph["i"])
                if f == 0:
                    dve.wait_ge(s_frhi, 1)
                    dve.scalar_tensor_tensor(fr_w[1][:], fr_raw[:], W_UP, fr_w[0][:], ALU.mult, ALU.subtract).then_inc(s_frlo, 1)
                for s in (0, SUB):
                    if ph["i"] == 0:
                        dve.wait_ge(s_x[s // SUB], 16)
                    prep_bn(n0 + s, s, SUB)
                    prep_aggr(n0 + s, SUB)
                    prep_norm(n0 + s, s, SUB)
                    prep_low(n0 + s, s, SUB)
                    if s == 0:
                        dve.wait_ge(s_con, 16)
                    shift_logits(r0 + s, SUB)
                    combine(r0 + s, SUB)
                if f == 0:
                    for e in range(E):
                        for t, w in enumerate((ffn_g, ffn_u, ffn_d)):
                            dve.wait_ge(s_whi, 3 * e + t + 1)
                            low_weights(w, slice(e * F, (e + 1) * F), 3 * F * (e % 2) + t * F).then_inc(s_wlo, 1)
                if ph["i"] == 0:
                    dve.wait_ge(s_x[2], 16 * (NB - 2))
                scale_x(m0, 0, 0, not f)
                scale_x(m0 + 1, 1, 0, not f)
                hidden(c0, 0, not f)
                hidden(c0 + 1, 1, not f)
                h_low(c0, 0)

                def body(i, prepare, last):
                    c = c0 + i * CH
                    s = i + LEAD
                    for k in range(CH):
                        if prepare and k == 0:
                            prep_bn(n0 + s, s, 1)
                        if not (last and k + 2 >= CH):
                            hidden(c + k + 2, k + 2, False)
                        if prepare and k == 0:
                            prep_aggr(n0 + s, 1)
                        if not (last and k + 1 >= CH):
                            h_low(c + k + 1, k + 1)
                        if not last and k == 1:
                            scale_x(m0 + 2 * i + 2, 0, (i + 1) // PAIRS, False)
                        if not last and k == 5:
                            scale_x(m0 + 2 * i + 3, 1, (i + 1) // PAIRS, False)
                        if prepare and k == 1:
                            prep_norm(n0 + s, s, 1)
                        if prepare and k == 3:
                            prep_low(n0 + s, s, 1)
                        if prepare and k == 4:
                            shift_logits(r0 + s, 1)
                        if prepare and k == 6:
                            combine(r0 + s, 1)
                    dve.wait_ge(s_hfree, HSLOTS + c0 + i * CH + CH)
                    dve.wait_ge(s_facc, a0 + f + i + 1)
                    b = i // PAIRS
                    dve.scalar_tensor_tensor(seq(facc, b), bank(4), 0.5 * W_DOWN, seq(facc, b), ALU.mult, ALU.add).then_inc(s_facc, 1)

                with dve.Fori(0, ITER - LEAD) as i:
                    body(i, True, False)
                with dve.Fori(ITER - LEAD, ITER - 1) as i:
                    body(i, False, False)
                body(ITER - 1, False, True)

            def moe(ph):
                n0, use = ph["n0"], ph["use"]
                t0, b0 = use * NS, use * NB

                def step(b, k):
                    dve.wait_ge(s_estep, b * E_STEPS + k)

                def route(b):
                    dve.wait_ge(s_elg, b + 1)
                    dve.tensor_scalar(e_lg, bank(7, 0, SUB * E), W_DOWN, None, ALU.mult).then_inc(s_elgd, 1)
                    dve.wait_ge(s_elgd, b + 1)
                    dve.tensor_reduce(e_max, by(e_lg, SUB), AX_X, ALU.max).then_inc(s_estep, 1)
                    step(b, 1)
                    dve.tensor_tensor(by(e_shift, SUB), by(e_lg, SUB), over(e_max, SUB, E), ALU.subtract).then_inc(s_esh, 1)

                def select(b):
                    dve.wait_ge(s_eexp, b + 1)
                    dve.tensor_reduce(e_sum, by(e_exp, SUB), AX_X, ALU.add).then_inc(s_estep, 1)
                    step(b, 2)
                    dve.reciprocal(e_rec, e_sum).then_inc(s_estep, 1)
                    step(b, 3)
                    dve.tensor_tensor(by(e_prob, SUB), by(e_exp, SUB), over(e_rec, SUB, E), ALU.mult).then_inc(s_estep, 1)
                    step(b, 4)
                    dve.tensor_reduce(e_top, by(e_prob, SUB), AX_X, ALU.max).then_inc(s_estep, 1)
                    step(b, 5)
                    dve.tensor_tensor(by(e_hit, SUB), by(e_prob, SUB), over(e_top, SUB, E), ALU.is_equal).then_inc(s_estep, 1)
                    dve.tensor_scalar(e_weight, e_top, 0.5 * W_DOWN, None, ALU.mult).then_inc(s_estep, 1)
                    step(b, 7)
                    dve.tensor_tensor(e_rank, e_hit, con_("rev_index"), ALU.mult).then_inc(s_estep, 1)
                    step(b, 8)
                    dve.tensor_reduce(e_first, by(e_rank, SUB), AX_X, ALU.max).then_inc(s_estep, 1)
                    step(b, 9)
                    dve.tensor_tensor(by(e_one, SUB), by(e_rank, SUB), over(e_first, SUB, E), ALU.is_equal).then_inc(s_esel, 1)
                    dve.wait_ge(s_esel, 2 * b + 1)
                    dve.wait_ge(s_eza, b * SUB + 2)
                    dve.wait_ge(s_ezb, b * SUB + 2)
                    dve.tensor_tensor(by(e_sel, SUB), by(e_one, SUB), over(e_weight, SUB, E), ALU.mult).then_inc(s_esel, 1)

                def weigh(t, b, k):
                    q = k % 2
                    dve.wait_ge(s_esel, 2 * b + 2)
                    dve.wait_ge(s_eyb, t + 1)
                    dve.wait_ge(s_ez4, t + 1)
                    sel = over(e_sel[:, k * E + E // 2:(k + 1) * E], E // 2, C)
                    dve.tensor_tensor(by(e_zb[q], E // 2), by(bank(2 * q + 1), E // 2), sel, ALU.mult).then_inc(s_ezb, 1)

                def add(t, s, k):
                    q = k % 2
                    dve.wait_ge(s_ez2, t + 1)
                    dve.wait_ge(s_eadd, t + 1)
                    dve.tensor_tensor(e_z1[q], e_z2[q][:, 0:C], e_z2[q][:, C:2 * C], ALU.add).then_inc(s_ez1, 1)
                    dve.wait_ge(s_ez1, t + 2)
                    dve.tensor_tensor(sub(x_tok, s), sub(x_tok, s), e_z1[q], ALU.add).then_inc(s_eadd, 1)

                begin(dve, ph["i"])
                if ph["i"] == 0:
                    all_loaded()
                dve.wait_ge(s_ewhi, use + 1)
                low_weights(e_w, slice(0, E * C + E), LIN["experts"][0]).then_inc(s_ewlo, 1)
                dve.wait_ge(s_bhi, use + 1)
                dve.scalar_tensor_tensor(bias_w[32:33, :], bias_raw[32:33, :], W_UP, bias_w[32:33, :], ALU.mult,
                                         ALU.subtract).then_inc(s_blo, 1)
                if ph["merge"]:
                    prep_add(ph["g0"], 0)
                    dve.wait_ge(s_mrg, ph["g0"] + 1)
                prep_bn(n0, 0, SUB)
                prep_aggr(n0, SUB)
                prep_norm(n0, 0, SUB)
                prep_low(n0, 0, SUB)
                route(b0)
                select(b0)

                def body(b, last):
                    nx, sx = n0 + SUB * b + SUB, SUB * b + SUB
                    for k in range(SUB):
                        t = t0 + b * SUB + k
                        weigh(t, b0 + b, k)
                        if k == 0 and not last:
                            if ph["merge"]:
                                prep_add(ph["g0"] + b + 1, b + 1)
                                dve.wait_ge(s_mrg, ph["g0"] + b + 2)
                            prep_bn(nx, sx, SUB)
                        if k == 1 and not last:
                            prep_aggr(nx, SUB)
                            prep_norm(nx, sx, SUB)
                        if k >= 1:
                            add(t - 1, b * SUB + k - 1, k - 1)
                        if k == 2 and not last:
                            prep_low(nx, sx, SUB)
                    if not last:
                        route(b0 + b + 1)
                    add(t0 + b * SUB + SUB - 1, b * SUB + SUB - 1, SUB - 1)
                    if not last:
                        select(b0 + b + 1)

                with dve.Fori(0, NB - 1) as b:
                    body(b, False)
                body(NB - 1, True)

            def rwkv(ph):
                n0 = ph["n0"]

                def r_low(b):
                    dve.wait_ge(s_rhi, b + 1)
                    dve.scalar_tensor_tensor(rk[0][1], bank(6), W_DOWN, rk[0][0], ALU.mult, ALU.subtract).then_inc(s_rlo, 1)
                    dve.wait_ge(s_av, SUB * b)
                    dve.tensor_tensor(by(seq(r_decay, b % 2), SUB), by(bank(6), SUB),
                                      w_query.rearrange("p (o i) -> p o i", o=1).to_broadcast([P, SUB, P]), ALU.mult).then_inc(s_rdec, 1)

                def k_low(b):
                    dve.wait_ge(s_khi, b + 1)
                    dve.scalar_tensor_tensor(rk[1][1], bank(6), W_DOWN, rk[1][0], ALU.mult, ALU.subtract).then_inc(s_klo, 1)

                def keys_values(u, n):
                    dve.wait_ge(s_kv, u + 1)
                    dve.wait_ge(s_av, u + 1)
                    if n < SUB - 1:
                        dve.tensor_tensor(by(k_w[n], H), by(bank(7, 0, C), H), over(w_key, H, K), ALU.mult)
                        dve.tensor_scalar(v_tok[n], bank(7, C, 2 * C), W_DOWN, None, ALU.mult)
                    dve.tensor_tensor(by(v_by_head[n], HG), bank(7, C, 2 * C).rearrange("p (o c) -> p o c", o=1).to_broadcast([P, HG, C]),
                                      by(con_("v_head"), HG), ALU.mult).then_inc(s_vbyh, 1)

                def new_state(b, n):
                    dve.wait_ge(s_stp, (SUB - 1) * b + n + 1)
                    dve.wait_ge(s_av, SUB * b + n + 2)
                    if n == 0:
                        dve.tensor_tensor(state[1], bank(7, 2 * C, 3 * C), con_("same_head"), ALU.mult).then_inc(s_state, 1)
                        return
                    dve.tensor_tensor(st_new, bank(7, 2 * C, 3 * C), con_("same_head"), ALU.mult).then_inc(s_stm, 1)
                    dve.wait_ge(s_stm, (SUB - 2) * b + n)
                    dve.wait_ge(s_state, (SUB - 1) * b + n)
                    dve.scalar_tensor_tensor(state[n + 1], state[n], w_chunk, st_new, ALU.mult, ALU.add).then_inc(s_state, 1)

                def weigh(u, n):
                    for g in range(NG):
                        dve.wait_ge(s_attp, 4 * SUB + NG * u + g + 1)
                        dve.wait_ge(s_av, u + 3)
                        dve.tensor_tensor(att[n % 2][g], bank(g % 2), w_intra[:, g * S:(g + 1) * S], ALU.mult).then_inc(s_attw, 1)

                def centre(b):
                    dve.wait_ge(s_gmean, b + 1)
                    dve.tensor_tensor(y_c, y8, bank(2), ALU.subtract).then_inc(s_yc, 1)

                def variance(b):
                    dve.wait_ge(s_gvarp, b + 1)
                    dve.tensor_scalar(g_var, bank(2, 0, SUB * H), GN_EPS, None, ALU.add).then_inc(s_gvar, 1)

                def group_norm(b):
                    dve.wait_ge(s_grb, b + 1)
                    dve.tensor_tensor(y_n, y_c, bank(2), ALU.mult).then_inc(s_yn, 1)

                def add(b):
                    dve.wait_ge(s_rop, b + 1)
                    dve.scalar_tensor_tensor(seq(x_tok, b), bank(2), W_DOWN, seq(x_tok, b), ALU.mult, ALU.add).then_inc(s_rout, 1)

                def prep_start(b):
                    if ph["merge"]:
                        prep_add(ph["g0"] + b, b)
                        dve.wait_ge(s_mrg, ph["g0"] + b + 1)
                    prep_bn(n0 + SUB * b, SUB * b, SUB)

                def prep_middle(b):
                    prep_aggr(n0 + SUB * b, SUB)
                    prep_norm(n0 + SUB * b, SUB * b, SUB)

                begin(dve, ph["i"])
                if ph["i"] == 0:
                    all_loaded()
                dve.wait_ge(s_con, 64)
                dve.wait_ge(s_lin, 48)
                dve.wait_ge(s_rexp, 2)
                dve.tensor_scalar(decay_neg, w_kexp, EXP_CAP, -1.0, ALU.min, ALU.mult).then_inc(s_rset, 1)
                dve.tensor_scalar(decay_row, w_qexp[:, 0:1], EXP_CAP, -1.0, ALU.min, ALU.mult).then_inc(s_rset, 1)
                dve.tensor_scalar(mix_scale[:, 0:4], col_("mix"), W_UP, None, ALU.mult)
                dve.tensor_scalar(mix_scale[:, 4:8], col_("mix"), -W_UP, W_UP, ALU.mult, ALU.add).then_inc(s_rset, 1)
                dve.wait_ge(s_rset, 3)
                for m in range(2):
                    for j in range(4):
                        c = slice(j * C, (j + 1) * C)
                        ins = dve.tensor_scalar(mixed[m][:, c], raw_("mixed")[:, c], mix_scale[:, 4 * m + j:4 * m + j + 1], None, ALU.mult)
                    ins.then_inc(s_rset, 1)
                for m in range(2):
                    dve.wait_ge(s_rset, 4 + m)
                    dve.wait_ge(s_rwhi, 1 + m)
                    dve.tensor_tensor(mix_w[m][1], mixed[m], mix_w[m][0], ALU.subtract).then_inc(s_rwlo, 1)
                dve.wait_ge(s_rwhi, 3)
                low_weights(r_wo, slice(0, C), LIN["wo_r"][0]).then_inc(s_rwlo, 1)
                dve.wait_ge(s_rexp, 6)
                dve.tensor_scalar(w_key, w_kexp, W_DOWN, None, ALU.mult).then_inc(s_rset, 1)
                dve.tensor_scalar(w_query, w_qexp, W_DOWN, None, ALU.mult).then_inc(s_rset, 1)
                dve.tensor_tensor(by(w_later, H), by(w_exp, H), con_("later").rearrange("p (o i) -> p o i", o=1).to_broadcast([P, H, P]),
                                  ALU.mult).then_inc(s_rset, 1)
                dve.wait_ge(s_rset, 8)
                for h in range(H):
                    c = slice(h * P, (h + 1) * P)
                    a = COL["bonus"][0] + h
                    ins = dve.scalar_tensor_tensor(w_intra[:, c], ident, col_sb[:, a:a + 1], w_later[:, c], ALU.mult, ALU.add)
                ins.then_inc(s_rset, 1)
                dve.wait_ge(s_rset, 9)
                for b in range(2):
                    prep_start(b)
                    prep_middle(b)
                    prep_low(n0 + SUB * b, SUB * b, SUB)
                r_low(0)
                k_low(0)
                for n in range(2):
                    keys_values(n, n)
                    new_state(0, n)
                weigh(0, 0)

                def body(b, first, prep, more):
                    for n in range(SUB):
                        u = SUB * b + n
                        if more or n < SUB - 2:
                            keys_values(u + 2, (n + 2) % SUB)
                        if n == 0 and not first:
                            centre(b - 1)
                        if n == 1 and prep:
                            prep_middle(b + 2)
                        if n == 1 and more:
                            r_low(b + 1)
                        if n == 3 and prep:
                            prep_low(n0 + SUB * b + 2 * SUB, SUB * b + 2 * SUB, SUB)
                        if more or n < SUB - 1:
                            weigh(u + 1, (n + 1) % SUB)
                        if n == 1 and more:
                            k_low(b + 1)
                        if (more or n < SUB - 2) and (n + 2) % SUB < SUB - 1:
                            new_state(b + (n + 2) // SUB, (n + 2) % SUB)
                        if n == 0 and not first:
                            variance(b - 1)
                        if n == 2 and not first:
                            group_norm(b - 1)
                        if n == 3 and not first:
                            add(b - 1)
                        if n == 0 and prep:
                            prep_start(b + 2)

                body(0, True, True, True)
                with dve.Fori(1, NB - 2) as b:
                    body(b, False, True, True)
                body(NB - 2, False, False, True)
                body(NB - 1, False, False, False)
                for step in (centre, variance, group_norm, add):
                    step(NB - 1)

            def attention(ph):
                n0 = ph["n0"]

                def q_low(b):
                    dve.wait_ge(s_mqhi, b + 1)
                    dve.scalar_tensor_tensor(qk[0][1], bank(4), W_DOWN, qk[0][0], ALU.mult, ALU.subtract).then_inc(s_mqlo, 1)

                def k_low(b):
                    dve.wait_ge(s_mkhi, b + 1)
                    dve.scalar_tensor_tensor(qk[1][1], bank(4), W_DOWN, qk[1][0], ALU.mult, ALU.subtract).then_inc(s_mklo, 1)

                def v_copy(b):
                    dve.wait_ge(s_mvp, b + 1)
                    dve.wait_ge(s_pvq, units_done(NG * b))
                    dve.tensor_scalar(by(v_aug, SUB * H)[:, :, 0:K], by(bank(4), SUB * H), W_DOWN, None, ALU.mult).then_inc(s_mv_in, 1)

                def key_stack(u, g):
                    dve.wait_ge(s_mks, u + 1)
                    dve.wait_ge(s_pvq, units_done(u - 3))
                    dve.tensor_copy(k_stack[g][0:STK], bank(5)[0:STK]).then_inc(s_mkst, 1)

                def max_rows(u, g):
                    dve.wait_ge(s_maug, u + 1)
                    dve.wait_ge(s_pvq, units_done(u - 3))
                    dst = by(q_by_head[g][STK:AUG], HG)
                    for r in range(HG):
                        ins = dve.tensor_scalar(dst[:, r], m_aug[STK:AUG], con_("row_head")[STK:AUG, r:r + 1], None, ALU.mult)
                    ins.then_inc(s_mqaug, 1)

                def maxima(u, g):
                    dve.wait_ge(s_mpad, u)
                    for t, (q, r, n) in enumerate(Q_TILES):
                        w = (q + 1) * P
                        dve.wait_ge(s_p1, QT * u + t + 1)
                        dve.tensor_reduce(neg_max[:, q * HG + r:q * HG + r + n], by(bank(2 + (g + t) % 2, 0, n * w), n), AX_X, ALU.max,
                                          negate=True).then_inc(s_p1used, 1)
                    dve.wait_ge(s_p1used, QT * u + QT + 2)
                    dve.wait_ge(s_mTp, u)
                    dve.tensor_scalar(by(max_pad, SUB)[:, :, STK:AUG], by(neg_max, SUB), M_DOWN, None, ALU.mult).then_inc(s_mpad, 1)

                def normalise(u, b, g):
                    dve.wait_ge(s_ytp, u + 1)
                    cols = bank(7).rearrange("p (q r c) -> p q r c", q=SUB, r=HG)
                    dve.reciprocal(by(den_rec, SUB * HG), by(bank(7), SUB * HG)[:, :, K:K + 1]).then_inc(s_drec, 1)
                    dve.wait_ge(s_yTp, b)
                    dve.wait_ge(s_drec, u + 1)
                    dve.tensor_tensor(y_tok.rearrange("p (q g r v) -> p q g r v", q=SUB, g=NG, r=HG)[:, :, g], cols[:, :, :, 0:K],
                                      den_rec.rearrange("p (q r o) -> p q r o", q=SUB, o=1).to_broadcast([P, SUB, HG, K]),
                                      ALU.mult).then_inc(s_ytok, 1)

                def out_low(b):
                    dve.wait_ge(s_yohi, b + 1)
                    dve.tensor_tensor(yo[1], bank(4), yo[0], ALU.subtract).then_inc(s_yolo, 1)

                def add(b):
                    dve.wait_ge(s_mop, b + 2)
                    dve.scalar_tensor_tensor(seq(x_tok, b), bank(4), W_DOWN, seq(x_tok, b), ALU.mult, ALU.add).then_inc(s_mout, 1)

                begin(dve, ph["i"])
                if ph["i"] == 0:
                    all_loaded()
                dve.wait_ge(s_con, 64)
                dve.wait_ge(s_lin, 48)
                dve.wait_ge(s_mwhi, 1)
                for g in range(NG):
                    dve.memset(k_stack[g][STK:AUG], M_UP)
                dve.memset(max_pad, 0.0).then_inc(s_mpad0, 1)
                dve.wait_ge(s_mpad0, 1)
                low_weights(m_w, slice(0, 4 * C), LIN["q"][0]).then_inc(s_mwlo, 1)
                for b in range(2):
                    prep_bn(n0 + SUB * b, SUB * b, SUB)
                    prep_aggr(n0 + SUB * b, SUB)
                    prep_norm(n0 + SUB * b, SUB * b, SUB)
                    prep_low(n0 + SUB * b, SUB * b, SUB, 4)
                q_low(0)
                k_low(0)
                dve.wait_ge(s_mset, 2)
                v_copy(0)
                for u in range(3):
                    key_stack(u, u)
                maxima(0, 0)
                max_rows(0, 0)
                maxima(1, 1)

                def body(b, first, prep, more):
                    for g in range(NG):
                        u = NG * b + g
                        if more or g < NG - 1:
                            max_rows(u + 1, (g + 1) % NG)
                        if g == 0 and not first:
                            out_low(b - 1)
                        if g == 1 and more:
                            k_low(b + 1)
                        if g == 1 and prep:
                            prep_aggr(n0 + SUB * b + 2 * SUB, SUB)
                        if g == 2 and prep:
                            prep_norm(n0 + SUB * b + 2 * SUB, SUB * b + 2 * SUB, SUB)
                        if g == 3 and prep:
                            prep_low(n0 + SUB * b + 2 * SUB, SUB * b + 2 * SUB, SUB, 4)
                        if g == 0 and not first:
                            add(b - 1)
                        if more or g < NG - 3:
                            key_stack(u + 3, (g + 3) % NG)
                        normalise(u, b, g)
                        if g == 0 and more:
                            q_low(b + 1)
                        if g == 3 and more:
                            v_copy(b + 1)
                        if more or g < NG - 2:
                            maxima(u + 2, (g + 2) % NG)
                        if g == 0 and prep:
                            prep_bn(n0 + SUB * b + 2 * SUB, SUB * b + 2 * SUB, SUB)

                body(0, True, True, True)
                with dve.Fori(1, NB - 2) as b:
                    body(b, False, True, True)
                body(NB - 2, False, False, True)
                body(NB - 1, False, False, False)
                out_low(NB - 1)
                add(NB - 1)

            for ph in plan:
                dict(F=ffn, E=moe, R=rwkv, M=attention)[ph["kind"]](ph)

        @block.tensor
        def _(pe):
            def prep_merge(m, n):
                pe.wait_ge(s_mrg_in, m + 1)
                pe.wait_ge(s_xlo, n)
                for q in range(SUB):
                    ins = pe.transpose(bank(6, q * P, (q + 1) * P), merge_in[:, q * P:(q + 1) * P], ident)
                ins.then_inc(s_mrg_ps, 1)

            def prep_transpose(n, g, at=6):
                pe.wait_ge(s_xn, n + g)
                pe.wait_ge(s_xlo, n)
                for q in range(g):
                    ins = pe.transpose(bank(at, q * P, (q + 1) * P), x_norm[:, q * P:(q + 1) * P], ident)
                ins.then_inc(s_xT, g)

            def three(dst, lhs, rhs, first=True, last=True):
                pe.matmul(dst, lhs[0], rhs[0], start=first, stop=False)
                pe.matmul(dst, lhs[0], rhs[1], start=False, stop=False)
                return pe.matmul(dst, lhs[1], rhs[0], start=False, stop=last)

            def ffn(ph):
                f, n0 = ph["use"], ph["n0"]
                r0, m0, c0, a0 = f * NS, f * NB * E, f * ITER * CH, f * ITER

                def logits(n, s, nx, g):
                    pe.wait_ge(s_xlo, nx + g)
                    pe.wait_ge(s_cwT, n)
                    for q in range(g):
                        ins = three(bank(7, q * 2 * E, (q + 1) * 2 * E), [xsub(t, s + q) for t in (x_hi, x_lo)], [w[:] for w in fr_w])
                    ins.then_inc(s_lg, g)

                def transpose_cw(n, g):
                    pe.wait_ge(s_cw, 2 * (n + g))
                    for q in range(g):
                        ins = pe.transpose(bank(7, 64 + q * P // 2, 64 + (q + 1) * P // 2)[0:2 * E].bitcast(F16),
                                           cw16[:, q * 2 * E:(q + 1) * 2 * E], ident16)
                    ins.then_inc(s_cwTp, g)

                def broadcast(m, e, b):
                    pe.wait_ge(s_xc, m)
                    pe.matmul(bank(5), sub(half_("pick_expert"), e), seq(cw_T, b), start=True, stop=True).then_inc(s_bc, 1)

                def cols(w, e, k):
                    return [t[:, ds(e * F + (k % FC) * P, P)] for t in w]

                def gate_up(c, k, m, e, b, first):
                    if not first:
                        pe.wait_ge(s_s, c - 1)
                    three(bank(k % 2), cols(ffn_g, e, k), [xseq(t, b) for t in (x_hi, x_lo)]).then_inc(s_g, 1)
                    if not first:
                        pe.wait_ge(s_h, c - 1)
                    q = (k // FC) % 2
                    if k % FC == 0:
                        pe.wait_ge(s_xclo, m + 1)
                    three(bank(2 + k % 2), cols(ffn_u, e, k), [xc_hi[q], xc_lo[q]]).then_inc(s_u, 1)

                def down(c, k, e, added):
                    pe.wait_ge(s_hlo, c + 1)
                    if k == 0:
                        pe.wait_ge(s_facc, added)
                    r = k % HSLOTS
                    three(bank(4), cols(ffn_d, e, k), [h_hi[r], h_lo[r]], k == 0, k == CH - 1).then_inc(s_hfree, 1)

                begin(pe, ph["i"])
                if f == 0:
                    pe.wait_ge(s_con, 32)
                    pe.wait_ge(s_frlo, 1)
                for s in (0, SUB):
                    prep_transpose(n0 + s, SUB)
                    logits(r0 + s, s, n0 + s, SUB)
                    transpose_cw(r0 + s, SUB)
                pe.wait_ge(s_cwT, r0 + SUB)
                broadcast(m0, 0, 0)
                broadcast(m0 + 1, 1, 0)
                pe.wait_ge(s_wlo, 3 * E)
                gate_up(c0, 0, m0, 0, 0, not f)
                gate_up(c0 + 1, 1, m0, 0, 0, not f)

                def body(i, prepare, last):
                    c = c0 + i * CH
                    s = i + LEAD
                    pair, b = i % PAIRS, i // PAIRS
                    npair, nb = (i + 1) % PAIRS, (i + 1) // PAIRS
                    for k in range(CH):
                        kk = k + 2
                        if kk < CH:
                            gate_up(c + kk, kk, m0 + 2 * i + kk // FC, 2 * pair + kk // FC, b, False)
                        elif not last:
                            if kk == CH:
                                pe.wait_ge(s_xlo, n0 + nb * SUB + SUB)
                            gate_up(c + kk, kk, m0 + 2 * i + kk // FC, 2 * npair, nb, False)
                        if not last and k == 1:
                            pe.wait_ge(s_cwT, r0 + nb * SUB + SUB)
                            broadcast(m0 + 2 * i + 2, 2 * npair, nb)
                        if not last and k == 5:
                            broadcast(m0 + 2 * i + 3, 2 * npair + 1, nb)
                        down(c + k, k, 2 * pair + k // FC, a0 + f + i + 1)
                        if prepare and k == 2:
                            prep_transpose(n0 + s, 1)
                        if prepare and k == 4:
                            logits(r0 + s, s, n0 + s, 1)
                        if prepare and k == 7:
                            transpose_cw(r0 + s, 1)

                with pe.Fori(0, ITER - LEAD) as i:
                    body(i, True, False)
                with pe.Fori(ITER - LEAD, ITER - 1) as i:
                    body(i, False, False)
                body(ITER - 1, False, True)

            def moe(ph):
                n0, use = ph["n0"], ph["use"]
                t0, b0 = use * NS, use * NB
                ones = half_("ones")

                def parts(s):
                    return [xsub(t, s) for t in (x_hi, x_lo)]

                def ecols(a, b):
                    return [w[:, a:b] for w in e_w]

                def logits(b, s, n):
                    pe.wait_ge(s_xlo, n + SUB)
                    pe.wait_ge(s_elgd, b)
                    for q in range(SUB):
                        dst = bank(7, q * E, (q + 1) * E)
                        pe.matmul(dst, ones, bias_w[:, E * C:E * C + E], start=True, stop=False)
                        ins = three(dst, parts(s + q), ecols(E * C, E * C + E), False)
                    ins.then_inc(s_elg, 1)

                def products(t, s, k):
                    for half_of, done, used in ((0, s_eya, s_eza), (1, s_eyb, s_ezb)):
                        pe.wait_ge(used, t + 1)
                        a = half_of * E // 2 * C
                        dst = bank(2 * (k % 2) + half_of)
                        pe.matmul(dst, ones, bias_w[:, a:a + BANK], start=True, stop=False)
                        three(dst, parts(s), ecols(a, a + BANK), False).then_inc(done, 1)

                begin(pe, ph["i"])
                pe.wait_ge(s_con, 64)
                if ph["merge"]:
                    prep_merge(ph["g0"], n0)
                prep_transpose(n0, SUB)
                pe.wait_ge(s_ewlo, use + 1)
                pe.wait_ge(s_blo, use + 1)
                logits(b0, 0, n0)

                def body(b, last):
                    nx, sx = n0 + SUB * b + SUB, SUB * b + SUB
                    if not last and ph["merge"]:
                        prep_merge(ph["g0"] + b + 1, nx)
                    for k in range(SUB):
                        products(t0 + b * SUB + k, b * SUB + k, k)
                        if k == 1 and not last:
                            prep_transpose(nx, SUB)
                        if k == 3 and not last:
                            logits(b0 + b + 1, sx, nx)

                with pe.Fori(0, NB - 1) as b:
                    body(b, False)
                body(NB - 1, True)

            pe.sem_inc(s_hfree, HSLOTS)
            for s in (s_eza, s_ezb, s_ez4):
                pe.sem_inc(s, 2)
            for s in (s_ez1, s_eadd, s_rout, s_mop):
                pe.sem_inc(s, 1)
            def rwkv(ph):
                n0 = ph["n0"]

                def project(dst, j, rhs):
                    w = [[t[:, j * C:(j + 1) * C] for t in mix_w[m]] for m in range(2)]
                    three(dst, w[0], rhs[0], True, False)
                    return three(dst, w[1], rhs[1], False, True)

                def both(b):
                    return [[xseq(t, b, m) for t in (x_hi, x_lo)] for m in range(2)]

                def r_proj(b):
                    pe.wait_ge(s_xlo, n0 + SUB * b + SUB)
                    pe.wait_ge(s_klo, b)
                    project(bank(6), 0, both(b)).then_inc(s_rp, 1)

                def k_proj(b):
                    pe.wait_ge(s_rdec, b + 1)
                    project(bank(6), 1, both(b)).then_inc(s_kp, 1)

                def stacks(u, b, n):
                    for j, dst, names, ready, used, done in ((0, bank(5), ("q_hi", "q_lo"), s_rlo, s_rbyh, s_rst),
                                                             (1, bank(3), ("k_hi", "k_lo"), s_klo, s_kstk, s_kst)):
                        pe.wait_ge(ready, b + 1)
                        pe.wait_ge(used, u)
                        for g in range(NG):
                            for h in range(2):
                                ins = pe.matmul(dst[0:STK, g * P:(g + 1) * P], pick(names[h], g), rk[j][h][:, n * P:(n + 1) * P],
                                                start=h == 0, stop=h == 1)
                        ins.then_inc(done, 1)
                    pe.wait_ge(s_vbyh, u)
                    pe.wait_ge(s_state, (SUB - 1) * b + n)
                    w = [[t[:, C:3 * C] for t in mix_w[m]] for m in range(2)]
                    chunk = [[xchunk(t, b, n, m) for t in (x_hi, x_lo)] for m in range(2)]
                    three(bank(7, 0, 2 * C), chunk[0], w[0], True, False)
                    three(bank(7, 0, 2 * C), chunk[1], w[1], False, True).then_inc(s_kv, 1)

                def state_product(u, b, n):
                    pe.wait_ge(s_vbyh, u + 1)
                    pe.wait_ge(s_state, (SUB - 1) * b + n)
                    pe.matmul(bank(7, 2 * C, 3 * C), k_w[n], v_tok[n], start=True, stop=True).then_inc(s_stp, 1)

                def scores(u, n):
                    pe.wait_ge(s_rbyh, u + 1)
                    pe.wait_ge(s_kstk, u + 1)
                    for g in range(NG):
                        pe.wait_ge(s_attw, NG * u + g + 1)
                        pe.matmul(bank(g % 2), k_stk[n][0:STK, g * P:(g + 1) * P], r_st[n][0:STK, g * S:(g + 1) * S],
                                  start=True, stop=True).then_inc(s_attp, 1)

                def outputs(u, b, n):
                    if n == 0:
                        pe.wait_ge(s_y8, b)
                    else:
                        pe.wait_ge(s_state, (SUB - 1) * b + n)
                        pe.wait_ge(s_rdec, b + 1)
                        pe.matmul(bank(4, n * P, (n + 1) * P), state[n], r_decay[:, ds((b % 2) * S + n * P, P)], start=True, stop=False)
                    pe.wait_ge(s_attw, 2 + NG * u + NG)
                    pe.wait_ge(s_vbyh, u + 1)
                    for r in range(HG):
                        for g in range(NG):
                            c = slice(r * C + g * GC, r * C + (g + 1) * GC)
                            ins = pe.matmul(bank(4, n * P, (n + 1) * P)[g * GC:(g + 1) * GC], v_by_head[n][:, c],
                                            att[n % 2][g][:, r * P:(r + 1) * P], start=n == 0 and r == 0, stop=r == HG - 1)
                    ins.then_inc(s_av, 1)

                def gn_mean(b):
                    pe.wait_ge(s_y8, b + 1)
                    pe.wait_ge(s_rout, b + 1)
                    pe.matmul(bank(2), con_("head_mean"), y8, start=True, stop=True).then_inc(s_gmean, 1)

                def gn_var(b):
                    pe.wait_ge(s_ysq, b + 1)
                    for n in range(SUB):
                        ins = pe.matmul(bank(2, n * H, (n + 1) * H), y_sq[:, n * P:(n + 1) * P], con_("head_mean16"), start=True, stop=True)
                    ins.then_inc(s_gvarp, 1)

                def g_proj(b):
                    pe.wait_ge(s_gvar, b + 1)
                    project(bank(2), 3, both(b)).then_inc(s_gp, 1)

                def gn_rstd(b):
                    pe.wait_ge(s_sg, b + 1)
                    pe.wait_ge(s_gwide, b + 1)
                    for n in range(SUB):
                        ins = pe.matmul(bank(2, n * P, (n + 1) * P), g_wide[:, n * P:(n + 1) * P], ident, start=True, stop=True)
                    ins.then_inc(s_grb, 1)

                def out_proj(b):
                    pe.wait_ge(s_yglo, b + 1)
                    for n in range(SUB):
                        ins = three(bank(2, n * P, (n + 1) * P), [t[:, n * P:(n + 1) * P] for t in y_parts], r_wo)
                    ins.then_inc(s_rop, 1)

                begin(pe, ph["i"])
                pe.sem_inc(s_attw, 2)
                pe.sem_inc(s_av, SUB)
                pe.sem_inc(s_attp, NG * SUB)
                pe.wait_ge(s_con, 64)
                for b in range(2):
                    if ph["merge"]:
                        prep_merge(ph["g0"] + b, n0 + SUB * b)
                    prep_transpose(n0 + SUB * b, SUB)
                pe.wait_ge(s_xlo, n0 + 2 * SUB)
                pe.wait_ge(s_rwlo, 3)
                r_proj(0)
                k_proj(0)
                for n in range(2):
                    stacks(n, 0, n)
                    state_product(n, 0, n)
                scores(0, 0)

                def body(b, first, prep, more):
                    for n in range(SUB):
                        u = SUB * b + n
                        b2, n2 = b + (n + 2) // SUB, (n + 2) % SUB
                        ahead = more or n < SUB - 2
                        if n == 0 and prep and ph["merge"]:
                            pe.wait_ge(s_klo, b + 1)
                            prep_merge(ph["g0"] + b + 2, n0 + SUB * b + 2 * SUB)
                        if ahead:
                            stacks(u + 2, b2, n2)
                        if n == 0 and not first:
                            gn_mean(b - 1)
                        if n == 1 and more:
                            if prep and ph["merge"]:
                                pe.wait_ge(s_mrg, ph["g0"] + b + 3)
                            r_proj(b + 1)
                        if n == 2 and prep:
                            pe.wait_ge(s_klo, b + 2)
                            prep_transpose(n0 + SUB * b + 2 * SUB, SUB)
                        if more or n < SUB - 1:
                            scores(u + 1, (n + 1) % SUB)
                        if n == 0 and not first:
                            gn_var(b - 1)
                        if n == 1 and not first:
                            g_proj(b - 1)
                        if n == 1 and more:
                            k_proj(b + 1)
                        outputs(u, b, n)
                        if ahead and n2 < SUB - 1:
                            state_product(u + 2, b2, n2)
                        if n == 2 and not first:
                            gn_rstd(b - 1)
                        if n == 3 and not first:
                            out_proj(b - 1)

                body(0, True, True, True)
                with pe.Fori(1, NB - 2) as b:
                    body(b, False, True, True)
                body(NB - 2, False, False, True)
                body(NB - 1, False, False, False)
                for step in (gn_mean, gn_var, g_proj, gn_rstd, out_proj):
                    step(NB - 1)

            def attention(ph):
                n0 = ph["n0"]
                wq, wk, wv, wo = [[w[:, j * C:(j + 1) * C] for w in m_w] for j in range(4)]
                ident_b, keys_after, queries_before = [big_sb[:, a:a + P] for a, _ in BIG.values()]

                def parts(b):
                    return [xseq(t, b) for t in (x_hi, x_lo)]

                def q_proj(b):
                    three(bank(4), wq, parts(b)).then_inc(s_mqp, 1)

                def k_proj(b):
                    pe.wait_ge(s_mqlo, b + 1)
                    three(bank(4), wk, parts(b)).then_inc(s_mkp, 1)

                def v_proj(b):
                    for n in range(SUB):
                        ins = three(bank(4, n * P, (n + 1) * P), [xchunk(t, b, n, 0) for t in (x_hi, x_lo)], wv)
                    ins.then_inc(s_mvp, 1)

                def stacks(u, b, g):
                    pe.wait_ge(s_mklo, b + 1)
                    pe.wait_ge(s_mkst, u)
                    for h, name in enumerate(("k_hi", "k_lo")):
                        ins = pe.matmul(bank(5)[0:STK], pick(name, g), qk[1][h], start=h == 0, stop=h == 1)
                    ins.then_inc(s_mks, 1)
                    pe.wait_ge(s_mqst, u)
                    if not isinstance(u, int) or u >= 3:
                        pe.wait_ge(s_maug, u - 1)
                    for h, name in enumerate(("q_hi", "q_lo")):
                        ins = pe.matmul(bank(6)[0:STK], pick(name, g), qk[0][h], start=h == 0, stop=h == 1)
                    ins.then_inc(s_mqs, 1)

                def by_query(u, g):
                    pe.wait_ge(s_mqh, u + 3)
                    pe.wait_ge(s_mkst, u + 1)
                    for t, (q, r0, n) in enumerate(Q_TILES):
                        w = (q + 1) * P
                        pe.wait_ge(s_p1used, QT * u + t + 1)
                        for r in range(r0, r0 + n):
                            dst = bank(2 + (g + t) % 2, (r - r0) * w, (r - r0 + 1) * w)
                            pe.matmul(dst, q_by_head[g][0:STK, r * S + q * P:r * S + (q + 1) * P], k_stack[g][0:STK, 0:w], start=True, stop=False)
                            ins = pe.matmul(dst[:, w - P:w], ident_b, keys_after, start=False, stop=True)
                        ins.then_inc(s_p1, 1)

                def max_rows(u, stacked):
                    pe.wait_ge(s_mpad, u + 1)
                    pe.wait_ge(s_mqst, stacked)
                    for q in range(SUB):
                        ins = pe.matmul(bank(6, q * P, (q + 1) * P), max_pad[:, q * P:(q + 1) * P], ident16, start=True, stop=True)
                    ins.then_inc(s_mTp, 1)

                def by_key(u, g, j):
                    w = S - j * P
                    for t, (jt, r0, n) in enumerate(K_TILES):
                        if jt != j:
                            continue
                        pe.wait_ge(s_p2exp, KT * u + t + 1)
                        for r in range(r0, r0 + n):
                            dst = bank((g + t) % 2, (r - r0) * w, (r - r0 + 1) * w)
                            pe.matmul(dst, k_stack[g][0:AUG, j * P:(j + 1) * P], q_by_head[g][0:AUG, r * S + j * P:(r + 1) * S],
                                      start=True, stop=False)
                            ins = pe.matmul(dst[:, 0:P], ident_b, queries_before, start=False, stop=True)
                        ins.then_inc(s_p2, 1)

                def weighted_values(u, g, j):
                    w = S - j * P
                    pe.wait_ge(s_p2exp, KT * u + KT_END[j] + 2)
                    for r in range(HG):
                        a = (j * H + g * HG + r) * 32
                        ins = pe.matmul(bank(7, j * P, S)[r * 32:(r + 1) * 32], v_aug[:, a:a + 32], probs[j % 2][:, r * w:(r + 1) * w],
                                        start=j == 0, stop=j == SUB - 1)
                    ins.then_inc(s_pvq, 1)

                def unit(u, b, g):
                    pe.wait_ge(s_mqaug, u + 1)
                    by_key(u, g, 0)
                    by_key(u, g, 1)
                    pe.wait_ge(s_ytok, u)
                    pe.wait_ge(s_mv_in, b + 1)
                    weighted_values(u, g, 0)
                    by_key(u, g, 2)
                    weighted_values(u, g, 1)
                    by_key(u, g, 3)
                    weighted_values(u, g, 2)
                    weighted_values(u, g, 3)

                def transpose_values(u):
                    pe.wait_ge(s_yraw, u + 1)
                    for q in range(SUB):
                        ins = pe.transpose(bank(7, q * P, (q + 1) * P), y_raw[:, q * P:(q + 1) * P], ident)
                    ins.then_inc(s_ytp, 1)

                def transpose_out(b):
                    pe.wait_ge(s_ytok, NG * b + NG)
                    for n in range(SUB):
                        ins = pe.transpose(bank(4, n * P, (n + 1) * P), y_tok[:, n * P:(n + 1) * P], ident)
                    ins.then_inc(s_yTp, 1)

                def out_proj(b):
                    pe.wait_ge(s_yolo, b + 1)
                    for n in range(SUB):
                        ins = three(bank(4, n * P, (n + 1) * P), [t[:, n * P:(n + 1) * P] for t in yo], wo)
                    ins.then_inc(s_mop, 1)

                begin(pe, ph["i"])
                for s, n in ((s_p1used, 2), (s_p2exp, 2), (s_pvq, PV_CREDIT), (s_mqh, 2)):
                    pe.sem_inc(s, n)
                pe.wait_ge(s_con, 64)
                for b in range(2):
                    prep_transpose(n0 + SUB * b, SUB, 4)
                pe.wait_ge(s_mwlo, 1)
                pe.wait_ge(s_xlo, n0 + 2 * SUB)
                q_proj(0)
                k_proj(0)
                pe.wait_ge(s_mklo, 1)
                v_proj(0)
                for u in range(3):
                    stacks(u, 0, u)
                by_query(0, 0)
                max_rows(0, 3)
                by_query(1, 1)

                def body(b, first, prep, more):
                    for g in range(NG):
                        u = NG * b + g
                        if more or g < NG - 1:
                            max_rows(u + 1, u + 3 if more else min(u + 3, UNITS))
                        if g == 0 and not first:
                            pe.wait_ge(s_mv_in, b + 1)
                            transpose_out(b - 1)
                        if g == 1 and more:
                            k_proj(b + 1)
                        unit(u, b, g)
                        if g == 0 and not first:
                            out_proj(b - 1)
                        if g == 2 and prep:
                            pe.wait_ge(s_mklo, b + 2)
                            prep_transpose(n0 + SUB * b + 2 * SUB, SUB, 4)
                        if more or g < NG - 3:
                            stacks(u + 3, b + (g + 3) // NG, (g + 3) % NG)
                        transpose_values(u)
                        if g == 0 and more:
                            pe.wait_ge(s_mout, b)
                            pe.wait_ge(s_mv_in, b + 1)
                            q_proj(b + 1)
                        if g == 3 and more:
                            if prep:
                                pe.wait_ge(s_xlo, n0 + SUB * b + 3 * SUB)
                            v_proj(b + 1)
                        if more or g < NG - 2:
                            by_query(u + 2, (g + 2) % NG)

                body(0, True, True, True)
                with pe.Fori(1, NB - 2) as b:
                    body(b, False, True, True)
                body(NB - 2, False, False, True)
                body(NB - 1, False, False, False)
                transpose_out(NB - 1)
                out_proj(NB - 1)

            for ph in plan:
                dict(F=ffn, E=moe, R=rwkv, M=attention)[ph["kind"]](ph)


def shape_constants():
    c = np.arange(P)
    con = {n: np.zeros((P, w), np.float32) for n, (_, w) in CON.items()}
    con["ident"][:] = np.eye(P)
    same = (c[:, None] // K == c[None, :] // K)
    con["head_mean"][:] = same / K
    con["head_mean16"][c, c // K] = 1.0 / K
    con["same_head"][:] = same
    con["rev_index"][:] = np.tile(E - np.arange(E), SUB)
    con["logit_scale"][:] = np.tile(np.repeat([W_DOWN, W_DOWN / GATE_TEMP], E), SUB)
    rows = np.arange(AUG)
    head = np.where(rows < STK, rows % GC // K, rows - STK)
    con["row_head"][rows, head] = 1.0
    con["v_head"][:] = (W_DOWN * (c[None, :] % GC // K == np.arange(HG)[:, None])).reshape(1, HG * C)
    con["distance"][:] = np.maximum(c[None, :] - c[:, None] - 1, 0)
    con["later"][:] = c[None, :] > c[:, None]
    con["position"][:] = c[None, :]
    con["to_end"][:, 0] = P - 1 - c
    half = {n: np.zeros((P, w), np.float16) for n, (_, w) in HALF.items()}
    half["ident"][:] = np.eye(P)
    for e in range(E):
        half["pick_expert"][[e, E + e], e * P:(e + 1) * P] = 1.0
    half["ones"][:] = 1.0
    for name, parts in (("k_hi", (0, 2)), ("k_lo", (1,)), ("q_hi", (0, 1)), ("q_lo", (2,))):
        for g in range(NG):
            for part in parts:
                half[name][g * GC + np.arange(GC), g * STK + part * GC + np.arange(GC)] = 1.0
    after = np.where(c[None, :] > c[:, None], NEG_BIG, 0.0)
    big = np.concatenate([np.eye(P), after, after.T], axis=1)
    return (np.concatenate([con[n] for n in CON], axis=1), np.concatenate([half[n] for n in HALF], axis=1), big.astype(mybir.dt.np(BF16)))


def lay_out(v):
    def rows(a):
        return np.broadcast_to(a.reshape(1, -1), (P, a.size))

    con, half, big = shape_constants()
    x = v["L0_attn_xq"].reshape(NS, P, C).transpose(1, 0, 2).reshape(P, NS * C)
    down = v["L0_ffn_w_down"].reshape(E, FC, P, C).transpose(0, 2, 1, 3).reshape(E, P, F)
    qkv = v["L1_attn_w_qkv"].reshape(3, C, C)
    lin = dict(mixed=np.concatenate([v["L0_attn_W_" + n].T for n in "rkvg"], axis=1), wo_r=v["L0_attn_W_o"].T,
               experts=v["L1_ffn_expert_w"].transpose(2, 0, 1).reshape(C, E * C), router=v["L1_ffn_router_w"].T,
               q=qkv[0].T, k=qkv[1].T, v=qkv[2].T, wo_m=v["L1_attn_w_o"].T)
    col = dict(mix=np.stack([v["L0_attn_time_mix_" + n].reshape(C) for n in "rkvg"], axis=1),
               decay_row=np.repeat(v["L0_attn_time_decay"], K)[:, None], ln_w=v["L0_attn_ln_w"][:, None], ln_b=v["L0_attn_ln_b"][:, None],
               decay=rows(v["L0_attn_time_decay"]), bonus=rows(v["L0_attn_time_faaaa"]))
    bias = np.concatenate([v["L1_ffn_expert_b"].reshape(E * C), v["L1_ffn_router_b"]])
    return dict(x=x, ffn_router=np.concatenate([v["L0_ffn_w_router"], v["L0_ffn_w_gating"]], axis=1),
                ffn_w=np.concatenate([v["L0_ffn_w_gate"], v["L0_ffn_w_up"], down], axis=2),
                lin=np.concatenate([lin[n] for n in LIN], axis=1), col=np.concatenate([col[n] for n in COL], axis=1),
                bias=np.stack([bias, bias]), con=con, half=half, big=big)


def kernel(**inputs):
    import concourse.bacc as bacc
    from concourse.bass_utils import run_bass_kernel_spmd

    nc = bacc.Bacc("TRN2", target_bir_lowering=False, num_devices=1)
    arrays, args = {}, []
    for name, a in lay_out({n: np.asarray(a) for n, a in inputs.items()}).items():
        arrays[f"in_{name}_dram"] = np.ascontiguousarray(a)
        args.append(nc.dram_tensor(f"in_{name}_dram", a.shape, mybir.dt.from_np(a.dtype), kind="ExternalInput").ap())
    args.append(nc.dram_tensor("out_dram", (P, NS * C), F32, kind="ExternalOutput").ap())
    build(nc, *args)
    r = run_bass_kernel_spmd(nc, [arrays], core_ids=[0])
    return r.results[0]["out_dram"].reshape(P, NS, C).transpose(1, 0, 2).reshape(NB, S, C)
```

```python
from contextlib import ExitStack

import concourse.bass as bass
import numpy as np
from concourse import mybir

F32 = mybir.dt.float32
F16 = mybir.dt.float16
BF16 = mybir.dt.bfloat16
ALU = mybir.AluOpType
ACT = mybir.ActivationFunctionType
AX_X = mybir.AxisListType.X
ds = bass.ds

P = 128
BANK = 512
LN_EPS = 1e-5
GN_EPS = 1e-5
HEAD_DIV = 8.0
GATE_TEMP = 0.1
W_UP = 2.0 ** 6
W_DOWN = 1.0 / W_UP
M_UP = 2.0 ** 12
M_DOWN = 1.0 / M_UP
NEG_BIG = -1e30
EXP_CAP = 1e30

NB, S, C = 8, 512, 128
SUB = S // P
NS = NB * SUB
E, F = 8, 512
H, K = 16, 8
NG, HG = 4, 4
GC = HG * K
STK = 3 * GC
AUG = STK + HG
FC = F // P
PAIRS = E // 2
ITER = NB * PAIRS
CH = 2 * FC
HSLOTS = 4
LEAD = 2 * SUB
XW = S + 8
R_SCALE = float(1.0 / np.sqrt(np.float32(K)))
PHASES = ("F", "R", "F", "E", "M", "E")


def columns(parts):
    at, out = 0, {}
    for name, n in parts:
        out[name] = (at, n)
        at += n
    return out, at


LIN, LIN_N = columns([("mixed", 4 * C), ("wo_r", C), ("experts", E * C), ("router", E), ("q", C), ("k", C), ("v", C), ("wo_m", C)])
COL, COL_N = columns([("mix", 4), ("decay_row", 1), ("ln_w", 1), ("ln_b", 1), ("decay", H), ("bonus", H)])
CON, CON_N = columns([("ident", P), ("logit_scale", LEAD * 2 * E), ("head_mean", P), ("head_mean16", H), ("same_head", P),
                      ("rev_index", SUB * E), ("row_head", HG), ("v_head", HG * C), ("distance", P), ("later", P),
                      ("position", P), ("to_end", 1)])
HALF, HALF_N = columns([("ident", P), ("pick_expert", E * P), ("ones", P), ("k_hi", NG * STK), ("k_lo", NG * STK),
                        ("q_hi", NG * STK), ("q_lo", NG * STK)])
BIG, BIG_N = columns([("ident", P), ("keys_after", P), ("queries_before", P)])


def build(nc, x, ffn_router, ffn_w, lin, col, bias, con, half, big, out):
    with ExitStack() as ctx:
        def sb(name, cols, dt=F32):
            return ctx.enter_context(nc.sbuf_tensor(name, [P, cols], dt))

        def sem(name):
            return ctx.enter_context(nc.semaphore(name))

        psum = ctx.enter_context(nc.psum_tensor("psum", [P, 8 * BANK], F32))

        def bank(i, a=0, b=BANK):
            return psum[:, i * BANK + a:i * BANK + b]

        x_tok = sb("x_tok", NS * C)
        facc = sb("facc", NB * S)
        x_hi = sb("x_hi", NB * XW, F16)
        x_lo = sb("x_lo", NB * XW, F16)
        con_sb = sb("con_sb", CON_N)
        half_sb = sb("half_sb", HALF_N, F16)
        big_sb = sb("big_sb", BIG_N, BF16)
        col_sb = sb("col_sb", COL_N)
        neg_half = sb("neg_half", SUB * H)
        e_const = sb("e_const", 2 * E)
        raw = sb("raw", LIN_N + E * C + E)
        bias_raw = raw[:, LIN_N:LIN_N + E * C + E]
        ffn_g = [sb(f"ffn_gate_{h}", E * F, F16) for h in ("hi", "lo")]
        ffn_u = [sb(f"ffn_up_{h}", E * F, F16) for h in ("hi", "lo")]
        ffn_d = [sb(f"ffn_down_{h}", E * F, F16) for h in ("hi", "lo")]
        fr_w = [sb(f"fr_{h}", 2 * E, F16) for h in ("hi", "lo")]
        fr_raw = sb("fr_raw", 2 * E)
        ln_stat = sb("ln_stat", LEAD * 6)
        ln_mv = sb("ln_mv", LEAD * 2)
        ln_var = sb("ln_var", LEAD)
        ln_rstd = sb("ln_rstd", LEAD)
        x_norm = sb("x_norm", LEAD * P)
        merge_in = x_norm
        act_warm = sb("act_warm", 1)

        SCRATCH = 20850
        scratch = sb("scratch", SCRATCH)
        place = [0]

        def carve(cols, dt=F32):
            n = cols if dt == F32 else (cols + 1) // 2
            t = scratch[:, place[0]:place[0] + n]
            place[0] += n
            assert place[0] <= SCRATCH, place[0]
            return t if dt == F32 else t.bitcast(dt)

        x_T = carve(NB * S)
        cw_T = carve(NB * S, F16)
        lg = carve(LEAD * 2 * E)
        lg_max = carve(LEAD * 2)
        lg_shift = carve(LEAD * 2 * E)
        lg_exp = carve(LEAD * 2 * E)
        sm_sum = carve(LEAD * 2)
        cw_num = carve(LEAD * E)
        cw_sum = carve(LEAD)
        cw_eps = carve(LEAD)
        cw_den = carve(LEAD)
        cw_rec = carve(LEAD)
        cw_out = carve(LEAD * E)
        cw16 = carve(LEAD * 2 * E, F16)
        xc = [carve(S) for _ in range(2)]
        xc_hi = [carve(S, F16) for _ in range(2)]
        xc_lo = [carve(S, F16) for _ in range(2)]
        gate_act = [carve(S) for _ in range(2)]
        h32 = [carve(S) for _ in range(2)]
        h_hi = [carve(S, F16) for _ in range(HSLOTS)]
        h_lo = [carve(S, F16) for _ in range(HSLOTS)]

        place[0] = 0
        e_w = [carve(E * C + E, F16) for _ in range(2)]
        bias_w = carve(E * C + E, F16)
        e_max = carve(SUB)
        e_shift = carve(SUB * E)
        e_exp = carve(SUB * E)
        e_sum = carve(SUB)
        e_rec = carve(SUB)
        e_rank = carve(SUB * E)
        e_first = carve(SUB)
        e_one = carve(SUB * E)
        e_sel = carve(SUB * E)
        e_za = [carve(S) for _ in range(2)]
        e_zb = [carve(S) for _ in range(2)]
        e_z2 = [carve(S // 2) for _ in range(2)]
        e_z1 = [carve(S // 4) for _ in range(2)]

        place[0] = 0
        mix_scale = carve(8)
        mix_w = [[carve(4 * C, F16) for _ in range(2)] for _ in range(2)]
        r_wo = [carve(C, F16) for _ in range(2)]
        decay_neg = carve(H)
        decay_row = carve(1)
        w_intra = carve(H * P)
        w_qexp = carve(P)
        w_query = carve(P)
        w_chunk = carve(1)
        w_kexp = carve(H)
        w_key = carve(H)
        rk = [[carve(S, F16) for _ in range(2)] for _ in range(2)]
        r_decay = carve(2 * S)
        r_st = [carve(NG * HG * P, F16) for _ in range(SUB)]
        k_stk = [carve(NG * P, F16) for _ in range(SUB)]
        k_w = [carve(C) for _ in range(SUB - 1)]
        v_tok = [carve(C) for _ in range(SUB - 1)]
        v_by_head = [carve(HG * C) for _ in range(SUB)]
        setup_at = place[0]
        att = [[carve(S) for _ in range(NG)] for _ in range(2)]
        st_new = carve(C)
        state = [None] + [carve(C) for _ in range(SUB - 1)]
        y_at = place[0]
        y8 = carve(S)
        y_c = carve(S)
        y_sq = carve(S)
        g_var = carve(SUB * H)
        g_rstd = carve(SUB * H)
        silu_g = carve(S)
        y_n, g_wide, y_aff, y_g = y8, y_sq, y_sq, y_c
        y_parts = [carve(S, F16) for _ in range(2)]
        y_end, place[0] = place[0], setup_at
        w_exp = carve(H * P)
        w_later = carve(H * P)
        assert place[0] <= setup_at + 2 * NG * S
        place[0] = y_at
        mixed = [carve(4 * C) for _ in range(2)]
        assert place[0] <= y_end

        place[0] = 0
        m_w = [carve(4 * C, F16) for _ in range(2)]
        qk = [[carve(S, F16) for _ in range(2)] for _ in range(2)]
        q_stack = [carve(S, F16) for _ in range(2)]
        k_stack = [carve(S, F16) for _ in range(NG)]
        q_by_head = [carve(HG * S, F16) for _ in range(NG)]
        m_aug = carve(S, F16)
        neg_max = carve(SUB * HG)
        max_pad = carve(SUB * P, F16)
        v_aug = carve(SUB * H * 32)
        probs = [carve(HG * (S - j * P)) for j in range(SUB)]
        y_raw = carve(S)
        den_rec = carve(SUB * HG)
        y_tok = carve(S)
        yo = [carve(S, F16) for _ in range(2)]

        def con_(name):
            a, n = CON[name]
            return con_sb[:, a:a + n]

        def half_(name):
            a, n = HALF[name]
            return half_sb[:, a:a + n]

        def col_(name):
            a, n = COL[name]
            return col_sb[:, a:a + n]

        def raw_(name):
            a, n = LIN[name]
            return raw[:, a:a + n]

        def pick(name, g):
            return half_(name)[:, g * STK:(g + 1) * STK]

        ident = con_("ident")
        ident16 = half_("ident")

        def sub(t, s, n=1):
            return t[:, ds(s * P, n * P)]

        def seq(t, b):
            return t[:, ds(b * S, S)]

        def xsub(t, s):
            return t[:, ds((s // SUB) * XW + 8 + (s % SUB) * P, P)]

        def xchunk(t, b, n, before):
            return t[:, ds(b * XW + (8 + n * P - before), P)]

        def xseq(t, b, before=0):
            return t[:, ds(b * XW + (8 - before), S)]

        def xparts(t, s, g):
            if g == 1:
                return xsub(t, s)
            if g == SUB:
                return xseq(t, s // SUB)
            return by(t[:, 0:g // SUB * XW], g // SUB)[:, :, 8:XW]

        def prep_psum(g, at=6):
            return psum[:, (at + 1) * BANK - max(g, SUB) * P:(at + 1) * BANK][:, 0:g * P]

        def by(t, n):
            return t.rearrange("p (n c) -> p n c", n=n)

        def over(t, n, c):
            return t.rearrange("p (n o) -> p n o", o=1).to_broadcast([P, n, c])

        s_x = [sem(n) for n in ("x_loaded_first", "x_loaded_second", "x_loaded_rest")]
        s_fr = sem("ffn_router_loaded")
        s_con = sem("consts_loaded")
        s_lin = sem("other_weights_loaded")
        s_wraw = [sem(f"ffn_w_loaded{q}") for q in range(2)]
        s_pool_const = sem("pool_consts_set")
        s_bz = sem("bias_rows_cleared")
        s_frhi, s_frlo, s_whi, s_wlo = sem("router_hi"), sem("router_lo"), sem("ffn_w_hi"), sem("ffn_w_lo")
        s_bn, s_mv, s_var, s_rstd, s_xn, s_xT, s_xTs, s_xhi, s_xlo = [sem(n) for n in (
            "bn_stats_done", "mean_var_done", "var_ready", "rstd_ready", "x_norm_ready", "xT_in_psum", "xT_copied",
            "x_hi_ready", "x_lo_ready")]
        s_mrg_in, s_mrg_ps, s_mrg = sem("merge_in_ready"), sem("merge_in_psum"), sem("merged")
        s_lg, s_lgs, s_exp, s_cw, s_cwTp, s_cwT = [sem(n) for n in (
            "logits_in_psum", "logits_shifted", "logits_exp", "cw_ready", "cwT_in_psum", "cwT_ready")]
        s_rstep = sem("routing_step")
        ROUTE_STEPS = 9
        s_bc, s_xc, s_xchi, s_xclo = [sem(n) for n in ("cw_broadcast", "xc_ready", "xc_hi_ready", "xc_lo_ready")]
        s_g, s_u, s_s, s_h, s_hhi, s_hlo, s_hfree = [sem(n) for n in (
            "gate_in_psum", "up_in_psum", "gate_act_ready", "h_ready", "h_hi_ready", "h_lo_ready", "h_slot_free")]
        s_facc = sem("ffn_out_added")
        s_ewhi, s_ewlo, s_bhi, s_blo = [sem(n) for n in ("e_w_hi", "e_w_lo", "bias_hi", "bias_lo")]
        s_elg, s_esh, s_eexp, s_esel = [sem(n) for n in (
            "e_logits_in_psum", "e_logits_shifted", "e_exp", "e_selected")]
        s_estep = sem("e_routing_step")
        E_STEPS = 5
        s_eya, s_eyb, s_eza, s_ezb, s_ez2, s_ez1, s_eadd = [sem(n) for n in (
            "e_low_experts_in_psum", "e_high_experts_in_psum", "e_low_weighted", "e_high_added",
            "e_two_left", "e_one_left", "e_added")]
        s_st = sem("stored")

        plan, n_merge, seen = [], 0, dict(F=0, E=0, R=0, M=0)
        for i, kind in enumerate(PHASES):
            merge = i > 0 and PHASES[i - 1] == "F"
            plan.append(dict(i=i, kind=kind, n0=i * NS, use=seen[kind], merge=merge, g0=n_merge))
            n_merge += NB if merge else 0
            seen[kind] += 1

        def peeled(f):
            return 1 if f else PAIRS - 1

        def splits(f, i):
            return f == 0 and isinstance(i, int) and i < PAIRS - 1

        def cwT_psum(g):
            a = 4 * BANK if g == LEAD else 7 * BANK + 64
            return psum[0:2 * E, a:a + g * P // 2].bitcast(F16)

        def begin(eng, i):
            if i == 0:
                return
            before = plan[i - 1]
            if before["kind"] == "F":
                eng.wait_ge(s_facc, (before["use"] + 1) * (ITER + 1))
            if before["kind"] == "E":
                eng.wait_ge(s_eadd, (before["use"] + 1) * NS + 2)
            if before["kind"] == "R":
                eng.wait_ge(s_rout, NB + 1)
            if before["kind"] == "M":
                eng.wait_ge(s_mout, NB)

        s_rset, s_rexp, s_rwhi, s_rwlo = sem("rwkv_setup"), sem("rwkv_exps"), sem("rwkv_w_hi"), sem("rwkv_w_lo")
        s_rp, s_rhi, s_rlo, s_rdec, s_kp, s_khi, s_klo = [sem(n) for n in (
            "r_in_psum", "r_hi_ready", "r_lo_ready", "r_decay_ready", "k_in_psum", "k_hi_ready", "k_lo_ready")]
        s_y8, s_gmean, s_yc, s_ysq, s_gvarp, s_gvar, s_grstd, s_gp, s_sg, s_gwide, s_grb, s_yn, s_yaff, s_yg, s_yghi, s_yglo, s_rop, s_rout = [
            sem(n) for n in ("y_copied", "gn_mean_in_psum", "gn_centred", "gn_squares", "gn_var_in_psum", "gn_var_ready",
                             "gn_rstd_ready", "g_in_psum", "silu_g_ready", "gn_rstd_repeated", "gn_rstd_in_psum", "gn_normed", "gn_affine",
                             "y_gated", "y_hi_ready", "y_lo_ready", "rwkv_out_in_psum", "rwkv_added")]
        s_rst, s_kst, s_kv, s_rbyh, s_kstk, s_kw, s_vtok, s_vbyh, s_stp, s_stm, s_state, s_av = [sem(n) for n in (
            "r_stack_in_psum", "k_stack_in_psum", "kv_in_psum", "r_by_head", "k_stack_ready", "k_weighted", "v_ready",
            "v_by_head", "state_in_psum", "state_masked", "state_ready", "att_used")]
        s_attp, s_attw = sem("att_in_psum"), sem("att_weighted")
        s_mset, s_mpad0, s_mwhi, s_mwlo = sem("attention_setup"), sem("max_pad_cleared"), sem("attention_w_hi"), sem("attention_w_lo")
        s_mqp, s_mqhi, s_mqlo, s_mkp, s_mkhi, s_mklo, s_mvp, s_mv_in = [sem(n) for n in (
            "mq_in_psum", "mq_hi_ready", "mq_lo_ready", "mk_in_psum", "mk_hi_ready", "mk_lo_ready", "mv_in_psum", "mv_ready")]
        s_yTp, s_yohi, s_yolo, s_mop, s_mout = [sem(n) for n in (
            "my_transposed", "my_hi_ready", "my_lo_ready", "attention_out_in_psum", "attention_added")]
        s_mks, s_mqs, s_mkst, s_mqst, s_mqh, s_mmax, s_mpad, s_mTp, s_maug, s_mqaug, s_yraw, s_ytp, s_drec, s_ytok = [
            sem(n) for n in ("mk_stack_in_psum", "mq_stack_in_psum", "mk_stack_ready", "mq_stack_ready", "mq_by_head",
                             "max_ready", "max_padded", "max_transposed", "max_rows_ready", "max_rows_by_head",
                             "weighted_values_copied", "weighted_values_transposed",
                             "denominator_rec", "attention_normed")]
        s_p1, s_p1used = sem("scores_by_query_in_psum"), sem("scores_by_query_used")
        s_p2, s_p2exp = sem("scores_by_key_in_psum"), sem("probs_ready")
        s_pvq = sem("probs_used")
        block = ctx.enter_context(nc.Block())

        Q_TILES = [(0, 0, 4), (1, 0, 2), (1, 2, 2)] + [(q, r, 1) for q in (2, 3) for r in range(HG)]
        K_TILES = [(j, r, 1) for j in (0, 1) for r in range(HG)] + [(2, 0, 2), (2, 2, 2), (3, 0, 4)]
        QT, KT = len(Q_TILES), len(K_TILES)
        KT_END = [sum(t[0] <= j for t in K_TILES) for j in range(SUB)]
        UNITS = NB * NG
        SCORED, USED = KT * NG, SUB

        @block.sync
        def _(sp):
            def load_x(b):
                sp.dma_start(x_tok[:, b * S:(b + 1) * S], x[:, b * S:(b + 1) * S]).then_inc(s_x[min(b, 2)], 16)

            con_first, half_first = CON["head_mean"][0], HALF["ones"][0]
            load_x(0)
            load_x(1)
            sp.dma_start(con_sb[:, 0:con_first], con[:, 0:con_first]).then_inc(s_con, 16)
            sp.dma_start(fr_raw[:], ffn_router).then_inc(s_fr, 16)
            sp.dma_start(half_sb[:, 0:half_first], half[:, 0:half_first]).then_inc(s_con, 16)
            for e in range(E):
                if e >= 2:
                    sp.wait_ge(s_wlo, 3 * (e - 1))
                q = e % 2
                sp.dma_start(raw[:, 3 * F * q:3 * F * (q + 1)], ffn_w[e]).then_inc(s_wraw[q], 16)
                if e == 1:
                    for b in range(2, NB):
                        load_x(b)
            sp.dma_start(con_sb[:, con_first:], con[:, con_first:]).then_inc(s_con, 16)
            sp.dma_start(half_sb[:, half_first:], half[:, half_first:]).then_inc(s_con, 16)
            sp.dma_start(big_sb[:], big).then_inc(s_con, 16)
            sp.dma_start(col_sb[:], col).then_inc(s_con, 16)
            sp.wait_ge(s_wlo, 3 * E)
            sp.dma_start(raw[:, 0:LIN_N], lin).then_inc(s_lin, 16)
            sp.wait_ge(s_bz, 1)
            sp.dma_start(bias_raw[0:1, :], bias[0:1, :]).then_inc(s_lin, 16)
            sp.dma_start(bias_raw[32:33, :], bias[1:2, :]).then_inc(s_lin, 16)
            sp.wait_ge(s_lin, 48)
            begin(sp, len(plan))
            sp.dma_start(out, x_tok[:]).then_inc(s_st, 16)
            sp.wait_ge(s_st, 16)

        @block.gpsimd
        def _(pool):
            def prep_rstd(n, g):
                pool.wait_ge(s_var, n + g)
                pool.tensor_tensor(ln_rstd[:, 0:g], ln_var[:, 0:g], neg_half[:, 0:g], ALU.pow).then_inc(s_rstd, g)

            pool.memset(neg_half[:], -0.5).then_inc(s_pool_const, 1)
            pool.memset(e_const[:], float(np.exp(1.0))).then_inc(s_pool_const, 1)
            pool.memset(by(x_hi[:], NB)[:, :, 0:8], 0.0).then_inc(s_pool_const, 1)
            pool.memset(by(x_lo[:], NB)[:, :, 0:8], 0.0).then_inc(s_pool_const, 1)
            pool.wait_ge(s_pool_const, 2)

            def clear_bias():
                pool.wait_ge(s_wlo, 3 * E)
                pool.memset(bias_raw, 0.0).then_inc(s_bz, 1)

            def ffn(ph):
                f, n0 = ph["use"], ph["n0"]
                r0, m0 = f * NS, f * NB * E

                def exps(n):
                    pool.wait_ge(s_lgs, n + 1)
                    pool.tensor_tensor(lg_exp[:, 0:2 * E], e_const[:], lg_shift[:, 0:2 * E], ALU.pow).then_inc(s_exp, 1)

                def xc_low(m, q):
                    pool.wait_ge(s_xchi, m + 1)
                    pool.tensor_tensor(xc_lo[q], xc[q], xc_hi[q], ALU.subtract).then_inc(s_xclo, 1)

                begin(pool, ph["i"])
                pool.memset(cw_T, 0.0).then_inc(s_pool_const, 1)
                pool.memset(facc[:], 0.0).then_inc(s_facc, 1)
                prep_rstd(n0, LEAD)
                xc_low(m0, 0)
                xc_low(m0 + 1, 1)

                def body(i, prepare, last):
                    s = i + LEAD
                    if prepare:
                        prep_rstd(n0 + s, 1)
                    if not last:
                        xc_low(m0 + 2 * i + 2, 0)
                    if not last:
                        xc_low(m0 + 2 * i + 3, 1)
                    if prepare:
                        exps(r0 + s)

                for i in range(peeled(f)):
                    body(i, True, False)
                if f == 0:
                    clear_bias()
                with pool.Fori(peeled(f), ITER - LEAD) as i:
                    body(i, True, False)
                with pool.Fori(ITER - LEAD, ITER - 1) as i:
                    body(i, False, False)
                body(ITER - 1, False, True)

            def moe(ph):
                n0, t0 = ph["n0"], ph["use"] * NS

                def fold(t, q):
                    pool.wait_ge(s_ezb, t + 3)
                    pool.tensor_tensor(e_z2[q], e_zb[q][:, 0:2 * C], e_zb[q][:, 2 * C:4 * C], ALU.add).then_inc(s_ez2, 1)
                    pool.wait_ge(s_ez2, t + 3)
                    pool.wait_ge(s_eadd, t + 1)
                    pool.tensor_tensor(e_z1[q], e_z2[q][:, 0:C], e_z2[q][:, C:2 * C], ALU.add).then_inc(s_ez1, 1)

                prep_rstd(n0, LEAD)

                def body(b, prep):
                    for k in range(SUB):
                        fold(t0 + b * SUB + k, k % 2)
                        if k == 1 and prep:
                            prep_rstd(n0 + SUB * b + LEAD, SUB)

                with pool.Fori(0, NB - 2) as b:
                    body(b, True)
                body(NB - 2, False)
                body(NB - 1, False)

            def rwkv(ph):
                n0 = ph["n0"]

                def gn_rstd(b):
                    pool.wait_ge(s_gvar, b + 1)
                    pool.tensor_tensor(g_rstd, g_var, neg_half[:, 0:SUB * H], ALU.pow).then_inc(s_grstd, 1)

                def gate(b):
                    pool.wait_ge(s_yaff, b + 1)
                    pool.wait_ge(s_sg, b + 1)
                    pool.tensor_tensor(y_g, y_aff, silu_g, ALU.mult).then_inc(s_yg, 1)

                def gate_low(b):
                    pool.wait_ge(s_yghi, b + 1)
                    pool.tensor_tensor(y_parts[1], y_g, y_parts[0], ALU.subtract).then_inc(s_yglo, 1)

                begin(pool, ph["i"])
                prep_rstd(n0, LEAD)

                def body(b, first, prep):
                    if not first:
                        gn_rstd(b - 1)
                    if prep:
                        prep_rstd(n0 + SUB * b + 2 * SUB, SUB)
                    if not first:
                        gate(b - 1)
                        gate_low(b - 1)

                body(0, True, True)
                with pool.Fori(1, NB - 2) as b:
                    body(b, False, True)
                body(NB - 2, False, False)
                body(NB - 1, False, False)
                gn_rstd(NB - 1)
                gate(NB - 1)
                gate_low(NB - 1)

            def attention(ph):
                n0 = ph["n0"]

                def mask_queries(u, g):
                    pool.wait_ge(s_mqst, u + 1)
                    pool.wait_ge(s_p2, KT * u + KT)
                    stack = q_stack[g % 2][0:STK].rearrange("p (o i) -> p o i", o=1).to_broadcast([STK, HG, S])
                    mask = con_("row_head")[0:STK].rearrange("p (r o) -> p r o", o=1).to_broadcast([STK, HG, S])
                    pool.tensor_tensor(by(q_by_head[g][0:STK], HG), stack, mask, ALU.mult).then_inc(s_mqh, 1)

                begin(pool, ph["i"])
                pool.memset(v_aug, 0.0).then_inc(s_mset, 1)
                pool.wait_ge(s_mset, 1)
                pool.memset(by(v_aug, SUB * H)[:, :, K:2 * K], 1.0).then_inc(s_mset, 1)
                prep_rstd(n0, LEAD)
                pool.wait_ge(s_con, 96)
                for u in range(NG):
                    mask_queries(u, u)

                def body(b, prep, more):
                    for g in range(NG):
                        u = NG * b + g
                        if g == 1 and prep:
                            prep_rstd(n0 + SUB * b + 2 * SUB, SUB)
                        if more:
                            mask_queries(u + NG, g)

                body(0, True, True)
                with pool.Fori(1, NB - 2) as b:
                    body(b, True, True)
                body(NB - 2, False, True)
                body(NB - 1, False, False)

            for ph in plan:
                dict(F=ffn, E=moe, R=rwkv, M=attention)[ph["kind"]](ph)

        @block.scalar
        def _(act):
            def prep_merge(ph, b, n=1):
                act.wait_ge(s_mrg_ps, ph["g0"] + b)
                act.wait_ge(s_xT, ph["n0"] + SUB * b)
                act.activation(merge_in[:, 0:n * S], facc[:, ds(b * S, n * S)], ACT.Copy).then_inc(s_mrg_in, n)

            def prep_xT(n, s, g, keep, at=6):
                act.wait_ge(s_xT, n + g)
                src = prep_psum(g, at)
                if keep:
                    act.activation(sub(x_T, s, g), src, ACT.Copy).then_inc(s_xTs, g)
                act.activation(xparts(x_hi, s, g), by(src, 2) if g == LEAD else src, ACT.Copy).then_inc(s_xhi, g)

            def ffn(ph):
                f, n0 = ph["use"], ph["n0"]
                r0, m0, c0 = f * NS, f * NB * E, f * ITER * CH

                def split_weight(e, t):
                    if t == 0:
                        act.wait_ge(s_wraw[e % 2], 16 * (e // 2 + 1))
                    a = 3 * F * (e % 2) + t * F
                    act.activation((ffn_g, ffn_u, ffn_d)[t][0][:, e * F:(e + 1) * F], raw[:, a:a + F], ACT.Copy, scale=W_UP).then_inc(s_whi, 1)

                def copy_cwT(n, s, g):
                    act.wait_ge(s_cwTp, n + g)
                    act.activation(cw_T[0:2 * E, ds(s * P, g * P)], cwT_psum(g), ACT.Copy).then_inc(s_cwT, g)

                def silu(c, k):
                    act.wait_ge(s_g, c + 1)
                    if k >= 2 or f:
                        act.wait_ge(s_h, c - 1)
                    act.activation(gate_act[k % 2], bank(k % 2), ACT.Silu, scale=W_DOWN).then_inc(s_s, 1)

                def h_high(c, k):
                    act.wait_ge(s_h, c + 1)
                    act.wait_ge(s_hfree, c + 1)
                    act.activation(h_hi[k % HSLOTS], h32[k % 2], ACT.Copy).then_inc(s_hhi, 1)

                def xc_high(m, q, chunks_used):
                    act.wait_ge(s_xc, m + 1)
                    if chunks_used is not None:
                        act.wait_ge(s_u, chunks_used)
                    act.activation(xc_hi[q], xc[q], ACT.Copy).then_inc(s_xchi, 1)

                begin(act, ph["i"])
                if f == 0:
                    act.wait_ge(s_fr, 16)
                    act.activation(fr_w[0][:], fr_raw[:], ACT.Copy, scale=W_UP).then_inc(s_frhi, 1)
                prep_xT(n0, 0, LEAD, True)
                act.wait_ge(s_lgs, r0 + LEAD)
                act.activation(lg_exp, lg_shift, ACT.Exp).then_inc(s_exp, LEAD)
                act.wait_ge(s_pool_const, 4 + f + 1)
                copy_cwT(r0, 0, LEAD)
                if f == 0:
                    for e in range(2):
                        for t in range(3):
                            split_weight(e, t)
                xc_high(m0, 0, None)
                xc_high(m0 + 1, 1, None)
                silu(c0, 0)
                silu(c0 + 1, 1)
                h_high(c0, 0)

                def body(i, prepare, finish, last):
                    c = c0 + i * CH
                    s = i + LEAD
                    for k in range(CH):
                        if not (last and k + 2 >= CH):
                            silu(c + k + 2, k + 2)
                        if not (last and k + 1 >= CH):
                            h_high(c + k + 1, k + 1)
                        if not last and k == 2:
                            xc_high(m0 + 2 * i + 2, 0, c + FC)
                        if not last and k == 6:
                            xc_high(m0 + 2 * i + 3, 1, c + 2 * FC)
                        if finish and k == 5:
                            copy_cwT(r0 + s - 1, s - 1, 1)
                        if prepare and k == 4:
                            prep_xT(n0 + s, s, 1, True)
                        if k < 6 and splits(f, i):
                            split_weight(2 * i + 2 + k // 3, k % 3)

                for i in range(peeled(f)):
                    body(i, True, i > 0, False)
                with act.Fori(peeled(f), ITER - LEAD) as i:
                    body(i, True, True, False)
                body(ITER - LEAD, False, True, False)
                with act.Fori(ITER - LEAD + 1, ITER - 1) as i:
                    body(i, False, False, False)
                body(ITER - 1, False, False, True)

            def moe(ph):
                n0, use = ph["n0"], ph["use"]
                t0, b0 = use * NS, use * NB

                def exps(b):
                    act.wait_ge(s_esh, b + 1)
                    act.activation(e_exp, e_shift, ACT.Exp, scale=W_DOWN).then_inc(s_eexp, 1)

                def weigh(t, b, k):
                    act.wait_ge(s_esel, 2 * b + 2)
                    act.wait_ge(s_eya, t + 1)
                    act.wait_ge(s_ezb, t + 1)
                    for e in range(E // 2):
                        ins = act.activation(e_za[k % 2][:, e * C:(e + 1) * C], bank(2 * (k % 2), e * C, (e + 1) * C), ACT.Copy,
                                             scale=e_sel[:, k * E + e:k * E + e + 1])
                        if e == E // 2 - 1:
                            ins.then_inc(s_eza, 1)

                begin(act, ph["i"])
                act.wait_ge(s_lin, 48)
                act.wait_ge(s_con, 96)
                act.activation(e_w[0], raw[:, LIN["experts"][0]:LIN["experts"][0] + E * C + E], ACT.Copy, scale=W_UP).then_inc(s_ewhi, 1)
                act.activation(bias_w, bias_raw, ACT.Copy, scale=W_UP).then_inc(s_bhi, 1)
                if ph["merge"]:
                    prep_merge(ph, 0, 2)
                prep_xT(n0, 0, LEAD, False)
                exps(b0)

                def body(b, prep, more):
                    if prep and ph["merge"]:
                        prep_merge(ph, b + 2)
                    for k in range(SUB):
                        weigh(t0 + b * SUB + k, b0 + b, k)
                        if k == 2 and more:
                            exps(b0 + b + 1)
                    if prep:
                        prep_xT(n0 + SUB * b + LEAD, (b + 2) * SUB, SUB, False)

                with act.Fori(0, NB - 2) as b:
                    body(b, True, True)
                body(NB - 2, False, True)
                body(NB - 1, False, False)

            def rwkv(ph):
                n0 = ph["n0"]

                def r_high(b):
                    act.wait_ge(s_rp, b + 1)
                    act.wait_ge(s_rst, SUB * b)
                    act.activation(rk[0][0], bank(6), ACT.Copy, scale=W_DOWN).then_inc(s_rhi, 1)

                def k_high(b):
                    act.wait_ge(s_kp, b + 1)
                    act.wait_ge(s_kst, SUB * b)
                    act.activation(rk[1][0], bank(6), ACT.Copy, scale=W_DOWN).then_inc(s_khi, 1)

                def stacks(u, n):
                    act.wait_ge(s_rst, u + 1)
                    act.wait_ge(s_attp, SUB * u + SUB)
                    dst = r_st[n][0:STK].rearrange("p (g r i) -> p g r i", g=NG, r=HG)
                    for r in range(HG):
                        ins = act.activation(dst[:, :, r], by(bank(5)[0:STK], NG), ACT.Copy, scale=con_("row_head")[0:STK, r:r + 1])
                    ins.then_inc(s_rbyh, 1)
                    act.wait_ge(s_kst, u + 1)
                    act.activation(k_stk[n][0:STK], bank(3)[0:STK], ACT.Copy).then_inc(s_kstk, 1)

                def y_copy(b):
                    act.wait_ge(s_av, SUB * b + 2 * SUB)
                    act.wait_ge(s_rout, b + 1)
                    act.activation(y8, bank(4), ACT.Copy, scale=1.0 / HEAD_DIV).then_inc(s_y8, 1)

                def squares(b):
                    act.wait_ge(s_yc, b + 1)
                    act.activation(y_sq, y_c, ACT.Square).then_inc(s_ysq, 1)

                def gate_silu(b):
                    act.wait_ge(s_gp, b + 1)
                    act.activation(silu_g, bank(2), ACT.Silu, scale=W_DOWN).then_inc(s_sg, 1)

                def widen_rstd(b):
                    act.wait_ge(s_grstd, b + 1)
                    act.activation(by(g_wide, SUB * H), over(g_rstd, SUB * H, K), ACT.Copy).then_inc(s_gwide, 1)

                def affine(b):
                    act.wait_ge(s_yn, b + 1)
                    act.activation(y_aff, y_n, ACT.Identity, scale=col_("ln_w"), bias=col_("ln_b")).then_inc(s_yaff, 1)

                def y_high(b):
                    act.wait_ge(s_yg, b + 1)
                    act.activation(y_parts[0], y_g, ACT.Copy).then_inc(s_yghi, 1)

                begin(act, ph["i"])
                if ph["merge"]:
                    prep_merge(ph, 0, 2)
                act.wait_ge(s_lin, 48)
                act.wait_ge(s_con, 96)
                act.activation(w_kexp, col_("decay"), ACT.Exp).then_inc(s_rexp, 1)
                act.activation(w_qexp[:, 0:1], col_("decay_row"), ACT.Exp).then_inc(s_rexp, 1)
                act.wait_ge(s_rset, 2)
                for h in range(H):
                    ins = act.activation(w_exp[:, h * P:(h + 1) * P], con_("distance"), ACT.Exp, scale=decay_neg[:, h:h + 1])
                ins.then_inc(s_rexp, 1)
                act.activation(w_kexp, decay_neg, ACT.Exp, scale=con_("to_end")).then_inc(s_rexp, 1)
                act.activation(w_chunk, decay_row, ACT.Exp, scale=float(P)).then_inc(s_rexp, 1)
                act.activation(w_qexp, con_("position"), ACT.Exp, scale=decay_row).then_inc(s_rexp, 1)
                act.activation(act_warm[:], ident[:, 0:1], ACT.Silu)
                for m in range(2):
                    act.wait_ge(s_rset, 4 + m)
                    act.activation(mix_w[m][0], mixed[m], ACT.Copy).then_inc(s_rwhi, 1)
                act.activation(r_wo[0], raw_("wo_r"), ACT.Copy, scale=W_UP).then_inc(s_rwhi, 1)
                prep_xT(n0, 0, LEAD, False)
                r_high(0)
                k_high(0)
                stacks(0, 0)
                stacks(1, 1)

                def body(b, first, prep, more):
                    for n in range(SUB):
                        if n == 0 and not first:
                            y_copy(b - 1)
                        if n == 0 and prep and ph["merge"]:
                            prep_merge(ph, b + 2)
                        if more or n < SUB - 2:
                            stacks(SUB * b + n + 2, (n + 2) % SUB)
                        if n == 0 and not first:
                            squares(b - 1)
                        if n == 1 and more:
                            r_high(b + 1)
                        if n == 1 and not first:
                            gate_silu(b - 1)
                        if n == 1 and more:
                            k_high(b + 1)
                        if n == 3 and prep:
                            prep_xT(n0 + SUB * b + 2 * SUB, SUB * b + 2 * SUB, SUB, False)
                        if n == 2 and not first:
                            widen_rstd(b - 1)
                            affine(b - 1)
                        if n == 3 and not first:
                            y_high(b - 1)

                body(0, True, True, True)
                with act.Fori(1, NB - 2) as b:
                    body(b, False, True, True)
                body(NB - 2, False, False, True)
                body(NB - 1, False, False, False)
                for step in (y_copy, squares, gate_silu, widen_rstd, affine, y_high):
                    step(NB - 1)

            def attention(ph):
                n0 = ph["n0"]

                def q_high(b):
                    act.wait_ge(s_mqp, b + 1)
                    act.wait_ge(s_mqs, NG * b)
                    act.activation(qk[0][0], bank(5), ACT.Copy, scale=W_DOWN).then_inc(s_mqhi, 1)

                def k_high(b):
                    act.wait_ge(s_mkp, b + 1)
                    act.wait_ge(s_mks, NG * b)
                    act.activation(qk[1][0], bank(6), ACT.Copy, scale=W_DOWN).then_inc(s_mkhi, 1)

                def key_stack(u, g):
                    act.wait_ge(s_mks, u + 1)
                    act.wait_ge(s_p2, KT * u + KT)
                    act.activation(k_stack[g][0:STK], bank(5)[0:STK], ACT.Copy).then_inc(s_mkst, 1)

                def query_stack(u, g):
                    act.wait_ge(s_mqs, u + 1)
                    act.wait_ge(s_mqh, u + 1)
                    act.activation(q_stack[g % 2][0:STK], bank(6)[0:STK], ACT.Copy).then_inc(s_mqst, 1)

                def maxima(u):
                    act.wait_ge(s_mTp, u + 1)
                    act.wait_ge(s_mqaug, u)
                    act.activation(m_aug[STK:AUG], bank(6)[STK:AUG], ACT.Copy).then_inc(s_maug, 1)

                def exps(u, g, t):
                    j, r, n = K_TILES[t]
                    w = S - j * P
                    act.wait_ge(s_p2, SCORED + KT * u + t + 1)
                    act.wait_ge(s_pvq, SUB * u + j + 1)
                    act.activation(probs[j][:, r * w:(r + n) * w], bank((g + t) % 2, 0, n * w), ACT.Exp, scale=R_SCALE).then_inc(s_p2exp, 1)

                def values(u):
                    act.wait_ge(s_pvq, USED + SUB * u + SUB)
                    act.wait_ge(s_ytp, u)
                    act.activation(y_raw, bank(7), ACT.Copy).then_inc(s_yraw, 1)

                def out_high(b):
                    act.wait_ge(s_yTp, b + 1)
                    act.wait_ge(s_mop, b + 1)
                    act.activation(yo[0], bank(4), ACT.Copy).then_inc(s_yohi, 1)

                begin(act, ph["i"])
                act.wait_ge(s_lin, 48)
                act.wait_ge(s_con, 96)
                a = LIN["q"][0]
                act.activation(m_w[0], raw[:, a:a + 4 * C], ACT.Copy, scale=W_UP).then_inc(s_mwhi, 1)
                prep_xT(n0, 0, LEAD, False, 4)
                q_high(0)
                k_high(0)
                for u in range(NG):
                    key_stack(u, u)
                    query_stack(u, u)
                maxima(0)

                def body(b, first, prep, more):
                    for g in range(NG):
                        u = NG * b + g
                        if g == 0 and more:
                            q_high(b + 1)
                        if g == 1 and not first:
                            out_high(b - 1)
                        for t in range(KT):
                            if t == KT_END[1] and g == 0 and more:
                                k_high(b + 1)
                            if t == KT_END[1] and not (first and g == 0):
                                values(u - 1)
                            exps(u, g, t)
                            if t == KT_END[0] and (more or g < NG - 1):
                                maxima(u + 1)
                        if more:
                            key_stack(u + NG, g)
                            query_stack(u + NG, g)
                        if g == 2 and prep:
                            prep_xT(n0 + SUB * b + 2 * SUB, SUB * b + 2 * SUB, SUB, False, 4)

                body(0, True, True, True)
                with act.Fori(1, NB - 2) as b:
                    body(b, False, True, True)
                body(NB - 2, False, False, True)
                body(NB - 1, False, False, False)
                values(UNITS - 1)
                out_high(NB - 1)

            for ph in plan:
                dict(F=ffn, E=moe, R=rwkv, M=attention)[ph["kind"]](ph)

        @block.vector
        def _(dve):
            def prep_add(m, b, n=1):
                dve.wait_ge(s_mrg_ps, m + n)
                x_b = x_tok[:, ds(b * S, n * S)]
                dve.tensor_tensor(x_b, x_b, prep_psum(n * SUB), ALU.add).then_inc(s_mrg, n)

            def prep_bn(n, s, g):
                for q in range(g):
                    ins = dve.bn_stats(ln_stat[:, 6 * q:6 * q + 6], sub(x_tok, s + q))
                ins.then_inc(s_bn, g)
                dve.wait_ge(s_bn, n + g)

            def prep_aggr(n, g):
                for q in range(g):
                    ins = dve.bn_aggr(ln_mv[:, 2 * q:2 * q + 2], ln_stat[:, 6 * q:6 * q + 6])
                ins.then_inc(s_mv, g)
                dve.wait_ge(s_mv, n + g)
                dve.tensor_scalar(ln_var[:, 0:g], ln_mv[:, 1:2 * g:2], LN_EPS, None, ALU.add).then_inc(s_var, g)

            def prep_norm(n, s, g):
                dve.wait_ge(s_rstd, n + g)
                dve.wait_ge(s_xT, n)
                for q in range(g):
                    ins = dve.tensor_scalar(x_norm[:, q * P:(q + 1) * P], sub(x_tok, s + q), ln_mv[:, 2 * q:2 * q + 1],
                                            ln_rstd[:, q:q + 1], ALU.subtract, ALU.mult)
                ins.then_inc(s_xn, g)

            def prep_low(n, s, g, at=6):
                dve.wait_ge(s_xhi, n + g)
                lo, hi = [xparts(t, s, g) for t in (x_lo, x_hi)]
                src = prep_psum(g, at)
                dve.tensor_tensor(lo, by(src, 2) if g == LEAD else src, hi, ALU.subtract).then_inc(s_xlo, g)

            def low_weights(w, cols, a):
                return dve.scalar_tensor_tensor(w[1][:, cols], raw[:, a:a + cols.stop - cols.start], W_UP, w[0][:, cols], ALU.mult, ALU.subtract)

            def all_loaded():
                for s, n in zip(s_x, (1, 1, NB - 2)):
                    dve.wait_ge(s, 16 * n)

            def ffn(ph):
                f, n0 = ph["use"], ph["n0"]
                r0, m0, c0, a0 = f * NS, f * NB * E, f * ITER * CH, f * ITER

                def split_weight(e, t):
                    dve.wait_ge(s_whi, 3 * e + t + 1)
                    low_weights((ffn_g, ffn_u, ffn_d)[t], slice(e * F, (e + 1) * F), 3 * F * (e % 2) + t * F).then_inc(s_wlo, 1)

                def step(n, g, k):
                    dve.wait_ge(s_rstep, n * ROUTE_STEPS + k * g)

                def scale_logits(n, g):
                    dve.wait_ge(s_lg, n + g)
                    w = 2 * E * g
                    dve.tensor_tensor(lg[:, 0:w], bank(7, 0, w), con_("logit_scale")[:, 0:w], ALU.mult).then_inc(s_rstep, g)

                def shift_logits(n, g):
                    w = 2 * E * g
                    step(n, g, 1)
                    dve.tensor_reduce(lg_max[:, 0:2 * g], by(lg[:, 0:w], 2 * g), AX_X, ALU.max).then_inc(s_rstep, g)
                    step(n, g, 2)
                    dve.tensor_tensor(by(lg_shift[:, 0:w], 2 * g), by(lg[:, 0:w], 2 * g), over(lg_max[:, 0:2 * g], 2 * g, E),
                                      ALU.subtract).then_inc(s_lgs, g)

                def exp_sums(n, g):
                    w = 2 * E * g
                    ex = lg_exp[:, 0:w].rearrange("p (g s e) -> p g s e", g=g, s=2)
                    dve.wait_ge(s_exp, n + g)
                    dve.tensor_reduce(sm_sum[:, 0:2 * g], by(lg_exp[:, 0:w], 2 * g), AX_X, ALU.add).then_inc(s_rstep, g)
                    dve.tensor_tensor(by(cw_num[:, 0:E * g], g), ex[:, :, 0], ex[:, :, 1], ALU.mult).then_inc(s_rstep, g)

                def cw_sums(n, g):
                    step(n, g, 4)
                    dve.scalar_tensor_tensor(cw_eps[:, 0:g], sm_sum[:, 0:2 * g:2], 1e-9, sm_sum[:, 1:2 * g:2], ALU.mult,
                                             ALU.mult).then_inc(s_rstep, g)
                    dve.tensor_reduce(cw_sum[:, 0:g], by(cw_num[:, 0:E * g], g), AX_X, ALU.add).then_inc(s_rstep, g)

                def cw_divisor(n, g):
                    step(n, g, 6)
                    dve.tensor_tensor(cw_den[:, 0:g], cw_sum[:, 0:g], cw_eps[:, 0:g], ALU.add).then_inc(s_rstep, g)

                def cw_reciprocal(n, g):
                    step(n, g, 7)
                    dve.reciprocal(cw_rec[:, 0:g], cw_den[:, 0:g]).then_inc(s_rstep, g)

                def cw_parts(g):
                    return [cw16[:, 0:2 * E * g].rearrange("p (g s e) -> p g s e", g=g, s=2)[:, :, h] for h in range(2)]

                def cw_high(n, g):
                    num, out32 = [by(t[:, 0:E * g], g) for t in (cw_num, cw_out)]
                    step(n, g, 8)
                    dve.tensor_tensor(out32, num, over(cw_rec[:, 0:g], g, E), ALU.mult).then_inc(s_rstep, g)
                    dve.wait_ge(s_cwTp, n)
                    dve.tensor_tensor(cw_parts(g)[0], num, over(cw_rec[:, 0:g], g, E), ALU.mult).then_inc(s_cw, g)

                def cw_low(n, g):
                    step(n, g, 9)
                    dve.wait_ge(s_cw, 2 * n + g)
                    dve.tensor_tensor(cw_parts(g)[1], by(cw_out[:, 0:E * g], g), cw_parts(g)[0], ALU.subtract).then_inc(s_cw, g)

                def scale_x(m, q, b, first):
                    dve.wait_ge(s_bc, m + 1)
                    if not first:
                        dve.wait_ge(s_xclo, m - 1)
                    dve.tensor_tensor(xc[q], seq(x_T, b), bank(5), ALU.mult).then_inc(s_xc, 1)

                def hidden(c, k, first):
                    dve.wait_ge(s_u, c + 1)
                    dve.wait_ge(s_s, c + 1)
                    if not first:
                        dve.wait_ge(s_hhi, c - 1)
                        dve.wait_ge(s_hlo, c - 1)
                    dve.scalar_tensor_tensor(h32[k % 2], bank(2 + k % 2), W_DOWN, gate_act[k % 2], ALU.mult, ALU.mult).then_inc(s_h, 1)

                def h_low(c, k):
                    dve.wait_ge(s_hhi, c + 1)
                    dve.tensor_tensor(h_lo[k % HSLOTS], h32[k % 2], h_hi[k % HSLOTS], ALU.subtract).then_inc(s_hlo, 1)

                begin(dve, ph["i"])
                if f == 0:
                    dve.wait_ge(s_frhi, 1)
                    dve.scalar_tensor_tensor(fr_w[1][:], fr_raw[:], W_UP, fr_w[0][:], ALU.mult, ALU.subtract).then_inc(s_frlo, 1)
                if ph["i"] == 0:
                    dve.wait_ge(s_x[0], 16)
                    dve.wait_ge(s_x[1], 16)
                prep_bn(n0, 0, LEAD)
                prep_aggr(n0, LEAD)
                prep_norm(n0, 0, LEAD)
                prep_low(n0, 0, LEAD)
                dve.wait_ge(s_con, 32)
                scale_logits(r0, LEAD)
                shift_logits(r0, LEAD)
                exp_sums(r0, LEAD)
                cw_sums(r0, LEAD)
                cw_divisor(r0, LEAD)
                cw_reciprocal(r0, LEAD)
                cw_high(r0, LEAD)
                cw_low(r0, LEAD)
                if f == 0:
                    for e in range(2):
                        for t in range(3):
                            split_weight(e, t)
                if ph["i"] == 0:
                    dve.wait_ge(s_x[2], 16 * (NB - 2))
                scale_x(m0, 0, 0, not f)
                scale_x(m0 + 1, 1, 0, not f)
                hidden(c0, 0, not f)
                hidden(c0 + 1, 1, not f)
                h_low(c0, 0)

                def body(i, prepare, finish, last):
                    c = c0 + i * CH
                    s = i + LEAD
                    rp = r0 + s - 1
                    for k in range(CH):
                        if prepare and k == 0:
                            prep_bn(n0 + s, s, 1)
                        if not (last and k + 2 >= CH):
                            hidden(c + k + 2, k + 2, False)
                        if prepare and k == 0:
                            prep_aggr(n0 + s, 1)
                        if finish and k == 1:
                            exp_sums(rp, 1)
                        if finish and k == 2:
                            cw_sums(rp, 1)
                        if finish and k == 3:
                            cw_reciprocal(rp, 1)
                        if finish and k == 4:
                            cw_low(rp, 1)
                        if not (last and k + 1 >= CH):
                            h_low(c + k + 1, k + 1)
                        if k == CH - 1:
                            dve.wait_ge(s_hfree, HSLOTS + c + CH)
                            dve.wait_ge(s_facc, a0 + f + i + 1)
                            b = i // PAIRS
                            dve.scalar_tensor_tensor(seq(facc, b), bank(4), 0.5 * W_DOWN, seq(facc, b), ALU.mult, ALU.add).then_inc(s_facc, 1)
                        if not last and k == 1:
                            scale_x(m0 + 2 * i + 2, 0, (i + 1) // PAIRS, False)
                        if prepare and k == 2:
                            prep_norm(n0 + s, s, 1)
                        if finish and k == 2:
                            cw_divisor(rp, 1)
                        if finish and k == 3:
                            cw_high(rp, 1)
                        if prepare and k == 5:
                            prep_low(n0 + s, s, 1)
                        if not last and k == 5:
                            scale_x(m0 + 2 * i + 3, 1, (i + 1) // PAIRS, False)
                        if prepare and k == 6:
                            scale_logits(r0 + s, 1)
                            shift_logits(r0 + s, 1)
                        if k < 6 and splits(f, i):
                            split_weight(2 * i + 2 + k // 3, k % 3)

                for i in range(peeled(f)):
                    body(i, True, i > 0, False)
                with dve.Fori(peeled(f), ITER - LEAD) as i:
                    body(i, True, True, False)
                body(ITER - LEAD, False, True, False)
                with dve.Fori(ITER - LEAD + 1, ITER - 1) as i:
                    body(i, False, False, False)
                body(ITER - 1, False, False, True)

            def moe(ph):
                n0, use = ph["n0"], ph["use"]
                t0, b0 = use * NS, use * NB

                def step(b, k):
                    dve.wait_ge(s_estep, b * E_STEPS + k)

                def route(b):
                    dve.wait_ge(s_elg, b + 1)
                    dve.tensor_reduce(e_max, by(bank(7, 0, SUB * E), SUB), AX_X, ALU.max).then_inc(s_estep, 1)
                    step(b, 1)
                    dve.tensor_tensor(by(e_shift, SUB), by(bank(7, 0, SUB * E), SUB), over(e_max, SUB, E), ALU.subtract).then_inc(s_esh, 1)

                def select(b):
                    dve.wait_ge(s_eexp, b + 1)
                    dve.tensor_reduce(e_sum, by(e_exp, SUB), AX_X, ALU.add).then_inc(s_estep, 1)
                    dve.scalar_tensor_tensor(e_rank, e_shift, 0.0, con_("rev_index"), ALU.is_ge, ALU.mult).then_inc(s_estep, 1)
                    step(b, 3)
                    dve.reciprocal(e_rec, e_sum).then_inc(s_estep, 1)
                    dve.tensor_reduce(e_first, by(e_rank, SUB), AX_X, ALU.max).then_inc(s_estep, 1)
                    step(b, 5)
                    dve.tensor_tensor(by(e_one, SUB), by(e_rank, SUB), over(e_first, SUB, E), ALU.is_equal).then_inc(s_esel, 1)

                def choose(b):
                    dve.wait_ge(s_esel, 2 * b + 1)
                    dve.wait_ge(s_eza, b * SUB + 2)
                    dve.wait_ge(s_ezb, b * SUB + 2)
                    dve.tensor_tensor(by(e_sel, SUB), by(e_one, SUB), over(e_rec, SUB, E), ALU.mult).then_inc(s_esel, 1)

                def weigh(t, b, k):
                    q = k % 2
                    dve.wait_ge(s_esel, 2 * b + 2)
                    dve.wait_ge(s_eyb, t + 1)
                    dve.wait_ge(s_eza, t + 3)
                    dve.wait_ge(s_ez2, t + 1)
                    for e in range(E // 2):
                        c = slice(e * C, (e + 1) * C)
                        a = k * E + E // 2 + e
                        ins = dve.scalar_tensor_tensor(e_zb[q][:, c], bank(2 * q + 1, e * C, (e + 1) * C), e_sel[:, a:a + 1],
                                                       e_za[q][:, c], ALU.mult, ALU.add)
                    ins.then_inc(s_ezb, 1)

                def add(t, s, k):
                    dve.wait_ge(s_ez1, t + 3)
                    dve.scalar_tensor_tensor(sub(x_tok, s), e_z1[k % 2], 0.5 * W_DOWN, sub(x_tok, s), ALU.mult, ALU.add).then_inc(s_eadd, 1)

                begin(dve, ph["i"])
                if ph["i"] == 0:
                    all_loaded()
                dve.wait_ge(s_ewhi, use + 1)
                low_weights(e_w, slice(0, E * C + E), LIN["experts"][0]).then_inc(s_ewlo, 1)
                dve.wait_ge(s_bhi, use + 1)
                dve.scalar_tensor_tensor(bias_w[32:33, :], bias_raw[32:33, :], W_UP, bias_w[32:33, :], ALU.mult,
                                         ALU.subtract).then_inc(s_blo, 1)
                if ph["merge"]:
                    prep_add(ph["g0"], 0, 2)
                    dve.wait_ge(s_mrg, ph["g0"] + 2)
                prep_bn(n0, 0, LEAD)
                prep_aggr(n0, LEAD)
                prep_norm(n0, 0, LEAD)
                prep_low(n0, 0, LEAD)
                route(b0)
                select(b0)
                choose(b0)

                def body(b, prep, more):
                    nx, sx = n0 + SUB * b + LEAD, SUB * b + LEAD
                    for k in range(SUB):
                        t = t0 + b * SUB + k
                        weigh(t, b0 + b, k)
                        if k == 0 and prep:
                            if ph["merge"]:
                                prep_add(ph["g0"] + b + 2, b + 2)
                                dve.wait_ge(s_mrg, ph["g0"] + b + 3)
                            prep_bn(nx, sx, SUB)
                        if k == 1 and prep:
                            prep_aggr(nx, SUB)
                        if k == 2 and more:
                            route(b0 + b + 1)
                        if k == 2 and prep:
                            prep_norm(nx, sx, SUB)
                        if k >= 1:
                            add(t - 1, b * SUB + k - 1, k - 1)
                    if more:
                        select(b0 + b + 1)
                        choose(b0 + b + 1)
                    add(t0 + b * SUB + SUB - 1, b * SUB + SUB - 1, SUB - 1)
                    if prep:
                        prep_low(nx, sx, SUB)

                with dve.Fori(0, NB - 2) as b:
                    body(b, True, True)
                body(NB - 2, False, True)
                body(NB - 1, False, False)

            def rwkv(ph):
                n0 = ph["n0"]

                def r_low(b):
                    dve.wait_ge(s_rhi, b + 1)
                    dve.scalar_tensor_tensor(rk[0][1], bank(6), W_DOWN, rk[0][0], ALU.mult, ALU.subtract).then_inc(s_rlo, 1)
                    dve.wait_ge(s_av, SUB * b)
                    dve.tensor_tensor(by(seq(r_decay, b % 2), SUB), by(bank(6), SUB),
                                      w_query.rearrange("p (o i) -> p o i", o=1).to_broadcast([P, SUB, P]), ALU.mult).then_inc(s_rdec, 1)

                def k_low(b):
                    dve.wait_ge(s_khi, b + 1)
                    dve.scalar_tensor_tensor(rk[1][1], bank(6), W_DOWN, rk[1][0], ALU.mult, ALU.subtract).then_inc(s_klo, 1)

                def keys_values(u, n):
                    dve.wait_ge(s_kv, u + 1)
                    dve.wait_ge(s_av, u + 1)
                    if n < SUB - 1:
                        dve.tensor_tensor(by(k_w[n], H), by(bank(7, 0, C), H), over(w_key, H, K), ALU.mult)
                        dve.tensor_scalar(v_tok[n], bank(7, C, 2 * C), W_DOWN, None, ALU.mult)
                    dve.tensor_tensor(by(v_by_head[n], HG), bank(7, C, 2 * C).rearrange("p (o c) -> p o c", o=1).to_broadcast([P, HG, C]),
                                      by(con_("v_head"), HG), ALU.mult).then_inc(s_vbyh, 1)

                def new_state(b, n):
                    dve.wait_ge(s_stp, (SUB - 1) * b + n + 1)
                    dve.wait_ge(s_av, SUB * b + n + 2)
                    if n == 0:
                        dve.tensor_tensor(state[1], bank(7, 2 * C, 3 * C), con_("same_head"), ALU.mult).then_inc(s_state, 1)
                        return
                    dve.tensor_tensor(st_new, bank(7, 2 * C, 3 * C), con_("same_head"), ALU.mult).then_inc(s_stm, 1)
                    dve.wait_ge(s_stm, (SUB - 2) * b + n)
                    dve.wait_ge(s_state, (SUB - 1) * b + n)
                    dve.scalar_tensor_tensor(state[n + 1], state[n], w_chunk, st_new, ALU.mult, ALU.add).then_inc(s_state, 1)

                def weigh(u, n, groups):
                    for g in groups:
                        dve.wait_ge(s_attp, 4 * SUB + NG * u + g + 1)
                        dve.wait_ge(s_av, u + 3)
                        dve.tensor_tensor(att[n % 2][g], bank(g % 2), w_intra[:, g * S:(g + 1) * S], ALU.mult).then_inc(s_attw, 1)

                def centre(b):
                    dve.wait_ge(s_gmean, b + 1)
                    dve.tensor_tensor(y_c, y8, bank(2), ALU.subtract).then_inc(s_yc, 1)

                def variance(b):
                    dve.wait_ge(s_gvarp, b + 1)
                    dve.tensor_scalar(g_var, bank(2, 0, SUB * H), GN_EPS, None, ALU.add).then_inc(s_gvar, 1)

                def group_norm(b):
                    dve.wait_ge(s_grb, b + 1)
                    dve.tensor_tensor(y_n, y_c, bank(2), ALU.mult).then_inc(s_yn, 1)

                def add(b):
                    dve.wait_ge(s_rop, b + 1)
                    dve.scalar_tensor_tensor(seq(x_tok, b), bank(2), W_DOWN, seq(x_tok, b), ALU.mult, ALU.add).then_inc(s_rout, 1)

                def prep_start(b):
                    if ph["merge"]:
                        prep_add(ph["g0"] + b, b)
                        dve.wait_ge(s_mrg, ph["g0"] + b + 1)
                    prep_bn(n0 + SUB * b, SUB * b, SUB)

                begin(dve, ph["i"])
                if ph["i"] == 0:
                    all_loaded()
                if ph["merge"]:
                    prep_add(ph["g0"], 0, 2)
                    dve.wait_ge(s_mrg, ph["g0"] + 2)
                prep_bn(n0, 0, LEAD)
                prep_aggr(n0, LEAD)
                dve.wait_ge(s_con, 96)
                dve.wait_ge(s_lin, 48)
                dve.wait_ge(s_rexp, 2)
                dve.tensor_scalar(decay_neg, w_kexp, EXP_CAP, -1.0, ALU.min, ALU.mult).then_inc(s_rset, 1)
                dve.tensor_scalar(decay_row, w_qexp[:, 0:1], EXP_CAP, -1.0, ALU.min, ALU.mult).then_inc(s_rset, 1)
                dve.tensor_scalar(mix_scale[:, 0:4], col_("mix"), W_UP, None, ALU.mult)
                dve.tensor_scalar(mix_scale[:, 4:8], col_("mix"), -W_UP, W_UP, ALU.mult, ALU.add).then_inc(s_rset, 1)
                dve.wait_ge(s_rset, 3)
                for m in range(2):
                    for j in range(4):
                        c = slice(j * C, (j + 1) * C)
                        ins = dve.tensor_scalar(mixed[m][:, c], raw_("mixed")[:, c], mix_scale[:, 4 * m + j:4 * m + j + 1], None, ALU.mult)
                    ins.then_inc(s_rset, 1)
                for m in range(2):
                    dve.wait_ge(s_rset, 4 + m)
                    dve.wait_ge(s_rwhi, 1 + m)
                    dve.tensor_tensor(mix_w[m][1], mixed[m], mix_w[m][0], ALU.subtract).then_inc(s_rwlo, 1)
                dve.wait_ge(s_rwhi, 3)
                low_weights(r_wo, slice(0, C), LIN["wo_r"][0]).then_inc(s_rwlo, 1)
                dve.wait_ge(s_rexp, 6)
                dve.tensor_scalar(w_key, w_kexp, W_DOWN, None, ALU.mult).then_inc(s_rset, 1)
                dve.tensor_scalar(w_query, w_qexp, W_DOWN, None, ALU.mult).then_inc(s_rset, 1)
                dve.tensor_tensor(by(w_later, H), by(w_exp, H), con_("later").rearrange("p (o i) -> p o i", o=1).to_broadcast([P, H, P]),
                                  ALU.mult).then_inc(s_rset, 1)
                dve.wait_ge(s_rset, 8)
                for h in range(H):
                    c = slice(h * P, (h + 1) * P)
                    a = COL["bonus"][0] + h
                    ins = dve.scalar_tensor_tensor(w_intra[:, c], ident, col_sb[:, a:a + 1], w_later[:, c], ALU.mult, ALU.add)
                ins.then_inc(s_rset, 1)
                dve.wait_ge(s_rset, 9)
                prep_norm(n0, 0, LEAD)
                prep_low(n0, 0, LEAD)
                r_low(0)
                k_low(0)
                for n in range(2):
                    keys_values(n, n)
                    new_state(0, n)
                weigh(0, 0, range(NG))

                def body(b, first, prep, more):
                    for n in range(SUB):
                        u = SUB * b + n
                        if more or n < SUB - 1:
                            weigh(u + 1, (n + 1) % SUB, (0, 1))
                        if n == 0 and not first:
                            centre(b - 1)
                        if n == 1 and prep:
                            prep_aggr(n0 + SUB * b + 2 * SUB, SUB)
                        if n == 1 and more:
                            r_low(b + 1)
                        if more or n < SUB - 1:
                            weigh(u + 1, (n + 1) % SUB, (2, 3))
                        if more or n < SUB - 2:
                            keys_values(u + 2, (n + 2) % SUB)
                        if n == 1 and more:
                            k_low(b + 1)
                        if (more or n < SUB - 2) and (n + 2) % SUB < SUB - 1:
                            new_state(b + (n + 2) // SUB, (n + 2) % SUB)
                        if n == 0 and not first:
                            variance(b - 1)
                        if n == 2 and not first:
                            group_norm(b - 1)
                        if n == 2 and prep:
                            prep_norm(n0 + SUB * b + 2 * SUB, SUB * b + 2 * SUB, SUB)
                        if n == 3 and prep:
                            prep_low(n0 + SUB * b + 2 * SUB, SUB * b + 2 * SUB, SUB)
                        if n == 3 and not first:
                            add(b - 1)
                        if n == 0 and prep:
                            prep_start(b + 2)

                body(0, True, True, True)
                with dve.Fori(1, NB - 2) as b:
                    body(b, False, True, True)
                body(NB - 2, False, False, True)
                body(NB - 1, False, False, False)
                for step in (centre, variance, group_norm, add):
                    step(NB - 1)

            def attention(ph):
                n0 = ph["n0"]

                def q_low(b):
                    dve.wait_ge(s_mqhi, b + 1)
                    dve.scalar_tensor_tensor(qk[0][1], bank(5), W_DOWN, qk[0][0], ALU.mult, ALU.subtract).then_inc(s_mqlo, 1)

                def k_low(b):
                    dve.wait_ge(s_mkhi, b + 1)
                    dve.scalar_tensor_tensor(qk[1][1], bank(6), W_DOWN, qk[1][0], ALU.mult, ALU.subtract).then_inc(s_mklo, 1)

                def v_copy(b):
                    dve.wait_ge(s_mvp, b + 1)
                    dve.wait_ge(s_pvq, USED + SUB * NG * b)
                    dve.tensor_scalar(by(v_aug, SUB * H)[:, :, 0:K], by(bank(4), SUB * H), W_DOWN, None, ALU.mult).then_inc(s_mv_in, 1)

                def max_rows(u, g):
                    dve.wait_ge(s_maug, u + 1)
                    dve.wait_ge(s_p2, KT * u + KT)
                    dst = by(q_by_head[g][STK:AUG], HG)
                    for r in range(HG):
                        ins = dve.tensor_scalar(dst[:, r], m_aug[STK:AUG], con_("row_head")[STK:AUG, r:r + 1], None, ALU.mult)
                    ins.then_inc(s_mqaug, 1)

                def maxima(u, g, tiles):
                    for t in tiles:
                        q, r, n = Q_TILES[t]
                        w = (q + 1) * P
                        if t == 0:
                            dve.wait_ge(s_mpad, u)
                        dve.wait_ge(s_p1, QT * u + t + 1)
                        dve.tensor_reduce(neg_max[:, q * HG + r:q * HG + r + n], by(bank(2 + (g + t) % 2, 0, n * w), n), AX_X, ALU.max,
                                          negate=True).then_inc(s_p1used, 1)

                def pad_maxima(u):
                    dve.wait_ge(s_p1used, QT * u + QT + 2)
                    dve.wait_ge(s_mTp, u)
                    dve.tensor_scalar(by(max_pad, SUB)[:, :, STK:AUG], by(neg_max, SUB), M_DOWN, None, ALU.mult).then_inc(s_mpad, 1)

                def normalise(u, b, g):
                    dve.wait_ge(s_ytp, u + 1)
                    cols = bank(7).rearrange("p (q r c) -> p q r c", q=SUB, r=HG)
                    dve.reciprocal(by(den_rec, SUB * HG), by(bank(7), SUB * HG)[:, :, K:K + 1]).then_inc(s_drec, 1)
                    if g == 0:
                        dve.wait_ge(s_yTp, b)
                    dve.wait_ge(s_drec, u + 1)
                    dve.tensor_tensor(y_tok.rearrange("p (q g r v) -> p q g r v", q=SUB, g=NG, r=HG)[:, :, g], cols[:, :, :, 0:K],
                                      den_rec.rearrange("p (q r o) -> p q r o", q=SUB, o=1).to_broadcast([P, SUB, HG, K]),
                                      ALU.mult).then_inc(s_ytok, 1)

                def out_low(b):
                    dve.wait_ge(s_yohi, b + 1)
                    dve.tensor_tensor(yo[1], bank(4), yo[0], ALU.subtract).then_inc(s_yolo, 1)

                def add(b):
                    dve.wait_ge(s_mop, b + 2)
                    dve.scalar_tensor_tensor(seq(x_tok, b), bank(4), W_DOWN, seq(x_tok, b), ALU.mult, ALU.add).then_inc(s_mout, 1)

                begin(dve, ph["i"])
                if ph["i"] == 0:
                    all_loaded()
                prep_bn(n0, 0, LEAD)
                prep_aggr(n0, LEAD)
                dve.wait_ge(s_con, 96)
                dve.wait_ge(s_lin, 48)
                dve.wait_ge(s_mwhi, 1)
                for g in range(NG):
                    dve.memset(k_stack[g][STK:AUG], M_UP)
                dve.memset(max_pad, 0.0).then_inc(s_mpad0, 1)
                dve.wait_ge(s_mpad0, 1)
                low_weights(m_w, slice(0, 4 * C), LIN["q"][0]).then_inc(s_mwlo, 1)
                prep_norm(n0, 0, LEAD)
                prep_low(n0, 0, LEAD, 4)
                q_low(0)
                k_low(0)
                dve.wait_ge(s_mset, 2)
                maxima(0, 0, range(QT))
                pad_maxima(0)
                max_rows(0, 0)
                maxima(1, 1, range(QT))
                pad_maxima(1)

                def body(b, first, prep, more):
                    nx, sx = n0 + SUB * b + 2 * SUB, SUB * b + 2 * SUB
                    for g in range(NG):
                        u = NG * b + g
                        if g == 2 and prep:
                            prep_norm(nx, sx, SUB)
                        if g == 3 and prep:
                            prep_low(nx, sx, SUB, 4)
                        for t in range(QT):
                            if more or g < NG - 2:
                                maxima(u + 2, (g + 2) % NG, [t])
                            if t == 0 and g == 1 and prep:
                                prep_aggr(nx, SUB)
                            if t == KT_END[0] + 1 and (more or g < NG - 1):
                                max_rows(u + 1, (g + 1) % NG)
                            if t == KT_END[0] - 1 and g == 0 and more:
                                q_low(b + 1)
                            if t == KT_END[0] - 1 and g == 1 and not first:
                                out_low(b - 1)
                            if t == KT_END[1] - 1 and g == 0 and more:
                                k_low(b + 1)
                        if more or g < NG - 2:
                            pad_maxima(u + 2)
                        if g == 1 and not first:
                            add(b - 1)
                        if not (first and g == 0):
                            normalise(u - 1, b - (g == 0), (g - 1) % NG)
                        if g == 0:
                            v_copy(b)
                        if g == 0 and prep:
                            prep_bn(nx, sx, SUB)

                body(0, True, True, True)
                with dve.Fori(1, NB - 2) as b:
                    body(b, False, True, True)
                body(NB - 2, False, False, True)
                body(NB - 1, False, False, False)
                normalise(UNITS - 1, NB - 1, NG - 1)
                out_low(NB - 1)
                add(NB - 1)

            for ph in plan:
                dict(F=ffn, E=moe, R=rwkv, M=attention)[ph["kind"]](ph)

        @block.tensor
        def _(pe):
            def prep_merge(m, n, k=1):
                pe.wait_ge(s_mrg_in, m + k)
                pe.wait_ge(s_xlo, n)
                for q in range(k * SUB):
                    ins = pe.transpose(prep_psum(k * SUB)[:, q * P:(q + 1) * P], merge_in[:, q * P:(q + 1) * P], ident)
                ins.then_inc(s_mrg_ps, k)

            def prep_transpose(n, g, at=6):
                pe.wait_ge(s_xn, n + g)
                pe.wait_ge(s_xlo, n)
                for q in range(g):
                    ins = pe.transpose(prep_psum(g, at)[:, q * P:(q + 1) * P], x_norm[:, q * P:(q + 1) * P], ident)
                ins.then_inc(s_xT, g)

            def three(dst, lhs, rhs, first=True, last=True):
                pe.matmul(dst, lhs[0], rhs[0], start=first, stop=False)
                pe.matmul(dst, lhs[0], rhs[1], start=False, stop=False)
                return pe.matmul(dst, lhs[1], rhs[0], start=False, stop=last)

            def ffn(ph):
                f, n0 = ph["use"], ph["n0"]
                r0, m0, c0, a0 = f * NS, f * NB * E, f * ITER * CH, f * ITER

                def logits(n, s, nx, g):
                    pe.wait_ge(s_xlo, nx + g)
                    pe.wait_ge(s_cwT, n)
                    for q in range(g):
                        ins = three(bank(7, q * 2 * E, (q + 1) * 2 * E), [xsub(t, s + q) for t in (x_hi, x_lo)], [w[:] for w in fr_w])
                    ins.then_inc(s_lg, g)

                def transpose_cw(n, g):
                    pe.wait_ge(s_cw, 2 * (n + g))
                    for q in range(g):
                        ins = pe.transpose(cwT_psum(g)[:, q * P:(q + 1) * P], cw16[:, q * 2 * E:(q + 1) * 2 * E], ident16)
                    ins.then_inc(s_cwTp, g)

                def broadcast(m, e, b):
                    pe.wait_ge(s_xc, m)
                    pe.matmul(bank(5), sub(half_("pick_expert"), e), seq(cw_T, b), start=True, stop=True).then_inc(s_bc, 1)

                def cols(w, e, k):
                    return [t[:, ds(e * F + (k % FC) * P, P)] for t in w]

                def gate_up(c, k, m, e, b, first):
                    if not first:
                        pe.wait_ge(s_s, c - 1)
                    three(bank(k % 2), cols(ffn_g, e, k), [xseq(t, b) for t in (x_hi, x_lo)]).then_inc(s_g, 1)
                    if not first:
                        pe.wait_ge(s_h, c - 1)
                    q = (k // FC) % 2
                    if k % FC == 0:
                        pe.wait_ge(s_xclo, m + 1)
                    three(bank(2 + k % 2), cols(ffn_u, e, k), [xc_hi[q], xc_lo[q]]).then_inc(s_u, 1)

                def down(c, k, e, added):
                    pe.wait_ge(s_hlo, c + 1)
                    if k == 0:
                        pe.wait_ge(s_facc, added)
                    r = k % HSLOTS
                    three(bank(4), cols(ffn_d, e, k), [h_hi[r], h_lo[r]], k == 0, k == CH - 1).then_inc(s_hfree, 1)

                begin(pe, ph["i"])
                if f == 0:
                    pe.wait_ge(s_con, 32)
                    pe.wait_ge(s_frlo, 1)
                prep_transpose(n0, LEAD)
                logits(r0, 0, n0, LEAD)
                transpose_cw(r0, LEAD)
                pe.wait_ge(s_cwT, r0 + LEAD)
                broadcast(m0, 0, 0)
                broadcast(m0 + 1, 1, 0)
                pe.wait_ge(s_wlo, 3 * 2)
                gate_up(c0, 0, m0, 0, 0, not f)
                gate_up(c0 + 1, 1, m0, 0, 0, not f)

                def body(i, prepare, finish, last):
                    c = c0 + i * CH
                    s = i + LEAD
                    pair, b = i % PAIRS, i // PAIRS
                    npair, nb = (i + 1) % PAIRS, (i + 1) // PAIRS
                    for k in range(CH):
                        kk = k + 2
                        if kk == FC and splits(f, i):
                            pe.wait_ge(s_wlo, 3 * (2 * i + 2))
                        if kk < CH:
                            gate_up(c + kk, kk, m0 + 2 * i + kk // FC, 2 * pair + kk // FC, b, False)
                        elif not last:
                            if kk == CH and splits(f, i):
                                pe.wait_ge(s_wlo, 3 * (2 * i + 3 + (i == PAIRS - 2)))
                            if kk == CH:
                                pe.wait_ge(s_xlo, n0 + nb * SUB + SUB)
                            gate_up(c + kk, kk, m0 + 2 * i + kk // FC, 2 * npair, nb, False)
                        if not last and k == 1:
                            pe.wait_ge(s_cwT, r0 + nb * SUB + SUB)
                            broadcast(m0 + 2 * i + 2, 2 * npair, nb)
                        if not last and k == 5:
                            broadcast(m0 + 2 * i + 3, 2 * npair + 1, nb)
                        if finish and k == 5:
                            transpose_cw(r0 + s - 1, 1)
                        down(c + k, k, 2 * pair + k // FC, a0 + f + i + 1)
                        if prepare and k == 6:
                            logits(r0 + s, s, n0 + s, 1)
                        if prepare and k == 3:
                            prep_transpose(n0 + s, 1)

                for i in range(peeled(f)):
                    body(i, True, i > 0, False)
                with pe.Fori(peeled(f), ITER - LEAD) as i:
                    body(i, True, True, False)
                body(ITER - LEAD, False, True, False)
                with pe.Fori(ITER - LEAD + 1, ITER - 1) as i:
                    body(i, False, False, False)
                body(ITER - 1, False, False, True)

            def moe(ph):
                n0, use = ph["n0"], ph["use"]
                t0, b0 = use * NS, use * NB
                ones = half_("ones")

                def parts(s):
                    return [xsub(t, s) for t in (x_hi, x_lo)]

                def ecols(a, b):
                    return [w[:, a:b] for w in e_w]

                def logits(b, s, n):
                    pe.wait_ge(s_xlo, n)
                    pe.wait_ge(s_esh, b)
                    for q in range(SUB):
                        dst = bank(7, q * E, (q + 1) * E)
                        pe.matmul(dst, ones, bias_w[:, E * C:E * C + E], start=True, stop=False)
                        ins = three(dst, parts(s + q), ecols(E * C, E * C + E), False)
                    ins.then_inc(s_elg, 1)

                def products(t, s, k):
                    for half_of, done, used in ((0, s_eya, s_eza), (1, s_eyb, s_ezb)):
                        pe.wait_ge(used, t + 1)
                        a = half_of * E // 2 * C
                        dst = bank(2 * (k % 2) + half_of)
                        pe.matmul(dst, ones, bias_w[:, a:a + BANK], start=True, stop=False)
                        three(dst, parts(s), ecols(a, a + BANK), False).then_inc(done, 1)

                begin(pe, ph["i"])
                pe.wait_ge(s_con, 96)
                if ph["merge"]:
                    prep_merge(ph["g0"], n0, 2)
                prep_transpose(n0, LEAD)
                pe.wait_ge(s_ewlo, use + 1)
                pe.wait_ge(s_blo, use + 1)
                logits(b0, 0, n0 + LEAD)

                def body(b, prep, more):
                    nx, sx = n0 + SUB * b + LEAD, SUB * b + LEAD
                    for k in range(SUB):
                        products(t0 + b * SUB + k, b * SUB + k, k)
                        if k == 1 and more:
                            logits(b0 + b + 1, sx - SUB, nx)
                        if k == 0 and prep and ph["merge"]:
                            prep_merge(ph["g0"] + b + 2, nx)
                        if k == 3 and prep:
                            prep_transpose(nx, SUB)

                with pe.Fori(0, NB - 2) as b:
                    body(b, True, True)
                body(NB - 2, False, True)
                body(NB - 1, False, False)

            pe.sem_inc(s_hfree, HSLOTS)
            for s in (s_eza, s_ezb, s_ez2, s_ez1, s_eadd):
                pe.sem_inc(s, 2)
            for s in (s_rout, s_mop):
                pe.sem_inc(s, 1)
            def rwkv(ph):
                n0 = ph["n0"]

                def project(dst, j, rhs):
                    w = [[t[:, j * C:(j + 1) * C] for t in mix_w[m]] for m in range(2)]
                    three(dst, w[0], rhs[0], True, False)
                    return three(dst, w[1], rhs[1], False, True)

                def both(b):
                    return [[xseq(t, b, m) for t in (x_hi, x_lo)] for m in range(2)]

                def r_proj(b):
                    pe.wait_ge(s_xlo, n0 + SUB * b + SUB)
                    pe.wait_ge(s_klo, b)
                    project(bank(6), 0, both(b)).then_inc(s_rp, 1)

                def k_proj(b):
                    pe.wait_ge(s_rdec, b + 1)
                    project(bank(6), 1, both(b)).then_inc(s_kp, 1)

                def stacks(u, b, n):
                    for j, dst, names, ready, used, done in ((0, bank(5), ("q_hi", "q_lo"), s_rlo, s_rbyh, s_rst),
                                                             (1, bank(3), ("k_hi", "k_lo"), s_klo, s_kstk, s_kst)):
                        pe.wait_ge(ready, b + 1)
                        pe.wait_ge(used, u)
                        for g in range(NG):
                            for h in range(2):
                                ins = pe.matmul(dst[0:STK, g * P:(g + 1) * P], pick(names[h], g), rk[j][h][:, n * P:(n + 1) * P],
                                                start=h == 0, stop=h == 1)
                        ins.then_inc(done, 1)

                def keys_values(u, b, n):
                    pe.wait_ge(s_vbyh, u)
                    pe.wait_ge(s_state, (SUB - 1) * b + n)
                    w = [[t[:, C:3 * C] for t in mix_w[m]] for m in range(2)]
                    chunk = [[xchunk(t, b, n, m) for t in (x_hi, x_lo)] for m in range(2)]
                    three(bank(7, 0, 2 * C), chunk[0], w[0], True, False)
                    three(bank(7, 0, 2 * C), chunk[1], w[1], False, True).then_inc(s_kv, 1)

                def state_product(u, b, n):
                    pe.wait_ge(s_vbyh, u + 1)
                    pe.wait_ge(s_state, (SUB - 1) * b + n)
                    pe.matmul(bank(7, 2 * C, 3 * C), k_w[n], v_tok[n], start=True, stop=True).then_inc(s_stp, 1)

                def scores(u, n, groups):
                    pe.wait_ge(s_rbyh, u + 1)
                    pe.wait_ge(s_kstk, u + 1)
                    for g in groups:
                        pe.wait_ge(s_attw, NG * u + g + 1)
                        pe.matmul(bank(g % 2), k_stk[n][0:STK, g * P:(g + 1) * P], r_st[n][0:STK, g * S:(g + 1) * S],
                                  start=True, stop=True).then_inc(s_attp, 1)

                def outputs(u, b, n):
                    if n == 0:
                        pe.wait_ge(s_y8, b)
                    else:
                        pe.wait_ge(s_state, (SUB - 1) * b + n)
                        pe.wait_ge(s_rdec, b + 1)
                        pe.matmul(bank(4, n * P, (n + 1) * P), state[n], r_decay[:, ds((b % 2) * S + n * P, P)], start=True, stop=False)
                    pe.wait_ge(s_attw, 2 + NG * u + NG)
                    pe.wait_ge(s_vbyh, u + 1)
                    for r in range(HG):
                        for g in range(NG):
                            c = slice(r * C + g * GC, r * C + (g + 1) * GC)
                            ins = pe.matmul(bank(4, n * P, (n + 1) * P)[g * GC:(g + 1) * GC], v_by_head[n][:, c],
                                            att[n % 2][g][:, r * P:(r + 1) * P], start=n == 0 and r == 0, stop=r == HG - 1)
                    ins.then_inc(s_av, 1)

                def gn_mean(b):
                    pe.wait_ge(s_y8, b + 1)
                    pe.wait_ge(s_rout, b + 1)
                    pe.matmul(bank(2), con_("head_mean"), y8, start=True, stop=True).then_inc(s_gmean, 1)

                def gn_var(b):
                    pe.wait_ge(s_ysq, b + 1)
                    for n in range(SUB):
                        ins = pe.matmul(bank(2, n * H, (n + 1) * H), y_sq[:, n * P:(n + 1) * P], con_("head_mean16"), start=True, stop=True)
                    ins.then_inc(s_gvarp, 1)

                def g_proj(b):
                    pe.wait_ge(s_gvar, b + 1)
                    project(bank(2), 3, both(b)).then_inc(s_gp, 1)

                def gn_rstd(b):
                    pe.wait_ge(s_sg, b + 1)
                    pe.wait_ge(s_gwide, b + 1)
                    for n in range(SUB):
                        ins = pe.matmul(bank(2, n * P, (n + 1) * P), g_wide[:, n * P:(n + 1) * P], ident, start=True, stop=True)
                    ins.then_inc(s_grb, 1)

                def out_proj(b):
                    pe.wait_ge(s_yglo, b + 1)
                    for n in range(SUB):
                        ins = three(bank(2, n * P, (n + 1) * P), [t[:, n * P:(n + 1) * P] for t in y_parts], r_wo)
                    ins.then_inc(s_rop, 1)

                begin(pe, ph["i"])
                pe.sem_inc(s_attw, 2)
                pe.sem_inc(s_av, SUB)
                pe.sem_inc(s_attp, NG * SUB)
                pe.wait_ge(s_con, 96)
                if ph["merge"]:
                    prep_merge(ph["g0"], n0, 2)
                prep_transpose(n0, LEAD)
                pe.wait_ge(s_xlo, n0 + 2 * SUB)
                pe.wait_ge(s_rwlo, 3)
                r_proj(0)
                k_proj(0)
                for n in range(2):
                    stacks(n, 0, n)
                    keys_values(n, 0, n)
                    state_product(n, 0, n)
                scores(0, 0, range(NG))

                def body(b, first, prep, more):
                    for n in range(SUB):
                        u = SUB * b + n
                        b2, n2 = b + (n + 2) // SUB, (n + 2) % SUB
                        ahead = more or n < SUB - 2
                        if more or n < SUB - 1:
                            scores(u + 1, (n + 1) % SUB, (0, 1))
                        if n == 0 and prep and ph["merge"]:
                            pe.wait_ge(s_klo, b + 1)
                            prep_merge(ph["g0"] + b + 2, n0 + SUB * b + 2 * SUB)
                        if ahead:
                            stacks(u + 2, b2, n2)
                        if n == 0 and not first:
                            gn_mean(b - 1)
                        if n == 1 and more:
                            if prep and ph["merge"]:
                                pe.wait_ge(s_mrg, ph["g0"] + b + 3)
                            r_proj(b + 1)
                        if n == 3 and prep:
                            pe.wait_ge(s_klo, b + 2)
                            prep_transpose(n0 + SUB * b + 2 * SUB, SUB)
                        if more or n < SUB - 1:
                            scores(u + 1, (n + 1) % SUB, (2, 3))
                        if ahead:
                            keys_values(u + 2, b2, n2)
                        if n == 0 and not first:
                            gn_var(b - 1)
                        if n == 1 and not first:
                            g_proj(b - 1)
                        if n == 1 and more:
                            k_proj(b + 1)
                        outputs(u, b, n)
                        if ahead and n2 < SUB - 1:
                            state_product(u + 2, b2, n2)
                        if n == 2 and not first:
                            gn_rstd(b - 1)
                        if n == 3 and not first:
                            out_proj(b - 1)

                body(0, True, True, True)
                with pe.Fori(1, NB - 2) as b:
                    body(b, False, True, True)
                body(NB - 2, False, False, True)
                body(NB - 1, False, False, False)
                for step in (gn_mean, gn_var, g_proj, gn_rstd, out_proj):
                    step(NB - 1)

            def attention(ph):
                n0 = ph["n0"]
                wq, wk, wv, wo = [[w[:, j * C:(j + 1) * C] for w in m_w] for j in range(4)]
                ident_b, keys_after, queries_before = [big_sb[:, a:a + P] for a, _ in BIG.values()]

                def parts(b):
                    return [xseq(t, b) for t in (x_hi, x_lo)]

                def q_proj(b):
                    pe.wait_ge(s_xlo, n0 + SUB * b + SUB)
                    pe.wait_ge(s_mkst, NG * b)
                    three(bank(5), wq, parts(b)).then_inc(s_mqp, 1)

                def k_proj(b, first):
                    if not first:
                        pe.wait_ge(s_mqst, NG * b)
                        pe.wait_ge(s_maug, NG * b - 2)
                    three(bank(6), wk, parts(b)).then_inc(s_mkp, 1)

                def v_proj(b):
                    for n in range(SUB):
                        ins = three(bank(4, n * P, (n + 1) * P), [xchunk(t, b, n, 0) for t in (x_hi, x_lo)], wv)
                    ins.then_inc(s_mvp, 1)

                def stacks(u, b, g, first):
                    pe.wait_ge(s_mklo, b + 1)
                    pe.wait_ge(s_mkst, u)
                    for h, name in enumerate(("k_hi", "k_lo")):
                        ins = pe.matmul(bank(5)[0:STK], pick(name, g), qk[1][h], start=h == 0, stop=h == 1)
                    ins.then_inc(s_mks, 1)
                    pe.wait_ge(s_mqst, u)
                    if not first:
                        pe.wait_ge(s_maug, u - 2)
                    for h, name in enumerate(("q_hi", "q_lo")):
                        ins = pe.matmul(bank(6)[0:STK], pick(name, g), qk[0][h], start=h == 0, stop=h == 1)
                    ins.then_inc(s_mqs, 1)

                def by_query(u, g, t):
                    q, r0, n = Q_TILES[t]
                    w = (q + 1) * P
                    if t == 0:
                        pe.wait_ge(s_mqh, u + 3)
                        pe.wait_ge(s_mkst, u + 1)
                    pe.wait_ge(s_p1used, QT * u + t + 1)
                    for r in range(r0, r0 + n):
                        dst = bank(2 + (g + t) % 2, (r - r0) * w, (r - r0 + 1) * w)
                        pe.matmul(dst, q_by_head[g][0:STK, r * S + q * P:r * S + (q + 1) * P], k_stack[g][0:STK, 0:w], start=True, stop=False)
                        ins = pe.matmul(dst[:, w - P:w], ident_b, keys_after, start=False, stop=True)
                    ins.then_inc(s_p1, 1)

                def max_rows(u, stacked):
                    pe.wait_ge(s_mpad, u + 1)
                    pe.wait_ge(s_mqst, stacked)
                    for q in range(SUB):
                        ins = pe.matmul(bank(6, q * P, (q + 1) * P), max_pad[:, q * P:(q + 1) * P], ident16, start=True, stop=True)
                    ins.then_inc(s_mTp, 1)

                def by_key(u, g, t):
                    j, r0, n = K_TILES[t]
                    w = S - j * P
                    if t == 0:
                        pe.wait_ge(s_mqaug, u + 1)
                    pe.wait_ge(s_p2exp, KT * u + t + 1)
                    for r in range(r0, r0 + n):
                        dst = bank((g + t) % 2, (r - r0) * w, (r - r0 + 1) * w)
                        pe.matmul(dst, k_stack[g][0:AUG, j * P:(j + 1) * P], q_by_head[g][0:AUG, r * S + j * P:(r + 1) * S],
                                  start=True, stop=False)
                        ins = pe.matmul(dst[:, 0:P], ident_b, queries_before, start=False, stop=True)
                    ins.then_inc(s_p2, 1)

                def weighted_values(u, b, g, j):
                    w = S - j * P
                    if j == 0:
                        pe.wait_ge(s_ytok, u)
                        pe.wait_ge(s_mv_in, b + 1)
                    pe.wait_ge(s_p2exp, KT * u + KT_END[j] + 2)
                    for r in range(HG):
                        a = (j * H + g * HG + r) * 32
                        ins = pe.matmul(bank(7, j * P, S)[r * 32:(r + 1) * 32], v_aug[:, a:a + 32], probs[j][:, r * w:(r + 1) * w],
                                        start=j == 0, stop=j == SUB - 1)
                    ins.then_inc(s_pvq, 1)

                def transpose_values(u):
                    pe.wait_ge(s_yraw, u + 1)
                    for q in range(SUB):
                        ins = pe.transpose(bank(7, q * P, (q + 1) * P), y_raw[:, q * P:(q + 1) * P], ident)
                    ins.then_inc(s_ytp, 1)

                def transpose_out(b):
                    pe.wait_ge(s_ytok, NG * b + NG)
                    for n in range(SUB):
                        ins = pe.transpose(bank(4, n * P, (n + 1) * P), y_tok[:, n * P:(n + 1) * P], ident)
                    ins.then_inc(s_yTp, 1)

                def out_proj(b):
                    pe.wait_ge(s_yolo, b + 1)
                    for n in range(SUB):
                        ins = three(bank(4, n * P, (n + 1) * P), [t[:, n * P:(n + 1) * P] for t in yo], wo)
                    ins.then_inc(s_mop, 1)

                begin(pe, ph["i"])
                for s, n in ((s_p1used, 2), (s_p2exp, 2), (s_mqh, 2), (s_p2, SCORED), (s_pvq, USED)):
                    pe.sem_inc(s, n)
                pe.wait_ge(s_con, 96)
                prep_transpose(n0, LEAD, 4)
                pe.wait_ge(s_mwlo, 1)
                pe.wait_ge(s_xlo, n0 + 2 * SUB)
                q_proj(0)
                k_proj(0, True)
                for u in range(NG):
                    stacks(u, 0, u, True)
                for t in range(QT):
                    by_query(0, 0, t)
                max_rows(0, NG)
                for t in range(QT):
                    by_query(1, 1, t)

                def body(b, first, prep, more):
                    for g in range(NG):
                        u = NG * b + g
                        before = (u - 1, b - (g == 0), (g - 1) % NG)
                        if g == 0 and more:
                            q_proj(b + 1)
                        if g == 1 and not first:
                            pe.wait_ge(s_mv_in, b + 1)
                            transpose_out(b - 1)
                        for t in range(KT):
                            if not (first and g == 0):
                                if t == 0:
                                    weighted_values(*before, 0)
                                if t == KT_END[0]:
                                    weighted_values(*before, 1)
                                if t == KT_END[1]:
                                    weighted_values(*before, 2)
                                    weighted_values(*before, 3)
                            by_key(u, g, t)
                            if more or g < NG - 2:
                                by_query(u + 2, (g + 2) % NG, t)
                            if t == KT_END[0] - 1 and (more or g < NG - 1):
                                max_rows(u + 1, u + 4 if more else UNITS)
                            if t == KT_END[1] - 1 and g == 0 and more:
                                k_proj(b + 1, False)
                        if g == 1 and not first:
                            out_proj(b - 1)
                        if g == 2 and prep:
                            if first:
                                pe.wait_ge(s_mv_in, b + 1)
                            else:
                                pe.wait_ge(s_mout, b)
                            prep_transpose(n0 + SUB * b + 2 * SUB, SUB, 4)
                        if more:
                            stacks(u + NG, b + 1, g, False)
                        if not (first and g == 0):
                            transpose_values(u - 1)
                        if g == 0:
                            pe.wait_ge(s_xlo, n0 + SUB * b + (2 * SUB if more else SUB))
                            v_proj(b)

                body(0, True, True, True)
                with pe.Fori(1, NB - 2) as b:
                    body(b, False, True, True)
                body(NB - 2, False, False, True)
                body(NB - 1, False, False, False)
                for j in range(SUB):
                    weighted_values(UNITS - 1, NB - 1, NG - 1, j)
                transpose_values(UNITS - 1)
                transpose_out(NB - 1)
                out_proj(NB - 1)

            for ph in plan:
                dict(F=ffn, E=moe, R=rwkv, M=attention)[ph["kind"]](ph)


def shape_constants():
    c = np.arange(P)
    con = {n: np.zeros((P, w), np.float32) for n, (_, w) in CON.items()}
    con["ident"][:] = np.eye(P)
    same = (c[:, None] // K == c[None, :] // K)
    con["head_mean"][:] = same / K
    con["head_mean16"][c, c // K] = 1.0 / K
    con["same_head"][:] = same
    con["rev_index"][:] = np.tile(E - np.arange(E), SUB)
    con["logit_scale"][:] = np.tile(np.repeat([W_DOWN, W_DOWN / GATE_TEMP], E), LEAD)
    rows = np.arange(AUG)
    head = np.where(rows < STK, rows % GC // K, rows - STK)
    con["row_head"][rows, head] = 1.0
    con["v_head"][:] = (W_DOWN * (c[None, :] % GC // K == np.arange(HG)[:, None])).reshape(1, HG * C)
    con["distance"][:] = np.maximum(c[None, :] - c[:, None] - 1, 0)
    con["later"][:] = c[None, :] > c[:, None]
    con["position"][:] = c[None, :]
    con["to_end"][:, 0] = P - 1 - c
    half = {n: np.zeros((P, w), np.float16) for n, (_, w) in HALF.items()}
    half["ident"][:] = np.eye(P)
    for e in range(E):
        half["pick_expert"][[e, E + e], e * P:(e + 1) * P] = 1.0
    half["ones"][:] = 1.0
    for name, parts in (("k_hi", (0, 2)), ("k_lo", (1,)), ("q_hi", (0, 1)), ("q_lo", (2,))):
        for g in range(NG):
            for part in parts:
                half[name][g * GC + np.arange(GC), g * STK + part * GC + np.arange(GC)] = 1.0
    after = np.where(c[None, :] > c[:, None], NEG_BIG, 0.0)
    big = np.concatenate([np.eye(P), after, after.T], axis=1)
    return (np.concatenate([con[n] for n in CON], axis=1), np.concatenate([half[n] for n in HALF], axis=1), big.astype(mybir.dt.np(BF16)))


def lay_out(v):
    def rows(a):
        return np.broadcast_to(a.reshape(1, -1), (P, a.size))

    con, half, big = shape_constants()
    x = v["L0_attn_xq"].reshape(NS, P, C).transpose(1, 0, 2).reshape(P, NS * C)
    down = v["L0_ffn_w_down"].reshape(E, FC, P, C).transpose(0, 2, 1, 3).reshape(E, P, F)
    qkv = v["L1_attn_w_qkv"].reshape(3, C, C)
    lin = dict(mixed=np.concatenate([v["L0_attn_W_" + n].T for n in "rkvg"], axis=1), wo_r=v["L0_attn_W_o"].T,
               experts=v["L1_ffn_expert_w"].transpose(2, 0, 1).reshape(C, E * C), router=v["L1_ffn_router_w"].T,
               q=qkv[0].T, k=qkv[1].T, v=qkv[2].T, wo_m=v["L1_attn_w_o"].T)
    col = dict(mix=np.stack([v["L0_attn_time_mix_" + n].reshape(C) for n in "rkvg"], axis=1),
               decay_row=np.repeat(v["L0_attn_time_decay"], K)[:, None], ln_w=v["L0_attn_ln_w"][:, None], ln_b=v["L0_attn_ln_b"][:, None],
               decay=rows(v["L0_attn_time_decay"]), bonus=rows(v["L0_attn_time_faaaa"]))
    bias = np.concatenate([v["L1_ffn_expert_b"].reshape(E * C), v["L1_ffn_router_b"]])
    return dict(x=x, ffn_router=np.concatenate([v["L0_ffn_w_router"], v["L0_ffn_w_gating"]], axis=1),
                ffn_w=np.concatenate([v["L0_ffn_w_gate"], v["L0_ffn_w_up"], down], axis=2),
                lin=np.concatenate([lin[n] for n in LIN], axis=1), col=np.concatenate([col[n] for n in COL], axis=1),
                bias=np.stack([bias, bias]), con=con, half=half, big=big)


def kernel(**inputs):
    import concourse.bacc as bacc
    from concourse.bass_utils import run_bass_kernel_spmd

    nc = bacc.Bacc("TRN2", target_bir_lowering=False, num_devices=1)
    arrays, args = {}, []
    for name, a in lay_out({n: np.asarray(a) for n, a in inputs.items()}).items():
        arrays[f"in_{name}_dram"] = np.ascontiguousarray(a)
        args.append(nc.dram_tensor(f"in_{name}_dram", a.shape, mybir.dt.from_np(a.dtype), kind="ExternalInput").ap())
    args.append(nc.dram_tensor("out_dram", (P, NS * C), F32, kind="ExternalOutput").ap())
    build(nc, *args)
    r = run_bass_kernel_spmd(nc, [arrays], core_ids=[0])
    return r.results[0]["out_dram"].reshape(P, NS, C).transpose(1, 0, 2).reshape(NB, S, C)
```

```python
from contextlib import ExitStack

import concourse.bass as bass
import numpy as np
from concourse import mybir

F32 = mybir.dt.float32
F16 = mybir.dt.float16
BF16 = mybir.dt.bfloat16
ALU = mybir.AluOpType
ACT = mybir.ActivationFunctionType
AX_X = mybir.AxisListType.X
ds = bass.ds

P = 128
BANK = 512
LN_EPS = 1e-5
GN_EPS = 1e-5
HEAD_DIV = 8.0
GATE_TEMP = 0.1
W_UP = 2.0 ** 6
W_DOWN = 1.0 / W_UP
M_UP = 2.0 ** 12
M_DOWN = 1.0 / M_UP
NEG_BIG = -1e30
EXP_CAP = 1e30

NB, S, C = 8, 512, 128
SUB = S // P
NS = NB * SUB
E, F = 8, 512
H, K = 16, 8
NG, HG = 4, 4
GC = HG * K
HR = P // HG
MAX_ROW = 3 * K
FC = F // P
PAIRS = E // 2
ITER = NB * PAIRS
CH = 2 * FC
HSLOTS = 4
LEAD = 2 * SUB
XW = S + 8
R_SCALE = float(1.0 / np.sqrt(np.float32(K)))
PHASES = ("F", "R", "F", "E", "M", "E")


def columns(parts):
    at, out = 0, {}
    for name, n in parts:
        out[name] = (at, n)
        at += n
    return out, at


LIN, LIN_N = columns([("mixed", 4 * C), ("wo_r", C), ("experts", E * C), ("router", E), ("q", C), ("k", C), ("v", C), ("wo_m", C)])
COL, COL_N = columns([("mix", 4), ("decay_row", 1), ("ln_w", 1), ("ln_b", 1), ("decay", H), ("bonus", H)])
CON, CON_N = columns([("ident", P), ("logit_scale", LEAD * 2 * E), ("distance", P), ("later", P), ("position", P), ("to_end", 1),
                      ("head_mean", P), ("head_mean16", H), ("same_head", P), ("rev_index", SUB * E), ("row_head", HG), ("max_row", 1),
                      ("v_head", HG * C)])
HALF, HALF_N = columns([("ident", P), ("pick_expert", E * P), ("ones", P), ("k_hi", NG * P), ("k_lo", NG * P),
                        ("q_hi", NG * P), ("q_lo", NG * P)])
BIG, BIG_N = columns([("ident", P), ("keys_after", P), ("queries_before", P)])


def build(nc, x, ffn_router, ffn_w, lin, col, bias, con, half, big, out):
    with ExitStack() as ctx:
        def sb(name, cols, dt=F32):
            return ctx.enter_context(nc.sbuf_tensor(name, [P, cols], dt))

        def sem(name):
            return ctx.enter_context(nc.semaphore(name))

        psum = ctx.enter_context(nc.psum_tensor("psum", [P, 8 * BANK], F32))

        def bank(i, a=0, b=BANK):
            return psum[:, i * BANK + a:i * BANK + b]

        x_tok = sb("x_tok", NS * C)
        facc = sb("facc", NB * S)
        x_hi = sb("x_hi", NB * XW, F16)
        x_lo = sb("x_lo", NB * XW, F16)
        con_sb = sb("con_sb", CON_N)
        half_sb = sb("half_sb", HALF_N, F16)
        big_sb = sb("big_sb", BIG_N, BF16)
        col_sb = sb("col_sb", COL_N)
        neg_half = sb("neg_half", SUB * H)
        e_const = sb("e_const", 2 * E)
        raw = sb("raw", LIN_N + E * C + E)
        bias_raw = raw[:, LIN_N:LIN_N + E * C + E]
        ffn_g = [sb(f"ffn_gate_{h}", E * F, F16) for h in ("hi", "lo")]
        ffn_u = [sb(f"ffn_up_{h}", E * F, F16) for h in ("hi", "lo")]
        ffn_d = [sb(f"ffn_down_{h}", E * F, F16) for h in ("hi", "lo")]
        fr_w = [sb(f"fr_{h}", 2 * E, F16) for h in ("hi", "lo")]
        fr_raw = sb("fr_raw", 2 * E)
        ln_stat = sb("ln_stat", LEAD * 6)
        ln_mv = sb("ln_mv", LEAD * 2)
        ln_var = sb("ln_var", LEAD)
        ln_rstd = sb("ln_rstd", LEAD)
        x_norm = sb("x_norm", LEAD * P)
        merge_in = x_norm

        SCRATCH = 20768
        scratch = sb("scratch", SCRATCH)
        place, limit = [0], [SCRATCH]

        def carve(cols, dt=F32):
            n = cols if dt == F32 else (cols + 1) // 2
            t = scratch[:, place[0]:place[0] + n]
            place[0] += n
            assert place[0] <= limit[0], (place[0], limit[0])
            return t if dt == F32 else t.bitcast(dt)

        def carve_from(a, b=SCRATCH):
            place[0], limit[0] = a, b

        x_T = carve(NB * S)
        cw_T = carve(NB * S, F16)
        lg = carve(LEAD * 2 * E)
        lg_max = carve(LEAD * 2)
        lg_shift = carve(LEAD * 2 * E)
        lg_exp = carve(LEAD * 2 * E)
        sm_sum = carve(LEAD * 2)
        cw_num = carve(LEAD * E)
        cw_sum = carve(LEAD)
        cw_eps = carve(LEAD)
        cw_den = carve(LEAD)
        cw_rec = carve(LEAD)
        cw_out = carve(LEAD * E)
        cw16 = carve(LEAD * 2 * E, F16)
        xc = [carve(S) for _ in range(2)]
        xc_hi = [carve(S, F16) for _ in range(2)]
        xc_lo = [carve(S, F16) for _ in range(2)]
        gate_act = [carve(S) for _ in range(2)]
        h32 = [carve(S) for _ in range(2)]
        h_hi = [carve(S, F16) for _ in range(HSLOTS)]
        h_lo = [carve(S, F16) for _ in range(HSLOTS)]

        ffn_end = place[0]

        mix_scale = carve(8)
        mix_w = [[carve(4 * C, F16) for _ in range(2)] for _ in range(2)]
        r_wo = [carve(C, F16) for _ in range(2)]
        decay_neg = carve(H)
        decay_row = carve(1)
        w_intra = carve(H * P)
        w_query = carve(P)
        w_chunk = carve(1)
        w_key = carve(H)
        rwkv_set_end = place[0]
        mixed = [carve(4 * C) for _ in range(2)]

        carve_from(rwkv_set_end)
        att = [[carve(S) for _ in range(NG)] for _ in range(2)]
        st_new = carve(C)
        g_var = carve(SUB * H)
        g_rstd = carve(SUB * H)
        carve_from(0, ffn_end)
        rk = [[carve(S, F16) for _ in range(2)] for _ in range(2)]
        r_decay = carve(2 * S)
        r_st = [carve(NG * HG * P, F16) for _ in range(SUB)]
        k_stk = [carve(NG * P, F16) for _ in range(SUB)]
        k_w = [carve(C) for _ in range(SUB - 1)]
        v_tok = [carve(C) for _ in range(SUB - 1)]
        v_by_head = [carve(HG * C) for _ in range(SUB)]
        state = [None] + [carve(C) for _ in range(SUB - 1)]
        y8 = carve(S)
        y_c = carve(S)
        y_sq = carve(S)
        silu_g = carve(S)
        y_parts = [carve(S, F16) for _ in range(2)]

        carve_from(ffn_end)
        e_w = [carve(E * C + E, F16) for _ in range(2)]
        bias_w = carve(E * C + E, F16)
        m_w = [carve(4 * C, F16) for _ in range(2)]
        set_end = place[0]

        carve_from(0, ffn_end)
        e_max = carve(SUB)
        e_shift = carve(SUB * E)
        e_exp = carve(SUB * E)
        e_sum = carve(SUB)
        e_rec = carve(SUB)
        e_rank = carve(SUB * E)
        e_first = carve(SUB)
        e_one = carve(SUB * E)
        e_sel = [carve(SUB * E) for _ in range(2)]
        e_za = [carve(S) for _ in range(2)]
        e_zb = [carve(S) for _ in range(2)]
        e_z2 = [carve(S // 2) for _ in range(2)]
        e_z1 = [carve(S // 4) for _ in range(2)]
        e_end = place[0]

        carve_from(set_end)
        qk = [[carve(S, F16) for _ in range(2)] for _ in range(2)]
        q_stack = [carve(S, F16) for _ in range(NG)]
        neg_max = carve(SUB * HG)
        y_raw = carve(S)
        den_rec = carve(SUB * HG)
        y_tok = carve(S)
        yo = [carve(S, F16) for _ in range(2)]
        max_pad = carve(SUB * P, F16)
        k_stack = [carve(S, F16) for _ in range(NG)]
        carve_from(0, ffn_end)
        TILE_W = [S, S - P, S - P]
        probs = [[carve(HG * w) for w in TILE_W] for _ in range(2)]
        v_aug = carve(SUB * H * 32)
        assert ffn_end - SUB * H * 32 >= e_end

        GN_SET = (y8, y_c, y_sq, silu_g, g_var, g_rstd, 2)
        GN_LAST = (*att[0], st_new[:, 0:SUB * H], st_new[:, SUB * H:2 * SUB * H], 3)

        def gn_set(b):
            return GN_LAST if isinstance(b, int) and b == NB - 1 else GN_SET

        def con_(name):
            a, n = CON[name]
            return con_sb[:, a:a + n]

        def half_(name):
            a, n = HALF[name]
            return half_sb[:, a:a + n]

        def col_(name):
            a, n = COL[name]
            return col_sb[:, a:a + n]

        def raw_(name):
            a, n = LIN[name]
            return raw[:, a:a + n]

        def prob(g, j, r):
            w = S - j * P
            if j < 2:
                return probs[g % 2][j][:, r * w:(r + 1) * w]
            at = r * TILE_W[2] + (j - 2) * 2 * P
            return probs[g % 2][2][:, at:at + w]

        def pick(name, g):
            return half_(name)[:, g * P:(g + 1) * P]

        ident = con_("ident")
        ident16 = half_("ident")

        def sub(t, s, n=1):
            return t[:, ds(s * P, n * P)]

        def seq(t, b):
            return t[:, ds(b * S, S)]

        def xsub(t, s):
            return t[:, ds((s // SUB) * XW + 8 + (s % SUB) * P, P)]

        def xchunk(t, b, n, before):
            return t[:, ds(b * XW + (8 + n * P - before), P)]

        def xseq(t, b, before=0):
            return t[:, ds(b * XW + (8 - before), S)]

        def xparts(t, s, g):
            if g == 1:
                return xsub(t, s)
            if g == SUB:
                return xseq(t, s // SUB)
            return by(t[:, 0:g // SUB * XW], g // SUB)[:, :, 8:XW]

        def prep_psum(g, at=6):
            return psum[:, (at + 1) * BANK - max(g, SUB) * P:(at + 1) * BANK][:, 0:g * P]

        def by(t, n):
            return t.rearrange("p (n c) -> p n c", n=n)

        def over(t, n, c):
            return t.rearrange("p (n o) -> p n o", o=1).to_broadcast([P, n, c])

        s_x = [sem(n) for n in ("x_loaded_first", "x_loaded_second", "x_loaded_rest")]
        s_fr = sem("ffn_router_loaded")
        s_con1, s_con = sem("first_consts_loaded"), sem("other_consts_loaded")
        s_lin = sem("other_weights_loaded")
        s_wraw = [sem(f"ffn_w_loaded{q}") for q in range(2)]
        s_pool_const = sem("pool_consts_set")
        s_bz = sem("bias_rows_cleared")
        s_frhi, s_frlo, s_whi, s_wlo = sem("router_hi"), sem("router_lo"), sem("ffn_w_hi"), sem("ffn_w_lo")
        s_bn, s_mv, s_var, s_rstd, s_xn, s_xT, s_xTs, s_xhi, s_xlo = [sem(n) for n in (
            "bn_stats_done", "mean_var_done", "var_ready", "rstd_ready", "x_norm_ready", "xT_in_psum", "xT_copied",
            "x_hi_ready", "x_lo_ready")]
        s_mrg_in, s_mrg_ps, s_mrg = sem("merge_in_ready"), sem("merge_in_psum"), sem("merged")
        s_xT2 = sem("xT_in_psum_again")
        s_lg, s_lgs, s_exp, s_cw, s_cwTp, s_cwT = [sem(n) for n in (
            "logits_in_psum", "logits_shifted", "logits_exp", "cw_ready", "cwT_in_psum", "cwT_ready")]
        s_rstep = sem("routing_step")
        ROUTE_STEPS = 9
        s_bc, s_xc, s_xchi, s_xclo = [sem(n) for n in ("cw_broadcast", "xc_ready", "xc_hi_ready", "xc_lo_ready")]
        s_g, s_u, s_s, s_h, s_hhi, s_hlo, s_hfree = [sem(n) for n in (
            "gate_in_psum", "up_in_psum", "gate_act_ready", "h_ready", "h_hi_ready", "h_lo_ready", "h_slot_free")]
        s_facc = sem("ffn_out_added")
        s_ewhi, s_ewlo, s_bhi, s_blo = [sem(n) for n in ("e_w_hi", "e_w_lo", "bias_hi", "bias_lo")]
        s_elg, s_esh, s_eexp, s_esel = [sem(n) for n in (
            "e_logits_in_psum", "e_logits_shifted", "e_exp", "e_selected")]
        s_estep = sem("e_routing_step")
        E_STEPS = 5
        s_eya, s_eyb, s_eza, s_ezb, s_ez2, s_ez1, s_eadd = [sem(n) for n in (
            "e_low_experts_in_psum", "e_high_experts_in_psum", "e_low_weighted", "e_high_added",
            "e_two_left", "e_one_left", "e_added")]
        s_st = sem("stored")

        plan, n_merge, seen = [], 0, dict(F=0, E=0, R=0, M=0)
        for i, kind in enumerate(PHASES):
            merge = i > 0 and PHASES[i - 1] == "F"
            plan.append(dict(i=i, kind=kind, n0=i * NS, use=seen[kind], merge=merge, g0=n_merge, next=PHASES[i + 1:i + 2]))
            n_merge += NB if merge else 0
            plan[-1]["merges"] = n_merge
            seen[kind] += 1

        def peeled(f):
            return 1 if f else PAIRS

        def splits(f, i):
            return f == 0 and isinstance(i, int) and i < PAIRS - 1

        def ahead(i):
            return i - (ITER - LEAD) if isinstance(i, int) and 0 <= i - (ITER - LEAD) < 4 else None

        def cwT_psum(g):
            a = 4 * BANK if g == LEAD else 7 * BANK + 64
            return psum[0:2 * E, a:a + g * P // 2].bitcast(F16)

        def begin(eng, i):
            if i == 0:
                return
            before = plan[i - 1]
            if before["kind"] == "F":
                eng.wait_ge(s_facc, (before["use"] + 1) * (ITER + 1))
            if before["kind"] == "E":
                eng.wait_ge(s_eadd, (before["use"] + 1) * NS + 2)
            if before["kind"] == "R":
                eng.wait_ge(s_rout, NB + 1)
            if before["kind"] == "M":
                eng.wait_ge(s_mout, NB)

        s_rset, s_rexp, s_rwhi, s_rwlo = sem("rwkv_setup"), sem("rwkv_exps"), sem("rwkv_w_hi"), sem("rwkv_w_lo")
        s_rp, s_rhi, s_rlo, s_rdec, s_kp, s_khi, s_klo = [sem(n) for n in (
            "r_in_psum", "r_hi_ready", "r_lo_ready", "r_decay_ready", "k_in_psum", "k_hi_ready", "k_lo_ready")]
        s_y8, s_gmean, s_yc, s_ysq, s_gvarp, s_gvar, s_grstd, s_gp, s_sg, s_gwide, s_grb, s_yn, s_yg, s_yghi, s_yglo, s_rop, s_rout = [
            sem(n) for n in ("y_copied", "gn_mean_in_psum", "gn_centred", "gn_squares", "gn_var_in_psum", "gn_var_ready",
                             "gn_rstd_ready", "g_in_psum", "silu_g_ready", "gn_rstd_repeated", "gn_rstd_in_psum", "gn_normed",
                             "y_gated", "y_hi_ready", "y_lo_ready", "rwkv_out_in_psum", "rwkv_added")]
        s_rst, s_kst, s_kv, s_rbyh, s_kstk, s_vbyh, s_stp, s_stm, s_state, s_av = [sem(n) for n in (
            "r_stack_in_psum", "k_stack_in_psum", "kv_in_psum", "r_by_head", "k_stack_ready",
            "v_by_head", "state_in_psum", "state_masked", "state_ready", "att_used")]
        s_attp, s_attw = sem("att_in_psum"), sem("att_weighted")
        s_mset, s_mwhi, s_mwlo = sem("attention_setup"), sem("attention_w_hi"), sem("attention_w_lo")
        s_mqp, s_mqhi, s_mqlo, s_mkp, s_mkhi, s_mklo, s_mvp, s_mv_in = [sem(n) for n in (
            "mq_in_psum", "mq_hi_ready", "mq_lo_ready", "mk_in_psum", "mk_hi_ready", "mk_lo_ready", "mv_in_psum", "mv_ready")]
        s_yTp, s_yohi, s_yolo, s_mop, s_mout = [sem(n) for n in (
            "my_transposed", "my_hi_ready", "my_lo_ready", "attention_out_in_psum", "attention_added")]
        s_mks, s_mqs, s_mkst, s_mqst, s_mpad, s_mTp, s_mqaug, s_yraw, s_ytp, s_drec, s_ytok = [
            sem(n) for n in ("mk_stack_in_psum", "mq_stack_in_psum", "mk_stack_ready", "mq_stack_ready",
                             "max_padded", "max_transposed", "max_rows_ready",
                             "weighted_values_copied", "weighted_values_transposed",
                             "denominator_rec", "attention_normed")]
        s_p1, s_p1used = sem("scores_by_query_in_psum"), sem("scores_by_query_used")
        s_p2, s_p2exp = sem("scores_by_key_in_psum"), sem("probs_ready")
        s_pvq = sem("probs_used")
        block = ctx.enter_context(nc.Block())

        PIECES = [[(0, 0)], [(1, 0)], [(2, 0), (3, 2 * P)]]
        TILES = [(i, r, pieces) for i, pieces in enumerate(PIECES) for r in range(HG)]
        KT = len(TILES)
        KT_END = [HG, 2 * HG, 3 * HG, 3 * HG]
        UNITS = NB * NG
        SCORED, USED = KT * NG, 2 * SUB

        @block.sync
        def _(sp):
            def load_x(b):
                sp.dma_start(x_tok[:, b * S:(b + 1) * S], x[:, b * S:(b + 1) * S]).then_inc(s_x[min(b, 2)], 16)

            con_first, half_first = CON["head_mean"][0], HALF["ones"][0]
            load_x(0)
            load_x(1)
            sp.dma_start(con_sb[:, 0:con_first], con[:, 0:con_first]).then_inc(s_con1, 16)
            sp.dma_start(col_sb[:], col).then_inc(s_con1, 16)
            sp.dma_start(fr_raw[:], ffn_router).then_inc(s_fr, 16)
            sp.dma_start(half_sb[:, 0:half_first], half[:, 0:half_first]).then_inc(s_con1, 16)
            for e in range(E):
                if e >= 2:
                    sp.wait_ge(s_wlo, 3 * (e - 1))
                q = e % 2
                sp.dma_start(raw[:, 3 * F * q:3 * F * (q + 1)], ffn_w[e]).then_inc(s_wraw[q], 16)
                if e == 1:
                    for b in range(2, NB):
                        load_x(b)
            sp.dma_start(con_sb[:, con_first:], con[:, con_first:]).then_inc(s_con, 16)
            sp.dma_start(half_sb[:, half_first:], half[:, half_first:]).then_inc(s_con, 16)
            sp.dma_start(big_sb[:], big).then_inc(s_con, 16)
            sp.wait_ge(s_wlo, 3 * E)
            sp.dma_start(raw[:, 0:LIN_N], lin).then_inc(s_lin, 16)
            sp.wait_ge(s_bz, 1)
            sp.dma_start(bias_raw[0:1, :], bias[0:1, :]).then_inc(s_lin, 16)
            sp.dma_start(bias_raw[32:33, :], bias[1:2, :]).then_inc(s_lin, 16)
            sp.wait_ge(s_lin, 48)
            begin(sp, len(plan))
            sp.dma_start(out, x_tok[:]).then_inc(s_st, 16)
            sp.wait_ge(s_st, 16)

        @block.gpsimd
        def _(pool):
            def prep_rstd(n, g):
                pool.wait_ge(s_var, n + g)
                pool.tensor_tensor(ln_rstd[:, 0:g], ln_var[:, 0:g], neg_half[:, 0:g], ALU.pow).then_inc(s_rstd, g)

            pool.memset(neg_half[:], -0.5).then_inc(s_pool_const, 1)
            pool.memset(e_const[:], float(np.exp(1.0))).then_inc(s_pool_const, 1)
            pool.memset(by(x_hi[:], NB)[:, :, 0:8], 0.0).then_inc(s_pool_const, 1)
            pool.memset(by(x_lo[:], NB)[:, :, 0:8], 0.0).then_inc(s_pool_const, 1)
            pool.wait_ge(s_pool_const, 2)

            def clear_bias():
                pool.wait_ge(s_wlo, 3 * E)
                pool.memset(bias_raw, 0.0).then_inc(s_bz, 1)

            def clear_weights():
                pool.memset(cw_T, 0.0).then_inc(s_pool_const, 1)

            def ffn(ph, start, rest):
                f, n0 = ph["use"], ph["n0"]
                r0, m0 = f * NS, f * NB * E

                def clear_output():
                    pool.memset(facc[:], 0.0).then_inc(s_facc, 1)

                def exps(n):
                    pool.wait_ge(s_lgs, n + 1)
                    pool.tensor_tensor(lg_exp[:, 0:2 * E], e_const[:], lg_shift[:, 0:2 * E], ALU.pow).then_inc(s_exp, 1)

                def xc_low(m, q):
                    pool.wait_ge(s_xchi, m + 1)
                    pool.tensor_tensor(xc_lo[q], xc[q], xc_hi[q], ALU.subtract).then_inc(s_xclo, 1)

                if 1 in start and f == 0:
                    prep_rstd(n0, LEAD)
                    clear_weights()
                    clear_output()
                if 3 in start:
                    xc_low(m0, 0)
                    xc_low(m0 + 1, 1)
                if not rest:
                    return
                begin(pool, ph["i"])
                if f:
                    clear_output()

                def body(i, prepare, last):
                    s = i + LEAD
                    if prepare:
                        prep_rstd(n0 + s, 1)
                    if not last:
                        xc_low(m0 + 2 * i + 2, 0)
                    if not last:
                        xc_low(m0 + 2 * i + 3, 1)
                    if prepare:
                        exps(r0 + s)
                    if ph["next"] and ahead(i) in (0, 2):
                        prep_rstd(n0 + NS + SUB * (ahead(i) // 2), SUB)

                for i in range(peeled(f)):
                    body(i, True, False)
                if f == 0:
                    clear_bias()
                with pool.Fori(peeled(f), ITER - LEAD) as i:
                    body(i, True, False)
                for i in range(ITER - LEAD, ITER - LEAD + 4):
                    body(i, False, False)
                with pool.Fori(ITER - LEAD + 4, ITER - 1) as i:
                    body(i, False, False)
                body(ITER - 1, False, True)

            def moe(ph):
                n0, use = ph["n0"], ph["use"]
                t0 = use * NS

                def fold(t, q):
                    pool.wait_ge(s_ezb, t + 3)
                    pool.tensor_tensor(e_z2[q], e_zb[q][:, 0:2 * C], e_zb[q][:, 2 * C:4 * C], ALU.add).then_inc(s_ez2, 1)
                    pool.wait_ge(s_ez2, t + 3)
                    pool.wait_ge(s_eadd, t + 1)
                    pool.tensor_tensor(e_z1[q], e_z2[q][:, 0:C], e_z2[q][:, C:2 * C], ALU.add).then_inc(s_ez1, 1)

                begin(pool, ph["i"])
                if use == 0:
                    pool.memset(max_pad, 0.0).then_inc(s_mset, 1)
                    pool.memset(v_aug, 0.0).then_inc(s_mset, 1)
                    pool.wait_ge(s_mset, 2)
                    pool.memset(by(v_aug, SUB * H)[:, :, K:2 * K], 1.0).then_inc(s_mset, 1)

                def body(b, prep):
                    for k in range(SUB):
                        fold(t0 + b * SUB + k, k % 2)
                        if k == 1 and prep:
                            prep_rstd(n0 + SUB * b + LEAD, SUB)

                with pool.Fori(0, NB - 2) as b:
                    body(b, True)
                body(NB - 2, ph["next"])
                body(NB - 1, ph["next"])

            def rwkv(ph):
                n0 = ph["n0"]

                def gn_rstd(b):
                    pool.wait_ge(s_gvar, b + 1)
                    g_var, g_rstd = gn_set(b)[4:6]
                    pool.tensor_tensor(g_rstd, g_var, neg_half[:, 0:SUB * H], ALU.pow).then_inc(s_grstd, 1)

                def gate_low(b):
                    pool.wait_ge(s_yghi, b + 1)
                    pool.tensor_tensor(y_parts[1], gn_set(b)[1], y_parts[0], ALU.subtract).then_inc(s_yglo, 1)

                begin(pool, ph["i"])

                def body(b, before, prep):
                    if prep:
                        prep_rstd(n0 + SUB * b + LEAD, SUB)
                    if before:
                        gn_rstd(b - 1)
                        if isinstance(b, int) and b == NB - 1:
                            gn_rstd(b)
                        gate_low(b - 1)

                body(0, False, True)
                with pool.Fori(1, NB - 2) as b:
                    body(b, True, True)
                body(NB - 2, True, ph["next"])
                body(NB - 1, True, ph["next"])
                gate_low(NB - 1)
                if ph["next"]:
                    ffn(plan[ph["i"] + 1], (1, 2, 3), False)

            def attention(ph, start, rest):
                n0 = ph["n0"]
                begin(pool, ph["i"])
                with pool.Fori(0, NB - 2) as b:
                    prep_rstd(n0 + SUB * b + LEAD, SUB)
                if ph["next"]:
                    for b in range(NB - 2, NB):
                        prep_rstd(n0 + SUB * b + LEAD, SUB)
            for ph in plan:
                if ph["kind"] == "F":
                    ffn(ph, (1, 2, 3) if ph["i"] == 0 else (), True)
                elif ph["kind"] == "M":
                    attention(ph, 0, True)
                else:
                    dict(E=moe, R=rwkv)[ph["kind"]](ph)

        @block.scalar
        def _(act):
            def prep_merge(m, n, b):
                act.wait_ge(s_mrg_ps, m)
                act.wait_ge(s_xT, n)
                act.activation(merge_in[:, 0:S], seq(facc, b), ACT.Copy).then_inc(s_mrg_in, 1)

            def prep_xT(n, s, g, keep, at=6):
                act.wait_ge(s_xT, n + g)
                src = prep_psum(g, at)
                if keep:
                    act.activation(sub(x_T, s, g), src, ACT.Copy).then_inc(s_xTs, g)
                act.activation(xparts(x_hi, s, g), by(src, 2) if g == LEAD else src, ACT.Copy).then_inc(s_xhi, g)

            def ffn(ph, start, rest):
                f, n0 = ph["use"], ph["n0"]
                r0, m0, c0 = f * NS, f * NB * E, f * ITER * CH

                def split_weight(e, t):
                    if t == 0:
                        act.wait_ge(s_wraw[e % 2], 16 * (e // 2 + 1))
                    a = 3 * F * (e % 2) + t * F
                    act.activation((ffn_g, ffn_u, ffn_d)[t][0][:, e * F:(e + 1) * F], raw[:, a:a + F], ACT.Copy, scale=W_UP).then_inc(s_whi, 1)

                def copy_cwT(n, s, g):
                    act.wait_ge(s_cwTp, n + g)
                    act.activation(cw_T[0:2 * E, ds(s * P, g * P)], cwT_psum(g), ACT.Copy).then_inc(s_cwT, g)

                def silu(c, k):
                    act.wait_ge(s_g, c + 1)
                    if k >= 2 or f:
                        act.wait_ge(s_h, c - 1)
                    act.activation(gate_act[k % 2], bank(k % 2), ACT.Silu, scale=W_DOWN).then_inc(s_s, 1)

                def h_high(c, k):
                    act.wait_ge(s_h, c + 1)
                    act.wait_ge(s_hfree, c + 1)
                    act.activation(h_hi[k % HSLOTS], h32[k % 2], ACT.Copy).then_inc(s_hhi, 1)

                def xc_high(m, q, chunks_used):
                    act.wait_ge(s_xc, m + 1)
                    if chunks_used is not None:
                        act.wait_ge(s_u, chunks_used)
                    act.activation(xc_hi[q], xc[q], ACT.Copy).then_inc(s_xchi, 1)

                def rwkv_exps():
                    act.wait_ge(s_con1, 48)
                    act.activation(w_key, col_("decay"), ACT.Exp).then_inc(s_rexp, 1)
                    act.activation(w_query[:, 0:1], col_("decay_row"), ACT.Exp).then_inc(s_rexp, 1)
                    act.wait_ge(s_rset, 2)
                    for h in range(H):
                        act.activation(w_intra[:, h * P:(h + 1) * P], con_("distance"), ACT.Exp, scale=decay_neg[:, h:h + 1])
                    act.activation(w_key, decay_neg, ACT.Exp, scale=con_("to_end"))
                    act.activation(w_chunk, decay_row, ACT.Exp, scale=float(P))
                    act.activation(w_query, con_("position"), ACT.Exp, scale=decay_row).then_inc(s_rexp, 1)

                def rwkv_weights(j, k):
                    if k == CH - 1 and j < 2:
                        act.wait_ge(s_rset, 5 + j)
                        act.activation(mix_w[j][0], mixed[j], ACT.Copy).then_inc(s_rwhi, 1)
                    if k == 0 and j == 2:
                        act.activation(r_wo[0], raw_("wo_r"), ACT.Copy, scale=W_UP).then_inc(s_rwhi, 1)

                def late_weights(j, k):
                    n = (E * C + E) // 2
                    c = slice(j % 2 * n, j % 2 * n + n)
                    if k == 0 and j < 2:
                        a = LIN["experts"][0] + c.start
                        act.activation(e_w[0][:, c], raw[:, a:a + n], ACT.Copy, scale=W_UP).then_inc(s_ewhi, 1)
                    if k == 0 and j >= 2:
                        act.activation(bias_w[:, c], bias_raw[:, c], ACT.Copy, scale=W_UP).then_inc(s_bhi, 1)
                    if k == 5 and j == 0:
                        a = LIN["q"][0]
                        act.activation(m_w[0], raw[:, a:a + 4 * C], ACT.Copy, scale=W_UP).then_inc(s_mwhi, 1)

                if 1 in start:
                    if f == 0:
                        act.wait_ge(s_fr, 16)
                        act.activation(fr_w[0][:], fr_raw[:], ACT.Copy, scale=W_UP).then_inc(s_frhi, 1)
                    if f == 0:
                        rwkv_exps()
                        for t in range(3):
                            split_weight(0, t)
                        prep_xT(n0, 0, LEAD, True)
                        for t in range(3):
                            split_weight(1, t)
                    else:
                        act.wait_ge(s_xT2, 1)
                        act.activation(x_T[:, 0:LEAD * P], prep_psum(LEAD), ACT.Copy).then_inc(s_xTs, LEAD)
                    act.wait_ge(s_lgs, r0 + LEAD)
                    act.activation(lg_exp, lg_shift, ACT.Exp).then_inc(s_exp, LEAD)
                    silu(c0, 0)
                    silu(c0 + 1, 1)
                if 2 in start:
                    act.wait_ge(s_pool_const, 4 + f + 1)
                    copy_cwT(r0, 0, LEAD)
                if 3 in start:
                    xc_high(m0, 0, None)
                    xc_high(m0 + 1, 1, None)
                if not rest:
                    return
                begin(act, ph["i"])
                h_high(c0, 0)

                def body(i, prepare, finish, last):
                    c = c0 + i * CH
                    s = i + LEAD
                    for k in range(CH):
                        if not (last and k + 2 >= CH):
                            silu(c + k + 2, k + 2)
                        if not (last and k + 1 >= CH):
                            h_high(c + k + 1, k + 1)
                        if not last and k == 2:
                            xc_high(m0 + 2 * i + 2, 0, c + FC)
                        if not last and k == 6:
                            xc_high(m0 + 2 * i + 3, 1, c + 2 * FC)
                        if finish and k == 5:
                            copy_cwT(r0 + s - 1, s - 1, 1)
                        if prepare and k == 4:
                            prep_xT(n0 + s, s, 1, True)
                        if k < 6 and splits(f, i):
                            split_weight(2 * i + 2 + k // 3, k % 3)
                        if ph["next"] and ahead(i) is not None:
                            j, q = ahead(i), ahead(i) // 2
                            nx = n0 + NS + SUB * q
                            if j == 0 and k == 0:
                                act.wait_ge(s_lin, 48)
                                act.wait_ge(s_con, 48)
                            if j % 2 == 0 and k == 0:
                                prep_merge(ph["merges"] + q, nx, q)
                            if j % 2 == 1 and k == 4:
                                prep_xT(nx, q * SUB, SUB, False)
                            (late_weights if f else rwkv_weights)(j, k)

                for i in range(peeled(f)):
                    body(i, True, i > 0, False)
                with act.Fori(peeled(f), ITER - LEAD) as i:
                    body(i, True, True, False)
                for i in range(ITER - LEAD, ITER - LEAD + 4):
                    body(i, False, i == ITER - LEAD, False)
                with act.Fori(ITER - LEAD + 4, ITER - 1) as i:
                    body(i, False, False, False)
                body(ITER - 1, False, False, True)

            def moe(ph):
                n0, use = ph["n0"], ph["use"]
                t0, b0 = use * NS, use * NB

                def exps(b):
                    act.wait_ge(s_esh, b + 1)
                    act.activation(e_exp, e_shift, ACT.Exp, scale=W_DOWN).then_inc(s_eexp, 1)

                def weigh(t, b, k, odd):
                    act.wait_ge(s_esel, 2 * b + 2)
                    act.wait_ge(s_eya, t + 1)
                    act.wait_ge(s_ezb, t + 1)
                    for e in range(E // 2):
                        ins = act.activation(e_za[k % 2][:, e * C:(e + 1) * C], bank(2 * (k % 2), e * C, (e + 1) * C), ACT.Copy,
                                             scale=e_sel[odd][:, k * E + e:k * E + e + 1])
                        if e == E // 2 - 1:
                            ins.then_inc(s_eza, 1)

                begin(act, ph["i"])
                exps(b0)

                def body(b, odd, prep, merge, more):
                    if merge:
                        prep_merge(ph["g0"] + b + 2, n0 + SUB * b + LEAD, b + 2)
                    for k in range(SUB):
                        weigh(t0 + b * SUB + k, b0 + b, k, odd)
                        if k == 2 and more:
                            exps(b0 + b + 1)
                        if k == 2 and not more and ph["next"] == ("M",):
                            attention(plan[ph["i"] + 1], 1, False)
                    if not more and ph["next"] == ("M",):
                        attention(plan[ph["i"] + 1], 2, False)
                    if prep:
                        prep_xT(n0 + SUB * b + LEAD, (b + 2) % NB * SUB if isinstance(b, int) else (b + 2) * SUB, SUB, False)

                with act.Fori(0, NB // 2 - 1) as pair:
                    for odd in range(2):
                        body(2 * pair + odd, odd, True, ph["merge"], True)
                body(NB - 2, 0, ph["next"], False, True)
                body(NB - 1, 1, ph["next"], False, False)

            def rwkv(ph):
                n0 = ph["n0"]

                def r_high(b):
                    act.wait_ge(s_rp, b + 1)
                    act.wait_ge(s_rst, SUB * b)
                    act.activation(rk[0][0], bank(6), ACT.Copy, scale=W_DOWN).then_inc(s_rhi, 1)

                def k_high(b):
                    act.wait_ge(s_kp, b + 1)
                    act.wait_ge(s_kst, SUB * b)
                    act.activation(rk[1][0], bank(6), ACT.Copy, scale=W_DOWN).then_inc(s_khi, 1)

                def stacks(u, n):
                    act.wait_ge(s_rst, u + 1)
                    act.wait_ge(s_attp, SUB * u + SUB)
                    dst = r_st[n].rearrange("p (g r i) -> p g r i", g=NG, r=HG)
                    for r in range(HG):
                        ins = act.activation(dst[:, :, r], by(bank(5), NG), ACT.Copy, scale=con_("row_head")[:, r:r + 1])
                    ins.then_inc(s_rbyh, 1)
                    act.wait_ge(s_kst, u + 1)
                    act.activation(k_stk[n], bank(3), ACT.Copy).then_inc(s_kstk, 1)

                def y_copy(b):
                    act.wait_ge(s_av, SUB * b + 2 * SUB)
                    act.activation(gn_set(b)[0], bank(4), ACT.Copy, scale=1.0 / HEAD_DIV).then_inc(s_y8, 1)

                def squares(b):
                    act.wait_ge(s_yc, b + 1)
                    y_c, y_sq = gn_set(b)[1:3]
                    act.activation(y_sq, y_c, ACT.Square).then_inc(s_ysq, 1)

                def gate_silu(b):
                    act.wait_ge(s_gp, b + 1)
                    act.activation(gn_set(b)[3], bank(gn_set(b)[6]), ACT.Silu, scale=W_DOWN).then_inc(s_sg, 1)

                def widen_rstd(b):
                    act.wait_ge(s_grstd, b + 1)
                    g_wide, g_rstd = gn_set(b)[2], gn_set(b)[5]
                    act.activation(by(g_wide, SUB * H), over(g_rstd, SUB * H, K), ACT.Copy).then_inc(s_gwide, 1)

                def y_high(b):
                    act.wait_ge(s_yg, b + 1)
                    act.activation(y_parts[0], gn_set(b)[1], ACT.Copy).then_inc(s_yghi, 1)

                begin(act, ph["i"])
                r_high(0)
                k_high(0)
                stacks(0, 0)
                stacks(1, 1)

                def body(b, before, prep, merge, more):
                    for n in range(SUB):
                        if n == 0 and merge:
                            prep_merge(ph["g0"] + b + 2, n0 + SUB * b + LEAD, b + 2)
                        if n == 0 and before:
                            y_copy(b - 1)
                        if n == 3 and not more:
                            y_copy(b)
                            gate_silu(b - 1)
                            squares(b)
                        if n == 3 and before:
                            widen_rstd(b - 1)
                        if n == 2 and more:
                            k_high(b + 1)
                        if more or n < SUB - 2:
                            stacks(SUB * b + n + 2, (n + 2) % SUB)
                        if n == 0 and before:
                            squares(b - 1)
                        if n == 1 and more:
                            r_high(b + 1)
                        if n == 2 and before and more:
                            gate_silu(b - 1)
                        if n == 3 and before:
                            y_high(b - 1)
                        if n == 3 and prep:
                            prep_xT(n0 + SUB * b + LEAD, (b + 2) % NB * SUB if isinstance(b, int) else (b + 2) * SUB, SUB, False)

                body(0, 0, True, ph["merge"], True)
                body(1, 1, True, ph["merge"], True)
                with act.Fori(2, NB - 2) as b:
                    body(b, 2, True, ph["merge"], True)
                body(NB - 2, 2, ph["next"], False, True)
                body(NB - 1, 2, ph["next"], False, False)
                gate_silu(NB - 1)
                if ph["next"]:
                    ffn(plan[ph["i"] + 1], (1,), False)
                widen_rstd(NB - 1)
                if ph["next"]:
                    ffn(plan[ph["i"] + 1], (2,), False)
                y_high(NB - 1)
                if ph["next"]:
                    ffn(plan[ph["i"] + 1], (3,), False)

            def attention(ph, start, rest):
                n0 = ph["n0"]

                def q_high(b):
                    act.wait_ge(s_mqp, b + 1)
                    act.wait_ge(s_mqs, NG * b)
                    act.activation(qk[0][0], bank(5), ACT.Copy, scale=W_DOWN).then_inc(s_mqhi, 1)

                def k_high(b, at=6):
                    act.wait_ge(s_mkp, b + 1)
                    act.wait_ge(s_mks, NG * b)
                    act.activation(qk[1][0], bank(at), ACT.Copy, scale=W_DOWN).then_inc(s_mkhi, 1)

                def key_stack(u, g):
                    act.wait_ge(s_mks, u + 1)
                    act.wait_ge(s_p2, KT * u + KT)
                    act.activation(k_stack[g], bank(5), ACT.Identity, bias=con_("max_row")).then_inc(s_mkst, 1)

                def query_stack(u, g, at=6):
                    act.wait_ge(s_mqs, u + 1)
                    act.wait_ge(s_p2, KT * u + KT)
                    act.activation(q_stack[g], bank(at), ACT.Copy).then_inc(s_mqst, 1)

                def exps(u, g, t):
                    i, r, pieces = TILES[t]
                    w = TILE_W[i]
                    act.wait_ge(s_p2, SCORED + KT * u + t + 1)
                    act.wait_ge(s_pvq, SUB * u + pieces[-1][0] + 1)
                    act.activation(probs[g % 2][i][:, r * w:(r + 1) * w], bank(t % 2, 0, w), ACT.Exp, scale=R_SCALE).then_inc(s_p2exp, 1)

                def values(u):
                    act.wait_ge(s_pvq, USED + SUB * u + SUB)
                    act.wait_ge(s_ytp, u)
                    act.activation(y_raw, bank(7), ACT.Copy).then_inc(s_yraw, 1)

                def v_copy(b):
                    act.wait_ge(s_mvp, b + 1)
                    act.wait_ge(s_pvq, USED + SUB * NG * b)
                    act.activation(by(v_aug, SUB * H)[:, :, 0:K], by(bank(4), SUB * H), ACT.Copy, scale=W_DOWN).then_inc(s_mv_in, 1)

                def out_high(b):
                    act.wait_ge(s_yTp, b + 1)
                    act.wait_ge(s_mop, b + 1)
                    act.activation(yo[0], bank(4), ACT.Copy).then_inc(s_yohi, 1)

                if start == 1:
                    q_high(0)
                    k_high(0, 4)
                if start == 2:
                    key_stack(0, 0)
                    query_stack(0, 0, 4)
                if not rest:
                    return
                for u in range(1, NG):
                    key_stack(u, u)
                    query_stack(u, u)
                begin(act, ph["i"])
                act.wait_ge(s_mset, 3)

                def body(b, first, prep, more):
                    for g in range(NG):
                        u = NG * b + g
                        for t in range(KT):
                            exps(u, g, t)
                            if t == 1 and g == 0 and more:
                                q_high(b + 1)
                            if t == 6 and not (first and g == 0):
                                values(u - 1)
                            if t == 8 and g == 0:
                                v_copy(b)
                            if t == 7 and g == 0 and more:
                                k_high(b + 1)
                            if t == 8 and g == 2 and prep:
                                prep_xT(n0 + SUB * b + LEAD, (b + 2) % NB * SUB if isinstance(b, int) else (b + 2) * SUB, SUB, False, 4)
                            if t == 2 and g == 1 and not first:
                                out_high(b - 1)
                        if more:
                            key_stack(u + NG, g)
                            query_stack(u + NG, g)

                body(0, True, True, True)
                with act.Fori(1, NB - 2) as b:
                    body(b, False, True, True)
                body(NB - 2, False, ph["next"], True)
                body(NB - 1, False, ph["next"], False)
                values(UNITS - 1)
                out_high(NB - 1)

            for ph in plan:
                if ph["kind"] == "F":
                    ffn(ph, (1, 2, 3) if ph["i"] == 0 else (), True)
                elif ph["kind"] == "M":
                    attention(ph, 0, True)
                else:
                    dict(E=moe, R=rwkv)[ph["kind"]](ph)

        @block.vector
        def _(dve):
            def prep_add(m, b, at=6):
                dve.wait_ge(s_mrg_ps, m + 1)
                dve.tensor_tensor(seq(x_tok, b), seq(x_tok, b), prep_psum(SUB, at), ALU.add).then_inc(s_mrg, 1)

            def prep_bn(n, s, g):
                for q in range(g):
                    ins = dve.bn_stats(ln_stat[:, 6 * q:6 * q + 6], sub(x_tok, s + q))
                ins.then_inc(s_bn, g)
                dve.wait_ge(s_bn, n + g)

            def prep_aggr(n, g):
                for q in range(g):
                    ins = dve.bn_aggr(ln_mv[:, 2 * q:2 * q + 2], ln_stat[:, 6 * q:6 * q + 6])
                ins.then_inc(s_mv, g)
                dve.wait_ge(s_mv, n + g)
                dve.tensor_scalar(ln_var[:, 0:g], ln_mv[:, 1:2 * g:2], LN_EPS, None, ALU.add).then_inc(s_var, g)

            def prep_norm(n, s, g, at=0):
                dve.wait_ge(s_rstd, n + g)
                dve.wait_ge(s_xT, n)
                for q in range(g):
                    ins = dve.tensor_scalar(x_norm[:, (at + q) * P:(at + q + 1) * P], sub(x_tok, s + q), ln_mv[:, 2 * q:2 * q + 1],
                                            ln_rstd[:, q:q + 1], ALU.subtract, ALU.mult)
                ins.then_inc(s_xn, g)

            def prep_low(n, s, g, at=6):
                dve.wait_ge(s_xhi, n + g)
                lo, hi = [xparts(t, s, g) for t in (x_lo, x_hi)]
                src = prep_psum(g, at)
                dve.tensor_tensor(lo, by(src, 2) if g == LEAD else src, hi, ALU.subtract).then_inc(s_xlo, g)

            def low_weights(w, cols, a):
                return dve.scalar_tensor_tensor(w[1][:, cols], raw[:, a:a + cols.stop - cols.start], W_UP, w[0][:, cols], ALU.mult, ALU.subtract)

            def ffn(ph, start, rest):
                f, n0 = ph["use"], ph["n0"]
                r0, m0, c0, a0 = f * NS, f * NB * E, f * ITER * CH, f * ITER

                def split_weight(e, t):
                    dve.wait_ge(s_whi, 3 * e + t + 1)
                    low_weights((ffn_g, ffn_u, ffn_d)[t], slice(e * F, (e + 1) * F), 3 * F * (e % 2) + t * F).then_inc(s_wlo, 1)

                def step(n, g, k):
                    dve.wait_ge(s_rstep, n * ROUTE_STEPS + k * g)

                def scale_logits(n, g):
                    dve.wait_ge(s_lg, n + g)
                    w = 2 * E * g
                    dve.tensor_tensor(lg[:, 0:w], bank(7, 0, w), con_("logit_scale")[:, 0:w], ALU.mult).then_inc(s_rstep, g)

                def shift_logits(n, g):
                    w = 2 * E * g
                    step(n, g, 1)
                    dve.tensor_reduce(lg_max[:, 0:2 * g], by(lg[:, 0:w], 2 * g), AX_X, ALU.max).then_inc(s_rstep, g)
                    step(n, g, 2)
                    dve.tensor_tensor(by(lg_shift[:, 0:w], 2 * g), by(lg[:, 0:w], 2 * g), over(lg_max[:, 0:2 * g], 2 * g, E),
                                      ALU.subtract).then_inc(s_lgs, g)

                def exp_sums(n, g):
                    w = 2 * E * g
                    ex = lg_exp[:, 0:w].rearrange("p (g s e) -> p g s e", g=g, s=2)
                    dve.wait_ge(s_exp, n + g)
                    dve.tensor_reduce(sm_sum[:, 0:2 * g], by(lg_exp[:, 0:w], 2 * g), AX_X, ALU.add).then_inc(s_rstep, g)
                    dve.tensor_tensor(by(cw_num[:, 0:E * g], g), ex[:, :, 0], ex[:, :, 1], ALU.mult).then_inc(s_rstep, g)

                def cw_sums(n, g):
                    step(n, g, 4)
                    dve.scalar_tensor_tensor(cw_eps[:, 0:g], sm_sum[:, 0:2 * g:2], 1e-9, sm_sum[:, 1:2 * g:2], ALU.mult,
                                             ALU.mult).then_inc(s_rstep, g)
                    dve.tensor_reduce(cw_sum[:, 0:g], by(cw_num[:, 0:E * g], g), AX_X, ALU.add).then_inc(s_rstep, g)

                def cw_divisor(n, g):
                    step(n, g, 6)
                    dve.tensor_tensor(cw_den[:, 0:g], cw_sum[:, 0:g], cw_eps[:, 0:g], ALU.add).then_inc(s_rstep, g)

                def cw_reciprocal(n, g):
                    step(n, g, 7)
                    dve.reciprocal(cw_rec[:, 0:g], cw_den[:, 0:g]).then_inc(s_rstep, g)

                def cw_parts(g):
                    return [cw16[:, 0:2 * E * g].rearrange("p (g s e) -> p g s e", g=g, s=2)[:, :, h] for h in range(2)]

                def cw_high(n, g):
                    num, out32 = [by(t[:, 0:E * g], g) for t in (cw_num, cw_out)]
                    step(n, g, 8)
                    dve.tensor_tensor(out32, num, over(cw_rec[:, 0:g], g, E), ALU.mult).then_inc(s_rstep, g)
                    dve.wait_ge(s_cwTp, n)
                    dve.tensor_tensor(cw_parts(g)[0], num, over(cw_rec[:, 0:g], g, E), ALU.mult).then_inc(s_cw, g)

                def cw_low(n, g):
                    step(n, g, 9)
                    dve.wait_ge(s_cw, 2 * n + g)
                    dve.tensor_tensor(cw_parts(g)[1], by(cw_out[:, 0:E * g], g), cw_parts(g)[0], ALU.subtract).then_inc(s_cw, g)

                def scale_x(m, q, b, first):
                    dve.wait_ge(s_bc, m + 1)
                    if not first:
                        dve.wait_ge(s_xclo, m - 1)
                    dve.tensor_tensor(xc[q], seq(x_T, b), bank(5), ALU.mult).then_inc(s_xc, 1)

                def hidden(c, k, first):
                    dve.wait_ge(s_u, c + 1)
                    dve.wait_ge(s_s, c + 1)
                    if not first:
                        dve.wait_ge(s_hhi, c - 1)
                        dve.wait_ge(s_hlo, c - 1)
                    dve.scalar_tensor_tensor(h32[k % 2], bank(2 + k % 2), W_DOWN, gate_act[k % 2], ALU.mult, ALU.mult).then_inc(s_h, 1)

                def h_low(c, k):
                    dve.wait_ge(s_hhi, c + 1)
                    dve.tensor_tensor(h_lo[k % HSLOTS], h32[k % 2], h_hi[k % HSLOTS], ALU.subtract).then_inc(s_hlo, 1)

                def rwkv_rates():
                    dve.wait_ge(s_rexp, 2)
                    dve.tensor_scalar(decay_neg, w_key, EXP_CAP, -1.0, ALU.min, ALU.mult).then_inc(s_rset, 1)
                    dve.tensor_scalar(decay_row, w_query[:, 0:1], EXP_CAP, -1.0, ALU.min, ALU.mult).then_inc(s_rset, 1)
                    dve.tensor_scalar(mix_scale[:, 0:4], col_("mix"), W_UP, None, ALU.mult)
                    dve.tensor_scalar(mix_scale[:, 4:8], col_("mix"), -W_UP, W_UP, ALU.mult, ALU.add).then_inc(s_rset, 1)

                def rwkv_decay():
                    dve.wait_ge(s_rexp, 3)
                    dve.tensor_scalar(w_key, w_key, W_DOWN, None, ALU.mult)
                    dve.tensor_scalar(w_query, w_query, W_DOWN, None, ALU.mult)
                    dve.tensor_tensor(by(w_intra, H), by(w_intra, H), con_("later").rearrange("p (o i) -> p o i", o=1).to_broadcast([P, H, P]),
                                      ALU.mult).then_inc(s_rset, 1)

                def rwkv_weights(j, k):
                    if k == 0 and j < 2:
                        for r in range(4):
                            c = slice(r * C, (r + 1) * C)
                            ins = dve.tensor_scalar(mixed[j][:, c], raw_("mixed")[:, c], mix_scale[:, 4 * j + r:4 * j + r + 1], None, ALU.mult)
                        ins.then_inc(s_rset, 1)
                    if k == 0 and j >= 2:
                        dve.wait_ge(s_rwhi, j - 1)
                        dve.tensor_tensor(mix_w[j - 2][1], mixed[j - 2], mix_w[j - 2][0], ALU.subtract).then_inc(s_rwlo, 1)
                    if k == 4 and j == 2:
                        dve.wait_ge(s_rwhi, 3)
                        low_weights(r_wo, slice(0, C), LIN["wo_r"][0]).then_inc(s_rwlo, 1)
                    if k == 7:
                        for h in range(j * HG, (j + 1) * HG):
                            c = slice(h * P, (h + 1) * P)
                            a = COL["bonus"][0] + h
                            ins = dve.scalar_tensor_tensor(w_intra[:, c], ident, col_sb[:, a:a + 1], w_intra[:, c], ALU.mult, ALU.add)
                        ins.then_inc(s_rwlo, 1)

                def late_weights(j, k):
                    n = (E * C + E) // 2
                    c = slice(j % 2 * n, j % 2 * n + n)
                    if k == 3 and j < 2:
                        dve.wait_ge(s_ewhi, j + 1)
                        low_weights(e_w, c, LIN["experts"][0] + c.start).then_inc(s_ewlo, 1)
                    if k == 3 and j >= 2:
                        dve.wait_ge(s_bhi, j - 1)
                        dve.scalar_tensor_tensor(bias_w[32:33, c], bias_raw[32:33, c], W_UP, bias_w[32:33, c], ALU.mult,
                                                 ALU.subtract).then_inc(s_blo, 1)
                    if k == 0 and j == 1:
                        dve.wait_ge(s_mwhi, 1)
                        low_weights(m_w, slice(0, 4 * C), LIN["q"][0]).then_inc(s_mwlo, 1)

                if 1 in start:
                    if f == 0:
                        dve.wait_ge(s_frhi, 1)
                        dve.scalar_tensor_tensor(fr_w[1][:], fr_raw[:], W_UP, fr_w[0][:], ALU.mult, ALU.subtract).then_inc(s_frlo, 1)
                        dve.wait_ge(s_x[0], 16)
                        dve.wait_ge(s_x[1], 16)
                        prep_bn(n0, 0, LEAD)
                        rwkv_rates()
                        prep_aggr(n0, LEAD)
                        prep_norm(n0, 0, LEAD)
                        for t in range(3):
                            split_weight(0, t)
                        prep_low(n0, 0, LEAD)
                        for t in range(3):
                            split_weight(1, t)
                        dve.wait_ge(s_con1, 48)
                    scale_logits(r0, LEAD)
                    shift_logits(r0, LEAD)
                    exp_sums(r0, LEAD)
                    cw_sums(r0, LEAD)
                    cw_divisor(r0, LEAD)
                    cw_reciprocal(r0, LEAD)
                    cw_high(r0, LEAD)
                    cw_low(r0, LEAD)
                    if f == 0:
                        rwkv_decay()
                        dve.wait_ge(s_x[2], 16 * (NB - 2))
                if 3 in start:
                    scale_x(m0, 0, 0, not f)
                    scale_x(m0 + 1, 1, 0, not f)
                if not rest:
                    return
                begin(dve, ph["i"])
                hidden(c0, 0, not f)
                hidden(c0 + 1, 1, not f)
                h_low(c0, 0)

                def body(i, prepare, finish, last):
                    c = c0 + i * CH
                    s = i + LEAD
                    rp = r0 + s - 1
                    for k in range(CH):
                        if prepare and k == 0:
                            prep_bn(n0 + s, s, 1)
                        if not (last and k + 2 >= CH):
                            hidden(c + k + 2, k + 2, False)
                        if prepare and k == 0:
                            prep_aggr(n0 + s, 1)
                        if finish and k == 1:
                            exp_sums(rp, 1)
                        if finish and k == 2:
                            cw_sums(rp, 1)
                        if finish and k == 3:
                            cw_reciprocal(rp, 1)
                        if finish and k == 4:
                            cw_low(rp, 1)
                        if not (last and k + 1 >= CH):
                            h_low(c + k + 1, k + 1)
                        if k == CH - 1:
                            dve.wait_ge(s_hfree, HSLOTS + c + CH)
                            dve.wait_ge(s_facc, a0 + f + i + 1)
                            b = i // PAIRS
                            dve.scalar_tensor_tensor(seq(facc, b), bank(4), 0.5 * W_DOWN, seq(facc, b), ALU.mult, ALU.add).then_inc(s_facc, 1)
                        if not last and k == 1:
                            scale_x(m0 + 2 * i + 2, 0, (i + 1) // PAIRS, False)
                        if prepare and k == 2:
                            prep_norm(n0 + s, s, 1)
                        if finish and k == 2:
                            cw_divisor(rp, 1)
                        if finish and k == 3:
                            cw_high(rp, 1)
                        if prepare and k == 5:
                            prep_low(n0 + s, s, 1)
                        if not last and k == 5:
                            scale_x(m0 + 2 * i + 3, 1, (i + 1) // PAIRS, False)
                        if prepare and k == 6:
                            scale_logits(r0 + s, 1)
                            shift_logits(r0 + s, 1)
                        if k < 6 and splits(f, i):
                            split_weight(2 * i + 2 + k // 3, k % 3)
                        if ph["next"] and ahead(i) is not None:
                            j, q = ahead(i), ahead(i) // 2
                            nx, m = n0 + NS + SUB * q, ph["merges"] + q
                            if j == 0 and k == 0:
                                dve.wait_ge(s_lin, 48)
                                dve.wait_ge(s_con, 48)
                            if j % 2 == 0 and k == 2:
                                prep_add(m, q)
                            if j % 2 == 0 and k == 3:
                                dve.wait_ge(s_mrg, m + 1)
                                prep_bn(nx, SUB * q, SUB)
                            if j % 2 == 0 and k == 4:
                                prep_aggr(nx, SUB)
                            if j % 2 == 1 and k == 2:
                                prep_norm(nx, SUB * q, SUB)
                            if j % 2 == 1 and k == 6:
                                prep_low(nx, SUB * q, SUB)
                            (late_weights if f else rwkv_weights)(j, k)

                for i in range(peeled(f)):
                    body(i, True, i > 0, False)
                with dve.Fori(peeled(f), ITER - LEAD) as i:
                    body(i, True, True, False)
                for i in range(ITER - LEAD, ITER - LEAD + 4):
                    body(i, False, i == ITER - LEAD, False)
                with dve.Fori(ITER - LEAD + 4, ITER - 1) as i:
                    body(i, False, False, False)
                body(ITER - 1, False, False, True)

            def moe(ph):
                n0, use = ph["n0"], ph["use"]
                t0, b0 = use * NS, use * NB

                def step(b, k):
                    dve.wait_ge(s_estep, b * E_STEPS + k)

                def route(b):
                    dve.wait_ge(s_elg, b + 1)
                    dve.tensor_reduce(e_max, by(bank(7, 0, SUB * E), SUB), AX_X, ALU.max).then_inc(s_estep, 1)
                    step(b, 1)
                    dve.tensor_tensor(by(e_shift, SUB), by(bank(7, 0, SUB * E), SUB), over(e_max, SUB, E), ALU.subtract).then_inc(s_esh, 1)

                def select(b):
                    dve.wait_ge(s_eexp, b + 1)
                    dve.tensor_reduce(e_sum, by(e_exp, SUB), AX_X, ALU.add).then_inc(s_estep, 1)
                    dve.scalar_tensor_tensor(e_rank, e_shift, 0.0, con_("rev_index"), ALU.is_ge, ALU.mult).then_inc(s_estep, 1)
                    step(b, 3)
                    dve.reciprocal(e_rec, e_sum).then_inc(s_estep, 1)
                    dve.tensor_reduce(e_first, by(e_rank, SUB), AX_X, ALU.max).then_inc(s_estep, 1)
                    step(b, 5)
                    dve.tensor_tensor(by(e_one, SUB), by(e_rank, SUB), over(e_first, SUB, E), ALU.is_equal).then_inc(s_esel, 1)

                def choose(b, odd):
                    dve.wait_ge(s_esel, 2 * b + 1)
                    if not isinstance(b, int) or b:
                        dve.wait_ge(s_eza, (b - 1) * SUB + 2)
                        dve.wait_ge(s_ezb, (b - 1) * SUB + 2)
                    dve.tensor_tensor(by(e_sel[odd], SUB), by(e_one, SUB), over(e_rec, SUB, E), ALU.mult).then_inc(s_esel, 1)

                def weigh(t, b, k, odd):
                    q = k % 2
                    dve.wait_ge(s_esel, 2 * b + 2)
                    dve.wait_ge(s_eyb, t + 1)
                    dve.wait_ge(s_eza, t + 3)
                    dve.wait_ge(s_ez2, t + 1)
                    for e in range(E // 2):
                        c = slice(e * C, (e + 1) * C)
                        a = k * E + E // 2 + e
                        ins = dve.scalar_tensor_tensor(e_zb[q][:, c], bank(2 * q + 1, e * C, (e + 1) * C), e_sel[odd][:, a:a + 1],
                                                       e_za[q][:, c], ALU.mult, ALU.add)
                    ins.then_inc(s_ezb, 1)

                def add(t, s, k):
                    dve.wait_ge(s_ez1, t + 3)
                    dve.scalar_tensor_tensor(sub(x_tok, s), e_z1[k % 2], 0.5 * W_DOWN, sub(x_tok, s), ALU.mult, ALU.add).then_inc(s_eadd, 1)

                begin(dve, ph["i"])
                route(b0)
                select(b0)
                choose(b0, 0)

                def body(b, odd, first, prep, merge, more):
                    nx, sx = n0 + SUB * b + LEAD, SUB * b + LEAD
                    if isinstance(b, int) and b >= NB - 2:
                        sx %= NS
                    for k in range(SUB):
                        t = t0 + b * SUB + k
                        if k == 2 and more:
                            route(b0 + b + 1)
                        if k == 3 and more:
                            select(b0 + b + 1)
                            choose(b0 + b + 1, 1 - odd)
                        weigh(t, b0 + b, k, odd)
                        if k == 0 and prep:
                            if merge:
                                prep_add(ph["g0"] + b + 2, b + 2, 5)
                                dve.wait_ge(s_mrg, ph["g0"] + b + 3)
                            prep_bn(nx, sx, SUB)
                        if k == 1 and prep:
                            prep_aggr(nx, SUB)
                        if k == 2 and not more and ph["next"] == ("M",):
                            attention(plan[ph["i"] + 1], 1, False)
                        if k == 2 and prep:
                            prep_norm(nx, sx, SUB)
                        if k or not first:
                            add(t - 1, b * SUB + k - 1, (k - 1) % 2)
                    if prep:
                        prep_low(nx, sx, SUB)

                body(0, 0, True, True, ph["merge"], True)
                body(1, 1, False, True, ph["merge"], True)
                with dve.Fori(1, NB // 2 - 1) as pair:
                    for odd in range(2):
                        body(2 * pair + odd, odd, False, True, ph["merge"], True)
                body(NB - 2, 0, False, ph["next"], False, True)
                body(NB - 1, 1, False, ph["next"], False, False)
                add(t0 + NS - 1, NS - 1, 1)

            def rwkv(ph):
                n0 = ph["n0"]

                def r_low(b):
                    dve.wait_ge(s_rhi, b + 1)
                    dve.scalar_tensor_tensor(rk[0][1], bank(6), W_DOWN, rk[0][0], ALU.mult, ALU.subtract).then_inc(s_rlo, 1)
                    dve.wait_ge(s_av, SUB * b)
                    dve.tensor_tensor(by(seq(r_decay, b % 2), SUB), by(bank(6), SUB),
                                      w_query.rearrange("p (o i) -> p o i", o=1).to_broadcast([P, SUB, P]), ALU.mult).then_inc(s_rdec, 1)

                def k_low(b):
                    dve.wait_ge(s_khi, b + 1)
                    dve.scalar_tensor_tensor(rk[1][1], bank(6), W_DOWN, rk[1][0], ALU.mult, ALU.subtract).then_inc(s_klo, 1)

                def keys_values(u, n):
                    dve.wait_ge(s_kv, u + 1)
                    dve.wait_ge(s_av, u + 1)
                    if n < SUB - 1:
                        dve.tensor_tensor(by(k_w[n], H), by(bank(7, 0, C), H), over(w_key, H, K), ALU.mult)
                        dve.tensor_scalar(v_tok[n], bank(7, C, 2 * C), W_DOWN, None, ALU.mult)
                    dve.tensor_tensor(by(v_by_head[n], HG), bank(7, C, 2 * C).rearrange("p (o c) -> p o c", o=1).to_broadcast([P, HG, C]),
                                      by(con_("v_head"), HG), ALU.mult).then_inc(s_vbyh, 1)

                def new_state(b, n):
                    dve.wait_ge(s_stp, (SUB - 1) * b + n + 1)
                    dve.wait_ge(s_av, SUB * b + n + 2)
                    if n == 0:
                        dve.tensor_tensor(state[1], bank(7, 2 * C, 3 * C), con_("same_head"), ALU.mult).then_inc(s_state, 1)
                        return
                    dve.tensor_tensor(st_new, bank(7, 2 * C, 3 * C), con_("same_head"), ALU.mult).then_inc(s_stm, 1)
                    dve.wait_ge(s_stm, (SUB - 2) * b + n)
                    dve.wait_ge(s_state, (SUB - 1) * b + n)
                    dve.scalar_tensor_tensor(state[n + 1], state[n], w_chunk, st_new, ALU.mult, ALU.add).then_inc(s_state, 1)

                def weigh(u, n, groups):
                    for g in groups:
                        dve.wait_ge(s_attp, 4 * SUB + NG * u + g + 1)
                        dve.wait_ge(s_av, u + 3)
                        dve.tensor_tensor(att[n % 2][g], bank(g % 2), w_intra[:, g * S:(g + 1) * S], ALU.mult).then_inc(s_attw, 1)

                def centre(b):
                    dve.wait_ge(s_gmean, b + 1)
                    y8, y_c, at = gn_set(b)[0], gn_set(b)[1], gn_set(b)[6]
                    dve.tensor_tensor(y_c, y8, bank(at), ALU.subtract).then_inc(s_yc, 1)

                def variance(b):
                    dve.wait_ge(s_gvarp, b + 1)
                    dve.tensor_scalar(gn_set(b)[4], bank(gn_set(b)[6], 0, SUB * H), GN_EPS, None, ALU.add).then_inc(s_gvar, 1)

                def group_norm(b):
                    dve.wait_ge(s_grb, b + 1)
                    y8, y_c, _, silu_g, _, _, at = gn_set(b)
                    y_n, y_g = y8, y_c
                    dve.scalar_tensor_tensor(y_n, y_c, col_("ln_w"), bank(at), ALU.mult, ALU.mult).then_inc(s_yn, 1)
                    dve.wait_ge(s_yn, b + 1)
                    dve.wait_ge(s_sg, b + 1)
                    dve.scalar_tensor_tensor(y_g, y_n, col_("ln_b"), silu_g, ALU.add, ALU.mult).then_inc(s_yg, 1)

                def add(b):
                    dve.wait_ge(s_rop, b + 1)
                    dve.scalar_tensor_tensor(seq(x_tok, b), bank(gn_set(b)[6]), W_DOWN, seq(x_tok, b), ALU.mult, ALU.add).then_inc(s_rout, 1)

                begin(dve, ph["i"])
                r_low(0)
                k_low(0)
                keys_values(0, 0)
                new_state(0, 0)
                keys_values(1, 1)
                weigh(0, 0, range(NG))

                def body(b, before, prep, merge, more):
                    nx, sx = n0 + SUB * b + LEAD, SUB * b + LEAD
                    if isinstance(b, int):
                        sx %= NS
                    for n in range(SUB):
                        u = SUB * b + n
                        if more or n < SUB - 1:
                            weigh(u + 1, (n + 1) % SUB, (0, 1))
                        if n == 1 and prep:
                            prep_aggr(nx, SUB)
                        if (more or n < SUB - 1) and (n + 1) % SUB < SUB - 1:
                            new_state(b + (n + 1) // SUB, (n + 1) % SUB)
                        if n == 0 and before == 2:
                            add(b - 2)
                        if n == 2 and more:
                            k_low(b + 1)
                        if more or n < SUB - 1:
                            weigh(u + 1, (n + 1) % SUB, (2, 3))
                        if n == 1 and more:
                            r_low(b + 1)
                        if n == 3 and not more:
                            centre(b)
                            variance(b)
                        if n == 3 and before:
                            group_norm(b - 1)
                        if n == 3 and not more and ph["next"]:
                            dve.memset(cw_T, 0.0).then_inc(s_pool_const, 1)
                        if more or n < SUB - 2:
                            keys_values(u + 2, (n + 2) % SUB)
                        if n == 0 and before:
                            centre(b - 1)
                        if n == 2 and prep:
                            prep_norm(nx, sx, SUB, SUB if isinstance(b, int) and b == NB - 1 else 0)
                        if n == 3 and prep:
                            prep_low(nx, sx, SUB)
                        if n == 0 and merge:
                            prep_add(ph["g0"] + b + 2, b + 2)
                            dve.wait_ge(s_mrg, ph["g0"] + b + 3)
                        if n == 0 and prep:
                            prep_bn(nx, sx, SUB)
                        if n == 0 and before:
                            variance(b - 1)

                body(0, 0, True, ph["merge"], True)
                body(1, 1, True, ph["merge"], True)
                with dve.Fori(2, NB - 2) as b:
                    body(b, 2, True, ph["merge"], True)
                body(NB - 2, 2, ph["next"], False, True)
                body(NB - 1, 2, ph["next"], False, False)
                if ph["next"]:
                    ffn(plan[ph["i"] + 1], (1, 2), False)
                add(NB - 2)
                group_norm(NB - 1)
                if ph["next"]:
                    ffn(plan[ph["i"] + 1], (3,), False)
                add(NB - 1)

            def attention(ph, start, rest):
                n0 = ph["n0"]

                def q_low(b):
                    dve.wait_ge(s_mqhi, b + 1)
                    dve.scalar_tensor_tensor(qk[0][1], bank(5), W_DOWN, qk[0][0], ALU.mult, ALU.subtract).then_inc(s_mqlo, 1)

                def k_low(b, at=6):
                    dve.wait_ge(s_mkhi, b + 1)
                    dve.scalar_tensor_tensor(qk[1][1], bank(at), W_DOWN, qk[1][0], ALU.mult, ALU.subtract).then_inc(s_mklo, 1)

                def max_rows(u, g):
                    dve.wait_ge(s_mTp, u + 1)
                    dve.tensor_tensor(q_stack[g], bank(6), q_stack[g], ALU.add).then_inc(s_mqaug, 1)

                def maxima(u, g, tiles):
                    for t in tiles:
                        if t == 0:
                            dve.wait_ge(s_mpad, u)
                        dve.wait_ge(s_p1, KT * u + t + 1)
                        for j, at in TILES[t][2]:
                            c = (SUB - 1 - j) * HG + (TILES[t][1] ^ 1)
                            ins = dve.tensor_reduce(neg_max[:, c:c + 1], bank(2 + t % 2, at, at + S - j * P), AX_X, ALU.max, negate=True)
                        ins.then_inc(s_p1used, 1)

                def pad_maxima(u):
                    dve.wait_ge(s_p1used, KT * u + KT + 2)
                    dve.wait_ge(s_mTp, u)
                    dve.tensor_scalar(by(max_pad, SUB * HG)[:, :, MAX_ROW:MAX_ROW + 1], by(neg_max, SUB * HG), M_DOWN, None, ALU.mult).then_inc(s_mpad, 1)

                def normalise(u, b, g):
                    dve.wait_ge(s_ytp, u + 1)
                    cols = bank(7).rearrange("p (q r c) -> p q r c", q=SUB, r=HG)
                    dve.reciprocal(by(den_rec, SUB * HG), by(bank(7), SUB * HG)[:, :, K:K + 1]).then_inc(s_drec, 1)
                    if g == 0:
                        dve.wait_ge(s_yTp, b)
                    dve.wait_ge(s_drec, u + 1)
                    dve.tensor_tensor(y_tok.rearrange("p (q g r v) -> p q g r v", q=SUB, g=NG, r=HG)[:, :, g], cols[:, :, :, 0:K],
                                      den_rec.rearrange("p (q r o) -> p q r o", q=SUB, o=1).to_broadcast([P, SUB, HG, K]),
                                      ALU.mult).then_inc(s_ytok, 1)

                def out_low(b):
                    dve.wait_ge(s_yohi, b + 1)
                    dve.tensor_tensor(yo[1], bank(4), yo[0], ALU.subtract).then_inc(s_yolo, 1)

                def add(b):
                    dve.wait_ge(s_mop, b + 2)
                    dve.scalar_tensor_tensor(seq(x_tok, b), bank(4), W_DOWN, seq(x_tok, b), ALU.mult, ALU.add).then_inc(s_mout, 1)

                if start:
                    q_low(0)
                    k_low(0, 4)
                if not rest:
                    return
                begin(dve, ph["i"])
                dve.wait_ge(s_mset, 3)
                maxima(0, 0, range(KT))
                pad_maxima(0)
                maxima(1, 1, range(4))
                max_rows(0, 0)
                maxima(1, 1, range(4, KT))
                pad_maxima(1)

                def body(b, first, prep, more):
                    nx, sx = n0 + SUB * b + LEAD, SUB * b + LEAD
                    if isinstance(b, int):
                        sx %= NS
                    for g in range(NG):
                        u = NG * b + g
                        for t in range(KT):
                            if more or g < NG - 2:
                                maxima(u + 2, (g + 2) % NG, [t])
                            if t == 2 and g == 0 and more:
                                q_low(b + 1)
                            if t == 4 and (more or g < NG - 1):
                                max_rows(u + 1, (g + 1) % NG)
                            if t == 2 and g == 2 and prep:
                                prep_norm(nx, sx, SUB)
                            if t == 7 and g == 1 and not first:
                                add(b - 1)
                            if t == 10 and not (first and g == 0):
                                normalise(u - 1, b - (g == 0), (g - 1) % NG)
                            if t == 8 and g == 0 and more:
                                k_low(b + 1)
                            if t == 6 and g == 0 and prep:
                                prep_bn(nx, sx, SUB)
                            if t == 9 and g == 1 and prep:
                                prep_aggr(nx, SUB)
                            if t == 10 and g == 2 and prep:
                                prep_low(nx, sx, SUB, 4)
                            if t == 3 and g == 1 and not first:
                                out_low(b - 1)
                        if more or g < NG - 2:
                            pad_maxima(u + 2)

                body(0, True, True, True)
                with dve.Fori(1, NB - 2) as b:
                    body(b, False, True, True)
                body(NB - 2, False, ph["next"], True)
                body(NB - 1, False, ph["next"], False)
                normalise(UNITS - 1, NB - 1, NG - 1)
                out_low(NB - 1)
                add(NB - 1)

            for ph in plan:
                if ph["kind"] == "F":
                    ffn(ph, (1, 2, 3) if ph["i"] == 0 else (), True)
                elif ph["kind"] == "M":
                    attention(ph, 0, True)
                else:
                    dict(E=moe, R=rwkv)[ph["kind"]](ph)

        @block.tensor
        def _(pe):
            def prep_merge(m, n, at=6):
                pe.wait_ge(s_mrg_in, m + 1)
                if at == 6:
                    pe.wait_ge(s_xlo, n)
                else:
                    pe.wait_ge(s_mrg, m)
                for q in range(SUB):
                    ins = pe.transpose(prep_psum(SUB, at)[:, q * P:(q + 1) * P], merge_in[:, q * P:(q + 1) * P], ident)
                ins.then_inc(s_mrg_ps, 1)

            def prep_transpose(n, g, at=6, norm_at=0):
                pe.wait_ge(s_xn, n + g)
                pe.wait_ge(s_xlo, n)
                for q in range(g):
                    ins = pe.transpose(prep_psum(g, at)[:, q * P:(q + 1) * P], x_norm[:, (norm_at + q) * P:(norm_at + q + 1) * P], ident)
                ins.then_inc(s_xT, g)

            def keep_warm(n, at):
                for _ in range(n):
                    pe.matmul(bank(at), ident16, half_("pick_expert")[:, 0:BANK], start=True, stop=True)

            def three(dst, lhs, rhs, first=True, last=True):
                pe.matmul(dst, lhs[0], rhs[0], start=first, stop=False)
                pe.matmul(dst, lhs[0], rhs[1], start=False, stop=False)
                return pe.matmul(dst, lhs[1], rhs[0], start=False, stop=last)

            def ffn(ph, start, rest):
                f, n0 = ph["use"], ph["n0"]
                r0, m0, c0, a0 = f * NS, f * NB * E, f * ITER * CH, f * ITER

                def logits(n, s, nx, g):
                    pe.wait_ge(s_xlo, nx + g)
                    pe.wait_ge(s_cwT, n)
                    for q in range(g):
                        ins = three(bank(7, q * 2 * E, (q + 1) * 2 * E), [xsub(t, s + q) for t in (x_hi, x_lo)], [w[:] for w in fr_w])
                    ins.then_inc(s_lg, g)

                def transpose_cw(n, g):
                    pe.wait_ge(s_cw, 2 * (n + g))
                    for q in range(g):
                        ins = pe.transpose(cwT_psum(g)[:, q * P:(q + 1) * P], cw16[:, q * 2 * E:(q + 1) * 2 * E], ident16)
                    ins.then_inc(s_cwTp, g)

                def broadcast(m, e, b):
                    pe.wait_ge(s_xc, m)
                    pe.matmul(bank(5), sub(half_("pick_expert"), e), seq(cw_T, b), start=True, stop=True).then_inc(s_bc, 1)

                def cols(w, e, k):
                    return [t[:, ds(e * F + (k % FC) * P, P)] for t in w]

                def gate(c, k, e, b, first):
                    if not first:
                        pe.wait_ge(s_s, c - 1)
                    three(bank(k % 2), cols(ffn_g, e, k), [xseq(t, b) for t in (x_hi, x_lo)]).then_inc(s_g, 1)

                def up(c, k, m, e, first):
                    if not first:
                        pe.wait_ge(s_h, c - 1)
                    q = (k // FC) % 2
                    if k % FC == 0:
                        pe.wait_ge(s_xclo, m + 1)
                    three(bank(2 + k % 2), cols(ffn_u, e, k), [xc_hi[q], xc_lo[q]]).then_inc(s_u, 1)

                def gate_up(c, k, m, e, b):
                    gate(c, k, e, b, False)
                    up(c, k, m, e, False)

                def down(c, k, e, added):
                    pe.wait_ge(s_hlo, c + 1)
                    if k == 0:
                        pe.wait_ge(s_facc, added)
                    r = k % HSLOTS
                    three(bank(4), cols(ffn_d, e, k), [h_hi[r], h_lo[r]], k == 0, k == CH - 1).then_inc(s_hfree, 1)

                if 1 in start:
                    if f == 0:
                        pe.wait_ge(s_con1, 48)
                        keep_warm(8, 7)
                        pe.wait_ge(s_frlo, 1)
                        prep_transpose(n0, LEAD)
                        keep_warm(12, 7)
                    logits(r0, 0, n0, LEAD)
                    if f:
                        for q in range(LEAD):
                            ins = pe.transpose(prep_psum(LEAD)[:, q * P:(q + 1) * P], x_norm[:, q * P:(q + 1) * P], ident)
                        ins.then_inc(s_xT2, 1)
                    pe.wait_ge(s_wlo, 3 * 2)
                    gate(c0, 0, 0, 0, not f)
                    gate(c0 + 1, 1, 0, 0, not f)
                    pe.wait_ge(s_lgs, r0 + LEAD)
                    keep_warm(8, 7)
                if 2 in start:
                    transpose_cw(r0, LEAD)
                if 3 in start:
                    keep_warm(4, 7)
                    pe.wait_ge(s_cwT, r0 + LEAD)
                    broadcast(m0, 0, 0)
                    keep_warm(3, 7)
                    broadcast(m0 + 1, 1, 0)
                    keep_warm(4, 7)
                if not rest:
                    return
                begin(pe, ph["i"])
                up(c0, 0, m0, 0, not f)
                up(c0 + 1, 1, m0, 0, not f)

                def body(i, prepare, finish, last):
                    c = c0 + i * CH
                    s = i + LEAD
                    pair, b = i % PAIRS, i // PAIRS
                    npair, nb = (i + 1) % PAIRS, (i + 1) // PAIRS
                    for k in range(CH):
                        kk = k + 2
                        if kk == FC and f == 0 and isinstance(i, int) and i < PAIRS:
                            pe.wait_ge(s_wlo, 3 * (2 * i + 2))
                        if kk < CH:
                            gate_up(c + kk, kk, m0 + 2 * i + kk // FC, 2 * pair + kk // FC, b)
                        elif not last:
                            if kk == CH and splits(f, i):
                                pe.wait_ge(s_wlo, 3 * (2 * i + 3))
                            if kk == CH:
                                pe.wait_ge(s_xlo, n0 + nb * SUB + SUB)
                            gate_up(c + kk, kk, m0 + 2 * i + kk // FC, 2 * npair, nb)
                        if not last and k == 1:
                            pe.wait_ge(s_cwT, r0 + nb * SUB + SUB)
                            broadcast(m0 + 2 * i + 2, 2 * npair, nb)
                        if not last and k == 5:
                            broadcast(m0 + 2 * i + 3, 2 * npair + 1, nb)
                        if finish and k == 5:
                            transpose_cw(r0 + s - 1, 1)
                        down(c + k, k, 2 * pair + k // FC, a0 + f + i + 1)
                        if prepare and k == 6:
                            logits(r0 + s, s, n0 + s, 1)
                        if prepare and k == 3:
                            prep_transpose(n0 + s, 1)
                        if ph["next"] and k == 1 and ahead(i) in (0, 2):
                            prep_merge(ph["merges"] + ahead(i) // 2, n0 + NS + SUB * (ahead(i) // 2))
                        if ph["next"] and k == 3 and ahead(i) in (1, 3):
                            pe.wait_ge(s_mrg, ph["merges"] + ahead(i) // 2 + 1)
                            prep_transpose(n0 + NS + SUB * (ahead(i) // 2), SUB)

                for i in range(peeled(f)):
                    body(i, True, i > 0, False)
                with pe.Fori(peeled(f), ITER - LEAD) as i:
                    body(i, True, True, False)
                for i in range(ITER - LEAD, ITER - LEAD + 4):
                    body(i, False, i == ITER - LEAD, False)
                with pe.Fori(ITER - LEAD + 4, ITER - 1) as i:
                    body(i, False, False, False)
                body(ITER - 1, False, False, True)

            def moe(ph):
                n0, use = ph["n0"], ph["use"]
                t0, b0 = use * NS, use * NB
                ones = half_("ones")

                def parts(s):
                    return [xsub(t, s) for t in (x_hi, x_lo)]

                def ecols(a, b):
                    return [w[:, a:b] for w in e_w]

                def logits(b, s, n):
                    pe.wait_ge(s_xlo, n)
                    pe.wait_ge(s_esh, b)
                    for q in range(SUB):
                        dst = bank(7, q * E, (q + 1) * E)
                        pe.matmul(dst, ones, bias_w[:, E * C:E * C + E], start=True, stop=False)
                        ins = three(dst, parts(s + q), ecols(E * C, E * C + E), False)
                    ins.then_inc(s_elg, 1)

                def products(t, s, k):
                    for half_of, done, used in ((0, s_eya, s_eza), (1, s_eyb, s_ezb)):
                        pe.wait_ge(used, t + 1)
                        a = half_of * E // 2 * C
                        dst = bank(2 * (k % 2) + half_of)
                        pe.matmul(dst, ones, bias_w[:, a:a + BANK], start=True, stop=False)
                        three(dst, parts(s), ecols(a, a + BANK), False).then_inc(done, 1)

                pe.wait_ge(s_ewlo, 2)
                pe.wait_ge(s_blo, 2)
                logits(b0, 0, n0 + LEAD)
                begin(pe, ph["i"])

                def body(b, prep, merge, more):
                    nx, sx = n0 + SUB * b + LEAD, SUB * b + LEAD
                    for k in range(SUB):
                        products(t0 + b * SUB + k, b * SUB + k, k)
                        if k == 1 and more:
                            logits(b0 + b + 1, sx - SUB, nx)
                        if k == 0 and merge:
                            prep_merge(ph["g0"] + b + 2, nx, 5)
                        if k == 1 and not more and ph["next"] == ("M",):
                            attention(plan[ph["i"] + 1], 1, False)
                        if k == 3 and not more and ph["next"] == ("M",):
                            attention(plan[ph["i"] + 1], 2, False)
                        if k == 3 and prep:
                            prep_transpose(nx, SUB)

                with pe.Fori(0, NB - 2) as b:
                    body(b, True, ph["merge"], True)
                body(NB - 2, ph["next"], False, True)
                body(NB - 1, ph["next"], False, False)

            pe.sem_inc(s_hfree, HSLOTS)
            for s in (s_eza, s_ezb, s_ez2, s_ez1, s_eadd):
                pe.sem_inc(s, 2)
            for s in (s_rout, s_mop):
                pe.sem_inc(s, 1)
            def rwkv(ph):
                n0 = ph["n0"]

                def project(dst, j, rhs):
                    w = [[t[:, j * C:(j + 1) * C] for t in mix_w[m]] for m in range(2)]
                    three(dst, w[0], rhs[0], True, False)
                    return three(dst, w[1], rhs[1], False, True)

                def both(b):
                    return [[xseq(t, b, m) for t in (x_hi, x_lo)] for m in range(2)]

                def r_proj(b):
                    pe.wait_ge(s_xlo, n0 + SUB * b + SUB)
                    pe.wait_ge(s_klo, b)
                    project(bank(6), 0, both(b)).then_inc(s_rp, 1)

                def k_proj(b):
                    pe.wait_ge(s_rdec, b + 1)
                    project(bank(6), 1, both(b)).then_inc(s_kp, 1)

                def stacks(u, b, n):
                    for j, dst, names, ready, used, done in ((0, bank(5), ("q_hi", "q_lo"), s_rlo, s_rbyh, s_rst),
                                                             (1, bank(3), ("k_hi", "k_lo"), s_klo, s_kstk, s_kst)):
                        pe.wait_ge(ready, b + 1)
                        pe.wait_ge(used, u)
                        for g in range(NG):
                            for h in range(2):
                                ins = pe.matmul(dst[:, g * P:(g + 1) * P], pick(names[h], g), rk[j][h][:, n * P:(n + 1) * P],
                                                start=h == 0, stop=h == 1)
                        ins.then_inc(done, 1)

                def keys_values(u, b, n):
                    pe.wait_ge(s_vbyh, u)
                    pe.wait_ge(s_state, (SUB - 1) * b + n)
                    w = [[t[:, C:3 * C] for t in mix_w[m]] for m in range(2)]
                    chunk = [[xchunk(t, b, n, m) for t in (x_hi, x_lo)] for m in range(2)]
                    three(bank(7, 0, 2 * C), chunk[0], w[0], True, False)
                    three(bank(7, 0, 2 * C), chunk[1], w[1], False, True).then_inc(s_kv, 1)

                def state_product(u, b, n):
                    pe.wait_ge(s_vbyh, u + 1)
                    pe.wait_ge(s_state, (SUB - 1) * b + n)
                    pe.matmul(bank(7, 2 * C, 3 * C), k_w[n], v_tok[n], start=True, stop=True).then_inc(s_stp, 1)

                def scores(u, n, groups):
                    pe.wait_ge(s_rbyh, u + 1)
                    pe.wait_ge(s_kstk, u + 1)
                    for g in groups:
                        pe.wait_ge(s_attw, NG * u + g + 1)
                        pe.matmul(bank(g % 2), k_stk[n][:, g * P:(g + 1) * P], r_st[n][:, g * S:(g + 1) * S],
                                  start=True, stop=True).then_inc(s_attp, 1)

                def outputs(u, b, n):
                    if n == 0:
                        pe.wait_ge(s_y8, b)
                    else:
                        pe.wait_ge(s_state, (SUB - 1) * b + n)
                        pe.wait_ge(s_rdec, b + 1)
                        pe.matmul(bank(4, n * P, (n + 1) * P), state[n], r_decay[:, ds((b % 2) * S + n * P, P)], start=True, stop=False)
                    pe.wait_ge(s_attw, 2 + NG * u + NG)
                    pe.wait_ge(s_vbyh, u + 1)
                    for r in range(HG):
                        for g in range(NG):
                            c = slice(r * C + g * GC, r * C + (g + 1) * GC)
                            ins = pe.matmul(bank(4, n * P, (n + 1) * P)[g * GC:(g + 1) * GC], v_by_head[n][:, c],
                                            att[n % 2][g][:, r * P:(r + 1) * P], start=n == 0 and r == 0, stop=r == HG - 1)
                    ins.then_inc(s_av, 1)

                def gn_mean(b):
                    pe.wait_ge(s_y8, b + 1)
                    if gn_set(b) is GN_SET:
                        pe.wait_ge(s_rout, b + 1)
                    else:
                        pe.wait_ge(s_kstk, SUB * NB)
                    pe.matmul(bank(gn_set(b)[6]), con_("head_mean"), gn_set(b)[0], start=True, stop=True).then_inc(s_gmean, 1)

                def gn_var(b):
                    pe.wait_ge(s_ysq, b + 1)
                    y_sq, at = gn_set(b)[2], gn_set(b)[6]
                    for n in range(SUB):
                        ins = pe.matmul(bank(at, n * H, (n + 1) * H), y_sq[:, n * P:(n + 1) * P], con_("head_mean16"), start=True, stop=True)
                    ins.then_inc(s_gvarp, 1)

                def g_proj(b):
                    pe.wait_ge(s_gvar, b + 1)
                    project(bank(gn_set(b)[6]), 3, both(b)).then_inc(s_gp, 1)

                def gn_rstd(b):
                    pe.wait_ge(s_sg, b + 1)
                    pe.wait_ge(s_gwide, b + 1)
                    g_wide, at = gn_set(b)[2], gn_set(b)[6]
                    for n in range(SUB):
                        ins = pe.matmul(bank(at, n * P, (n + 1) * P), g_wide[:, n * P:(n + 1) * P], ident, start=True, stop=True)
                    ins.then_inc(s_grb, 1)

                def out_proj(b):
                    pe.wait_ge(s_yglo, b + 1)
                    for n in range(SUB):
                        ins = three(bank(gn_set(b)[6], n * P, (n + 1) * P), [t[:, n * P:(n + 1) * P] for t in y_parts], r_wo)
                    ins.then_inc(s_rop, 1)

                pe.sem_inc(s_attw, 2)
                pe.sem_inc(s_av, SUB)
                pe.sem_inc(s_attp, NG * SUB)
                pe.wait_ge(s_xlo, n0 + LEAD)
                pe.wait_ge(s_rwlo, 3 + SUB)
                r_proj(0)
                begin(pe, ph["i"])
                keep_warm(8, 2)
                k_proj(0)
                keep_warm(4, 2)
                for n in range(2):
                    stacks(n, 0, n)
                    keys_values(n, 0, n)
                    if n == 0:
                        state_product(n, 0, n)
                scores(0, 0, range(NG))

                def body(b, before, prep, merge, more):
                    for n in range(SUB):
                        u = SUB * b + n
                        b1, n1 = b + (n + 1) // SUB, (n + 1) % SUB
                        b2, n2 = b + (n + 2) // SUB, (n + 2) % SUB
                        ahead = more or n < SUB - 2
                        if more or n < SUB - 1:
                            scores(u + 1, (n + 1) % SUB, (0, 1))
                        if n == 2 and more:
                            k_proj(b + 1)
                        if n1 < SUB - 1 and (more or n < SUB - 1):
                            state_product(u + 1, b1, n1)
                        if ahead and n != 2:
                            stacks(u + 2, b2, n2)
                        if n == 0 and before == 2:
                            out_proj(b - 2)
                        if more or n < SUB - 1:
                            scores(u + 1, (n + 1) % SUB, (2, 3))
                        if n == 1 and more:
                            if merge:
                                pe.wait_ge(s_mrg, ph["g0"] + b + 3)
                            r_proj(b + 1)
                        if ahead and n == 2:
                            stacks(u + 2, b2, n2)
                        if n == 3 and not more:
                            outputs(u, b, n)
                            g_proj(b - 1)
                            gn_mean(b)
                            gn_var(b)
                        if n == 3 and before:
                            gn_rstd(b - 1)
                        if n == 3 and prep:
                            pe.wait_ge(s_klo, b + (2 if more else 1))
                            prep_transpose(n0 + SUB * b + LEAD, SUB, 6, 0 if more else SUB)
                        if ahead:
                            keys_values(u + 2, b2, n2)
                        if n == 0 and before:
                            gn_mean(b - 1)
                        if n == 0 and merge:
                            pe.wait_ge(s_klo, b + 1)
                            prep_merge(ph["g0"] + b + 2, n0 + SUB * b + 2 * SUB)
                        if more or n < SUB - 1:
                            outputs(u, b, n)
                        if n == 0 and before:
                            gn_var(b - 1)
                        if n == 2 and before and more:
                            g_proj(b - 1)

                body(0, 0, True, ph["merge"], True)
                body(1, 1, True, ph["merge"], True)
                with pe.Fori(2, NB - 2) as b:
                    body(b, 2, True, ph["merge"], True)
                body(NB - 2, 2, ph["next"], False, True)
                body(NB - 1, 2, ph["next"], False, False)
                g_proj(NB - 1)
                if ph["next"]:
                    ffn(plan[ph["i"] + 1], (1,), False)
                out_proj(NB - 2)
                if ph["next"]:
                    ffn(plan[ph["i"] + 1], (2,), False)
                gn_rstd(NB - 1)
                if ph["next"]:
                    ffn(plan[ph["i"] + 1], (3,), False)
                out_proj(NB - 1)

            def attention(ph, start, rest):
                n0 = ph["n0"]
                wq, wk, wv, wo = [[w[:, j * C:(j + 1) * C] for w in m_w] for j in range(4)]
                ident_b, keys_after, queries_before = [big_sb[:, a:a + P] for a, _ in BIG.values()]

                def parts(b):
                    return [xseq(t, b) for t in (x_hi, x_lo)]

                def q_proj(b):
                    pe.wait_ge(s_xlo, n0 + SUB * b + SUB)
                    pe.wait_ge(s_mkst, NG * b)
                    three(bank(5), wq, parts(b)).then_inc(s_mqp, 1)

                def k_proj(b, first):
                    if not first:
                        pe.wait_ge(s_mqst, NG * b)
                        pe.wait_ge(s_mqaug, NG * b - 2)
                    three(bank(4 if first else 6), wk, parts(b)).then_inc(s_mkp, 1)

                def v_proj(b):
                    for n in range(SUB):
                        ins = three(bank(4, n * P, (n + 1) * P), [xchunk(t, b, n, 0) for t in (x_hi, x_lo)], wv)
                    ins.then_inc(s_mvp, 1)

                def key_stack(u, b, g):
                    pe.wait_ge(s_mklo, b + 1)
                    pe.wait_ge(s_mkst, u)
                    for h, name in enumerate(("k_hi", "k_lo")):
                        ins = pe.matmul(bank(5), pick(name, g), qk[1][h], start=h == 0, stop=h == 1)
                    ins.then_inc(s_mks, 1)

                def query_stack(u, g, first):
                    pe.wait_ge(s_mqst, u)
                    if not first:
                        pe.wait_ge(s_mqaug, u - 2)
                    for h, name in enumerate(("q_hi", "q_lo")):
                        ins = pe.matmul(bank(4 if first and u == 0 else 6), pick(name, g), qk[0][h], start=h == 0, stop=h == 1)
                    ins.then_inc(s_mqs, 1)

                def max_rows(u, stacked):
                    pe.wait_ge(s_mpad, u + 1)
                    pe.wait_ge(s_mqst, stacked)
                    for q in range(SUB):
                        ins = pe.matmul(bank(6, q * P, (q + 1) * P), max_pad[:, q * P:(q + 1) * P], ident16, start=True, stop=True)
                    ins.then_inc(s_mTp, 1)

                def key_product(g, t, j, at):
                    head = slice(TILES[t][1] * HR, (TILES[t][1] + 1) * HR)
                    pe.matmul(bank(t % 2, at, at + S - j * P), k_stack[g][head, j * P:(j + 1) * P], q_stack[g][head, j * P:S],
                              start=True, stop=False)

                def key_mask(g, t, j, at):
                    return pe.matmul(bank(t % 2, at, at + P), ident_b, queries_before, start=False, stop=True)

                def query_product(g, t, j, at):
                    head = slice((TILES[t][1] ^ 1) * HR, ((TILES[t][1] ^ 1) + 1) * HR)
                    w = S - j * P
                    pe.matmul(bank(2 + t % 2, at, at + w), q_stack[g][head, w - P:w], k_stack[g][head, 0:w], start=True, stop=False)

                def query_mask(g, t, j, at):
                    end = at + S - j * P
                    return pe.matmul(bank(2 + t % 2, end - P, end), ident_b, keys_after, start=False, stop=True)

                def by_query(u, g, t):
                    pe.wait_ge(s_mqst, u + 1)
                    pe.wait_ge(s_mkst, u + 1)
                    pe.wait_ge(s_p1used, KT * u + t + 1)
                    for piece in TILES[t][2]:
                        query_product(g, t, *piece)
                        ins = query_mask(g, t, *piece)
                    ins.then_inc(s_p1, 1)

                def by_key(u, g, t):
                    pe.wait_ge(s_mqaug, u + 1)
                    pe.wait_ge(s_p2exp, KT * u + t + 1)
                    for piece in TILES[t][2]:
                        key_product(g, t, *piece)
                        ins = key_mask(g, t, *piece)
                    ins.then_inc(s_p2, 1)

                def by_both(u, g, t):
                    a = (g + 2) % NG
                    for n, piece in enumerate(TILES[t][2]):
                        if t == 0:
                            pe.wait_ge(s_mqaug, u + 1)
                        if n == 0:
                            pe.wait_ge(s_p2exp, KT * u + t + 1)
                        key_product(g, t, *piece)
                        if t == 0:
                            pe.wait_ge(s_mqst, u + 3)
                            pe.wait_ge(s_mkst, u + 3)
                        if n == 0:
                            pe.wait_ge(s_p1used, KT * (u + 2) + t + 1)
                        query_product(a, t, *piece)
                        key_ins = key_mask(g, t, *piece)
                        query_ins = query_mask(a, t, *piece)
                    key_ins.then_inc(s_p2, 1)
                    query_ins.then_inc(s_p1, 1)

                def weighted_values(u, b, g, j):
                    w = S - j * P
                    if j == 0:
                        pe.wait_ge(s_ytok, u)
                        pe.wait_ge(s_mv_in, b + 1)
                    pe.wait_ge(s_p2exp, KT * u + KT_END[j] + 2)
                    for r in range(HG):
                        a = (j * H + g * HG + r) * 32
                        ins = pe.matmul(bank(7, j * P, S)[r * 32:(r + 1) * 32], v_aug[:, a:a + 32], prob(g, j, r),
                                        start=j == 0, stop=j == SUB - 1)
                    ins.then_inc(s_pvq, 1)

                def transpose_values(u):
                    pe.wait_ge(s_yraw, u + 1)
                    for q in range(SUB):
                        ins = pe.transpose(bank(7, q * P, (q + 1) * P), y_raw[:, q * P:(q + 1) * P], ident)
                    ins.then_inc(s_ytp, 1)

                def transpose_out(b):
                    pe.wait_ge(s_ytok, NG * b + NG)
                    pe.wait_ge(s_mv_in, min(b + 2, NB) if isinstance(b, int) else b + 2)
                    for n in range(SUB):
                        ins = pe.transpose(bank(4, n * P, (n + 1) * P), y_tok[:, n * P:(n + 1) * P], ident)
                    ins.then_inc(s_yTp, 1)

                def out_proj(b):
                    pe.wait_ge(s_yolo, b + 1)
                    for n in range(SUB):
                        ins = three(bank(4, n * P, (n + 1) * P), [t[:, n * P:(n + 1) * P] for t in yo], wo)
                    ins.then_inc(s_mop, 1)

                if start == 1:
                    for c, n in ((s_p1used, 2), (s_p2exp, 2), (s_p2, SCORED), (s_pvq, USED)):
                        pe.sem_inc(c, n)
                    pe.wait_ge(s_mwlo, 1)
                    q_proj(0)
                    k_proj(0, True)
                if start == 2:
                    key_stack(0, 0, 0)
                    query_stack(0, 0, True)
                    keep_warm(4, 7)
                if not rest:
                    return
                for done in (s_eza, s_ezb):
                    pe.wait_ge(done, NS + 2)
                STACKS_AT = (1, 6, 18)
                for u in range(2):
                    for t in range(KT):
                        by_query(u, u, t)
                        keep_warm(1, 7)
                        for g in range(1, NG):
                            if KT * u + t == STACKS_AT[g - 1]:
                                key_stack(g, 0, g)
                            if KT * u + t == STACKS_AT[g - 1] + 1:
                                if g == 1:
                                    pe.wait_ge(s_xlo, n0 + LEAD)
                                query_stack(g, g, True)
                        if t == 2 and u == 1:
                            max_rows(0, 3)

                PV_AT = (1, 2, 4, 5)

                def body(b, first, prep, more):
                    for g in range(NG):
                        u = NG * b + g
                        follows = not (first and g == 0)
                        before = (u - 1, b - (g == 0), (g - 1) % NG)
                        for t in range(KT):
                            if more or g < NG - 2:
                                by_both(u, g, t)
                            else:
                                by_key(u, g, t)
                            if t == 0 and g == 0 and more:
                                q_proj(b + 1)
                            if t == 0 and g == 1 and not first:
                                transpose_out(b - 1)
                            if t in PV_AT and follows:
                                weighted_values(*before, PV_AT.index(t))
                            if t == 3 and (more or g < NG - 1):
                                max_rows(u + 1, u + 4 if more else UNITS)
                            if t == 3 and g == 0:
                                pe.wait_ge(s_xlo, n0 + SUB * b + (LEAD if more else SUB))
                                v_proj(b)
                            if t == 5 and g == 1 and not first:
                                out_proj(b - 1)
                            if t == 6 and g == 0 and more:
                                k_proj(b + 1, False)
                            if t == 7 and g == 2 and prep:
                                if first:
                                    pe.wait_ge(s_mv_in, b + 1)
                                else:
                                    pe.wait_ge(s_mout, b)
                                prep_transpose(n0 + SUB * b + LEAD, SUB, 4)
                            if t == 8 and follows:
                                transpose_values(u - 1)
                            if t == 10 and more:
                                key_stack(u + NG, b + 1, g)
                            if t == 11 and more:
                                query_stack(u + NG, g, False)

                body(0, True, True, True)
                with pe.Fori(1, NB - 2) as b:
                    body(b, False, True, True)
                body(NB - 2, False, ph["next"], True)
                body(NB - 1, False, ph["next"], False)
                for j in range(SUB):
                    weighted_values(UNITS - 1, NB - 1, NG - 1, j)
                transpose_values(UNITS - 1)
                transpose_out(NB - 1)
                out_proj(NB - 1)

            for ph in plan:
                if ph["kind"] == "F":
                    ffn(ph, (1, 2, 3) if ph["i"] == 0 else (), True)
                elif ph["kind"] == "M":
                    attention(ph, 0, True)
                else:
                    dict(E=moe, R=rwkv)[ph["kind"]](ph)


def shape_constants():
    c = np.arange(P)
    con = {n: np.zeros((P, w), np.float32) for n, (_, w) in CON.items()}
    con["ident"][:] = np.eye(P)
    same = (c[:, None] // K == c[None, :] // K)
    con["head_mean"][:] = same / K
    con["head_mean16"][c, c // K] = 1.0 / K
    con["same_head"][:] = same
    con["rev_index"][:] = np.tile(E - np.arange(E), SUB)
    con["logit_scale"][:] = np.tile(np.repeat([W_DOWN, W_DOWN / GATE_TEMP], E), LEAD)
    con["row_head"][c, c // HR] = 1.0
    con["max_row"][MAX_ROW::HR] = M_UP
    con["v_head"][:] = (W_DOWN * (c[None, :] % GC // K == np.arange(HG)[:, None])).reshape(1, HG * C)
    con["distance"][:] = np.maximum(c[None, :] - c[:, None] - 1, 0)
    con["later"][:] = c[None, :] > c[:, None]
    con["position"][:] = c[None, :]
    con["to_end"][:, 0] = P - 1 - c
    half = {n: np.zeros((P, w), np.float16) for n, (_, w) in HALF.items()}
    half["ident"][:] = np.eye(P)
    for e in range(E):
        half["pick_expert"][[e, E + e], e * P:(e + 1) * P] = 1.0
    half["ones"][:] = 1.0
    group = np.arange(GC)
    for name, parts in (("k_hi", (0, 2)), ("k_lo", (1,)), ("q_hi", (0, 1)), ("q_lo", (2,))):
        for g in range(NG):
            for part in parts:
                half[name][g * GC + group, g * P + group // K * HR + part * K + group % K] = 1.0
    after = np.where(c[None, :] > c[:, None], NEG_BIG, 0.0)
    big = np.concatenate([np.eye(P), after, after.T], axis=1)
    return (np.concatenate([con[n] for n in CON], axis=1), np.concatenate([half[n] for n in HALF], axis=1), big.astype(mybir.dt.np(BF16)))


def lay_out(v):
    def rows(a):
        return np.broadcast_to(a.reshape(1, -1), (P, a.size))

    con, half, big = shape_constants()
    x = v["L0_attn_xq"].reshape(NS, P, C).transpose(1, 0, 2).reshape(P, NS * C)
    down = v["L0_ffn_w_down"].reshape(E, FC, P, C).transpose(0, 2, 1, 3).reshape(E, P, F)
    qkv = v["L1_attn_w_qkv"].reshape(3, C, C)
    lin = dict(mixed=np.concatenate([v["L0_attn_W_" + n].T for n in "rkvg"], axis=1), wo_r=v["L0_attn_W_o"].T,
               experts=v["L1_ffn_expert_w"].transpose(2, 0, 1).reshape(C, E * C), router=v["L1_ffn_router_w"].T,
               q=qkv[0].T, k=qkv[1].T, v=qkv[2].T, wo_m=v["L1_attn_w_o"].T)
    col = dict(mix=np.stack([v["L0_attn_time_mix_" + n].reshape(C) for n in "rkvg"], axis=1),
               decay_row=np.repeat(v["L0_attn_time_decay"], K)[:, None], ln_w=v["L0_attn_ln_w"][:, None], ln_b=v["L0_attn_ln_b"][:, None],
               decay=rows(v["L0_attn_time_decay"]), bonus=rows(v["L0_attn_time_faaaa"]))
    bias = np.concatenate([v["L1_ffn_expert_b"].reshape(E * C), v["L1_ffn_router_b"]])
    return dict(x=x, ffn_router=np.concatenate([v["L0_ffn_w_router"], v["L0_ffn_w_gating"]], axis=1),
                ffn_w=np.concatenate([v["L0_ffn_w_gate"], v["L0_ffn_w_up"], down], axis=2),
                lin=np.concatenate([lin[n] for n in LIN], axis=1), col=np.concatenate([col[n] for n in COL], axis=1),
                bias=np.stack([bias, bias]), con=con, half=half, big=big)


def kernel(**inputs):
    import concourse.bacc as bacc
    from concourse.bass_utils import run_bass_kernel_spmd

    nc = bacc.Bacc("TRN2", target_bir_lowering=False, num_devices=1)
    arrays, args = {}, []
    for name, a in lay_out({n: np.asarray(a) for n, a in inputs.items()}).items():
        arrays[f"in_{name}_dram"] = np.ascontiguousarray(a)
        args.append(nc.dram_tensor(f"in_{name}_dram", a.shape, mybir.dt.from_np(a.dtype), kind="ExternalInput").ap())
    args.append(nc.dram_tensor("out_dram", (P, NS * C), F32, kind="ExternalOutput").ap())
    build(nc, *args)
    r = run_bass_kernel_spmd(nc, [arrays], core_ids=[0])
    return r.results[0]["out_dram"].reshape(P, NS, C).transpose(1, 0, 2).reshape(NB, S, C)
```
